# Optimizing a Trainium2 kernel written in Bass

```python
import numpy as np
import jax
import jax.numpy as jnp

def _softmax(x, axis=-1):
    return jax.nn.softmax(x, axis=axis)

def _gelu(x):
    return jax.nn.gelu(x, approximate=True)

def _silu(x):
    return jax.nn.silu(x)

def _sigmoid(x):
    return jax.nn.sigmoid(x)

def _layernorm(x, axis=-1, eps=1e-05):
    m = jnp.mean(x, axis=axis, keepdims=True)
    v = jnp.var(x, axis=axis, keepdims=True)
    return (x - m) / jnp.sqrt(v + eps)

def _scatter_add(tgt, idx, src, axis=0):
    return tgt.at[idx].add(src)

def _segment_sum(src, seg, n):
    return jax.ops.segment_sum(src, seg, n)
kernel_name = 'mk_xattn_ffn_d2_seqx_r8_736b6b'

def setup_inputs(seed: int=0):
    np.random.seed(seed)
    _w = jnp.asarray

    def _rec_inputs():
        import jax
        import jax.numpy as jnp
        _rk = jax.random.key(seed)
        x = -0.000125 + 0.9999 * jax.random.normal(jax.random.fold_in(_rk, 1), (32, 64, 128), jnp.float32)
        _lenS = 64 - jax.random.randint(jax.random.fold_in(_rk, 7), (32,), 0, max(1, 64 // 4) + 1, jnp.int32)
        _lenS2 = 64 - jax.random.randint(jax.random.fold_in(_rk, 8), (32,), 0, max(1, 64 // 4) + 1, jnp.int32)
        _ctx_1024P = jax.random.normal(jax.random.fold_in(_rk, 11), (32, 16, 128), jnp.float32)
        _ctx_1024c = jax.random.dirichlet(jax.random.fold_in(_rk, 511), 0.3 * jnp.ones((16,), jnp.float32), (32, 64))
        _ctx_1024t = jnp.einsum('bsk,bkd->bsd', _ctx_1024c, _ctx_1024P)
        _ctx_1024t = _ctx_1024t * jax.lax.rsqrt(jnp.mean(jnp.square(_ctx_1024t)) + 1e-12) * 0.953939
        ctx_1024 = -1.52775e-05 + 0.999936 * (_ctx_1024t + 0.3 * jax.random.normal(jax.random.fold_in(_rk, 611), (32, 64, 128), jnp.float32))
        return (x, ctx_1024)
    x, ctx_1024 = _rec_inputs()

    def _L0_xattn_setup():
        import jax, jax.numpy as jnp
        import numpy as np
        DECAY = 0.9
        key = jax.random.key(seed)
        k1, k2, k3 = jax.random.split(key, 3)
        B, S, D = (8, 512, 128)
        q = jax.random.normal(k1, (B, S, D), dtype=jnp.float32)
        k = jax.random.normal(k2, (B, S, D), dtype=jnp.float32)
        v = jax.random.normal(k3, (B, S, D), dtype=jnp.float32)
        return {'q': q, 'k': k, 'v': v}
    _L0_xattn_all = _L0_xattn_setup()
    _L0_xattn_in = {k: v for k, v in _L0_xattn_all.items() if k in ()}
    del _L0_xattn_all

    def _L0_ffn_setup():
        import jax, jax.numpy as jnp
        import numpy as np
        B, SEQ, DIM = (2, 512, 128)
        E, S = (8, 64)
        HID = 4 * DIM
        SCALE = DIM ** 0.5

        def rmsnorm(x, gamma):
            n = jnp.linalg.norm(x, axis=-1, keepdims=True)
            return x / jnp.maximum(n, 1e-12) * SCALE * gamma
        key = jax.random.key(seed)
        ks = jax.random.split(key, 4)
        w_init = lambda k, shape: jax.random.normal(k, shape, dtype=jnp.float32) * 0.02
        return {'x': jax.random.normal(ks[0], (B, SEQ, DIM), dtype=jnp.float32), 'norm_gamma': jnp.ones((DIM,), jnp.float32), 'slot_norm_gamma': jnp.ones((DIM,), jnp.float32), 'slot_embeds': jax.random.normal(ks[1], (E, S, DIM), dtype=jnp.float32), 'w1': w_init(ks[2], (E, DIM, HID)), 'b1': jnp.zeros((E, HID), jnp.float32), 'w2': w_init(ks[3], (E, HID, DIM)), 'b2': jnp.zeros((E, DIM), jnp.float32)}
    _L0_ffn_all = _L0_ffn_setup()
    _L0_ffn_in = {k: v for k, v in _L0_ffn_all.items() if k in ('norm_gamma', 'slot_norm_gamma', 'slot_embeds', 'w1', 'b1', 'w2', 'b2')}
    del _L0_ffn_all

    def _L1_xattn_setup():
        import jax, jax.numpy as jnp
        import numpy as np
        import math
        B, S, D, H = (1, 256, 128, 16)
        DK = D // H
        DH = 64
        LOG_T_MIN = math.log(0.1)
        LOG_T_MAX = math.log(10.0)

        def _linear(x, W, b):
            return x @ W.T + b
        key = jax.random.key(seed)
        ks = jax.random.split(key, 20)
        p = 0.02
        return {'query': jax.random.normal(ks[0], (B, S, D), jnp.float32), 'key': jax.random.normal(ks[1], (B, S, D), jnp.float32), 'value': jax.random.normal(ks[2], (B, S, D), jnp.float32), 'Wq': jax.random.normal(ks[3], (D, D), jnp.float32) * p, 'bq': jax.random.normal(ks[4], (D,), jnp.float32) * p, 'Wk': jax.random.normal(ks[5], (D, D), jnp.float32) * p, 'bk': jax.random.normal(ks[6], (D,), jnp.float32) * p, 'Wv': jax.random.normal(ks[7], (D, D), jnp.float32) * p, 'bv': jax.random.normal(ks[8], (D,), jnp.float32) * p, 'Wo': jax.random.normal(ks[9], (D, D), jnp.float32) * p, 'bo': jax.random.normal(ks[10], (D,), jnp.float32) * p, 'w1': jax.random.normal(ks[11], (DH, 3), jnp.float32) * 0.3, 'b1': jax.random.normal(ks[12], (DH,), jnp.float32) * 0.1, 'w2': jax.random.normal(ks[13], (DH, DH), jnp.float32) * 0.1, 'b2': jax.random.normal(ks[14], (DH,), jnp.float32) * 0.1, 'w3': jax.random.normal(ks[15], (1, DH), jnp.float32) * 0.1, 'b3': jnp.full((1,), (LOG_T_MIN + LOG_T_MAX) / 2, jnp.float32)}
    _L1_xattn_all = _L1_xattn_setup()
    _L1_xattn_in = {k: v for k, v in _L1_xattn_all.items() if k in ('Wq', 'bq', 'Wk', 'bk', 'Wv', 'bv', 'Wo', 'bo', 'w1', 'b1', 'w2', 'b2', 'w3', 'b3')}
    del _L1_xattn_all

    def _L1_ffn_setup():
        import jax, jax.numpy as jnp
        import numpy as np
        B, S, H, F, G = (8, 256, 128, 512, 128)
        EPS = 1e-05

        def _dequant(q, scales, g):
            K, N = q.shape
            w = (q.astype(jnp.float32) - 128.0).reshape(K // g, g, N) * scales[:, None, :]
            return w.reshape(K, N)
        key = jax.random.key(seed)
        ks = jax.random.split(key, 8)
        x = jax.random.normal(ks[0], (B, S, H), dtype=jnp.float32)
        ln_gamma = jnp.ones((H,), jnp.float32)
        ln_beta = jnp.zeros((H,), jnp.float32)
        fc1_q = jax.random.randint(ks[1], (H, F), 0, 32, dtype=jnp.int32)
        fc2_q = jax.random.randint(ks[2], (F, H), 0, 32, dtype=jnp.int32)
        fc1_scales = jax.random.uniform(ks[3], (H // G, F), jnp.float32) * 0.02 + 0.001
        fc2_scales = jax.random.uniform(ks[4], (F // G, H), jnp.float32) * 0.02 + 0.001
        fc1_bias = jax.random.normal(ks[5], (F,), jnp.float32) * 0.02
        fc2_bias = jax.random.normal(ks[6], (H,), jnp.float32) * 0.02
        return {'x': x, 'ln_gamma': ln_gamma, 'ln_beta': ln_beta, 'fc1_q': fc1_q, 'fc1_scales': fc1_scales, 'fc1_bias': fc1_bias, 'fc2_q': fc2_q, 'fc2_scales': fc2_scales, 'fc2_bias': fc2_bias}
    _L1_ffn_all = _L1_ffn_setup()
    _L1_ffn_in = {k: v for k, v in _L1_ffn_all.items() if k in ('ln_gamma', 'ln_beta', 'fc1_q', 'fc1_scales', 'fc1_bias', 'fc2_q', 'fc2_scales', 'fc2_bias')}
    del _L1_ffn_all
    return {'x': x, 'ctx_1024': ctx_1024, 'L0_ffn_norm_gamma': _L0_ffn_in['norm_gamma'], 'L0_ffn_slot_norm_gamma': _L0_ffn_in['slot_norm_gamma'], 'L0_ffn_slot_embeds': _L0_ffn_in['slot_embeds'], 'L0_ffn_w1': _L0_ffn_in['w1'], 'L0_ffn_b1': _L0_ffn_in['b1'], 'L0_ffn_w2': _L0_ffn_in['w2'], 'L0_ffn_b2': _L0_ffn_in['b2'], 'L1_xattn_Wq': _L1_xattn_in['Wq'], 'L1_xattn_bq': _L1_xattn_in['bq'], 'L1_xattn_Wk': _L1_xattn_in['Wk'], 'L1_xattn_bk': _L1_xattn_in['bk'], 'L1_xattn_Wv': _L1_xattn_in['Wv'], 'L1_xattn_bv': _L1_xattn_in['bv'], 'L1_xattn_Wo': _L1_xattn_in['Wo'], 'L1_xattn_bo': _L1_xattn_in['bo'], 'L1_xattn_w1': _L1_xattn_in['w1'], 'L1_xattn_b1': _L1_xattn_in['b1'], 'L1_xattn_w2': _L1_xattn_in['w2'], 'L1_xattn_b2': _L1_xattn_in['b2'], 'L1_xattn_w3': _L1_xattn_in['w3'], 'L1_xattn_b3': _L1_xattn_in['b3'], 'L1_ffn_ln_gamma': _L1_ffn_in['ln_gamma'], 'L1_ffn_ln_beta': _L1_ffn_in['ln_beta'], 'L1_ffn_fc1_q': _L1_ffn_in['fc1_q'], 'L1_ffn_fc1_scales': _L1_ffn_in['fc1_scales'], 'L1_ffn_fc1_bias': _L1_ffn_in['fc1_bias'], 'L1_ffn_fc2_q': _L1_ffn_in['fc2_q'], 'L1_ffn_fc2_scales': _L1_ffn_in['fc2_scales'], 'L1_ffn_fc2_bias': _L1_ffn_in['fc2_bias']}

def reference(x, ctx_1024, L0_ffn_norm_gamma, L0_ffn_slot_norm_gamma, L0_ffn_slot_embeds, L0_ffn_w1, L0_ffn_b1, L0_ffn_w2, L0_ffn_b2, L1_xattn_Wq, L1_xattn_bq, L1_xattn_Wk, L1_xattn_bk, L1_xattn_Wv, L1_xattn_bv, L1_xattn_Wo, L1_xattn_bo, L1_xattn_w1, L1_xattn_b1, L1_xattn_w2, L1_xattn_b2, L1_xattn_w3, L1_xattn_b3, L1_ffn_ln_gamma, L1_ffn_ln_beta, L1_ffn_fc1_q, L1_ffn_fc1_scales, L1_ffn_fc1_bias, L1_ffn_fc2_q, L1_ffn_fc2_scales, L1_ffn_fc2_bias):
    import jax
    import jax.numpy as jnp

    def _L0_xattn_ref(q, k, v):
        import jax, jax.numpy as jnp
        import numpy as np
        DECAY = 0.9
        kv = jnp.swapaxes(k * v, 0, 1)

        def step(r, kv_t):
            r = DECAY * r + kv_t
            return (r, r)
        r0 = jnp.zeros(q.shape[:1] + q.shape[2:], dtype=q.dtype)
        _, rs = jax.lax.scan(step, r0, kv)
        return q * jnp.swapaxes(rs, 0, 1)

    def _L0_ffn_ref(x, norm_gamma, slot_norm_gamma, slot_embeds, w1, b1, w2, b2):
        import jax, jax.numpy as jnp
        import numpy as np
        B, SEQ, DIM = (2, 512, 128)
        E, S = (8, 64)
        HID = 4 * DIM
        SCALE = DIM ** 0.5

        def rmsnorm(x, gamma):
            n = jnp.linalg.norm(x, axis=-1, keepdims=True)
            return x / jnp.maximum(n, 1e-12) * SCALE * gamma
        xn = rmsnorm(x, norm_gamma)
        sn = rmsnorm(slot_embeds, slot_norm_gamma)
        logits = jnp.einsum('bnd,esd->bnes', xn, sn)
        dispatch = jax.nn.softmax(logits, axis=1)
        b, n, e, s = logits.shape
        combine = jax.nn.softmax(logits.reshape(b, n, e * s), axis=-1)
        slots = jnp.einsum('bnd,bnes->besd', xn, dispatch)
        h = jnp.einsum('besd,edh->besh', slots, w1) + b1[None, :, None, :]
        h = jax.nn.gelu(h, approximate=False)
        eo = jnp.einsum('besh,ehd->besd', h, w2) + b2[None, :, None, :]
        eo = eo.reshape(b, e * s, DIM)
        out = jnp.einsum('bmd,bnm->bnd', eo, combine)
        return out

    def _L1_xattn_ref(query, key, value, Wq, bq, Wk, bk, Wv, bv, Wo, bo, w1, b1, w2, b2, w3, b3):
        import jax, jax.numpy as jnp
        import numpy as np
        import math
        B, S, D, H = (1, 256, 128, 16)
        DK = D // H
        DH = 64
        LOG_T_MIN = math.log(0.1)
        LOG_T_MAX = math.log(10.0)

        def _linear(x, W, b):
            return x @ W.T + b
        b, sq, d = query.shape
        sk = key.shape[1]
        h, dk = (H, DK)
        Q = _linear(query, Wq, bq).reshape(b, sq, h, dk).transpose(0, 2, 1, 3)
        K = _linear(key, Wk, bk).reshape(b, sk, h, dk).transpose(0, 2, 1, 3)
        V = _linear(value, Wv, bv).reshape(b, sk, h, dk).transpose(0, 2, 1, 3)
        qk = jnp.einsum('bhqd,bhkd->bhqk', Q, K)
        scores = qk / math.sqrt(dk)
        mean_sim = scores.mean(axis=(-2, -1))
        max_sim = scores.max(axis=-1).mean(axis=-1)
        probs = jax.nn.softmax(scores, axis=-1)
        entropy_proxy = jnp.var(probs, axis=-1, ddof=1).mean(axis=-1)
        feats = jnp.stack([mean_sim, max_sim, entropy_proxy], axis=-1)
        hidden = jax.nn.gelu(_linear(feats, w1, b1), approximate=False)
        hidden = jax.nn.gelu(_linear(hidden, w2, b2), approximate=False)
        log_t = jnp.clip(_linear(hidden, w3, b3), LOG_T_MIN, LOG_T_MAX)
        t = jnp.exp(log_t)[..., None]
        attn_scores = qk / (2.0 * t)
        attn = jax.nn.softmax(attn_scores, axis=-1)
        attn = jnp.nan_to_num(attn, nan=0.0)
        out = jnp.einsum('bhqk,bhkd->bhqd', attn, V)
        out = out.transpose(0, 2, 1, 3).reshape(b, sq, d)
        return _linear(out, Wo, bo)

    def _L1_ffn_ref(x, ln_gamma, ln_beta, fc1_q, fc1_scales, fc1_bias, fc2_q, fc2_scales, fc2_bias):
        import jax, jax.numpy as jnp
        import numpy as np
        B, S, H, F, G = (8, 256, 128, 512, 128)
        EPS = 1e-05

        def _dequant(q, scales, g):
            K, N = q.shape
            w = (q.astype(jnp.float32) - 128.0).reshape(K // g, g, N) * scales[:, None, :]
            return w.reshape(K, N)
        residual = x
        mu = jnp.mean(x, axis=-1, keepdims=True)
        var = jnp.mean(jnp.square(x - mu), axis=-1, keepdims=True)
        h = (x - mu) * jax.lax.rsqrt(var + EPS) * ln_gamma + ln_beta
        hf = h.reshape(-1, H)
        w1 = _dequant(fc1_q, fc1_scales, G)
        y = hf @ w1 + fc1_bias
        y = jax.nn.silu(y)
        w2 = _dequant(fc2_q, fc2_scales, G)
        z = y @ w2 + fc2_bias
        return residual + 0.5 * z.reshape(residual.shape)
    x = x + _L0_xattn_ref(_layernorm(x, axis=-1), ctx_1024, ctx_1024)
    x = x + _L0_ffn_ref(_layernorm(x, axis=-1), L0_ffn_norm_gamma, L0_ffn_slot_norm_gamma, L0_ffn_slot_embeds, L0_ffn_w1, L0_ffn_b1, L0_ffn_w2, L0_ffn_b2)
    x = x + _L1_xattn_ref(_layernorm(x, axis=-1), ctx_1024, ctx_1024, L1_xattn_Wq, L1_xattn_bq, L1_xattn_Wk, L1_xattn_bk, L1_xattn_Wv, L1_xattn_bv, L1_xattn_Wo, L1_xattn_bo, L1_xattn_w1, L1_xattn_b1, L1_xattn_w2, L1_xattn_b2, L1_xattn_w3, L1_xattn_b3)
    x = x + _L1_ffn_ref(_layernorm(x, axis=-1), L1_ffn_ln_gamma, L1_ffn_ln_beta, L1_ffn_fc1_q, L1_ffn_fc1_scales, L1_ffn_fc1_bias, L1_ffn_fc2_q, L1_ffn_fc2_scales, L1_ffn_fc2_bias)
    return x

_drawn_inputs = setup_inputs


def setup_inputs(seed=0):
    import zlib

    import numpy as np

    out = dict(_drawn_inputs(seed))
    spreads = {'L0_ffn_norm_gamma': (1.0, 0.6),
     'L0_ffn_slot_norm_gamma': (1.0, 0.6),
     'L0_ffn_b1': (0.0, 0.8),
     'L0_ffn_b2': (0.0, 0.8),
     'L1_ffn_ln_gamma': (1.0, 0.2),
     'L1_ffn_ln_beta': (0.0, 0.1)}
    factors = {'L0_ffn_slot_embeds': 8.0,
     'L0_ffn_w1': 8.0,
     'L0_ffn_w2': 8.0,
     'L1_xattn_Wq': 8.0,
     'L1_xattn_bq': 8.0,
     'L1_xattn_Wk': 8.0,
     'L1_xattn_bk': 64.0,
     'L1_xattn_Wv': 8.0,
     'L1_xattn_bv': 8.0,
     'L1_xattn_Wo': 8.0,
     'L1_xattn_bo': 23.81,
     'L1_xattn_w1': 29.595,
     'L1_xattn_b1': 200.0,
     'L1_xattn_w2': 200.0,
     'L1_xattn_b2': 8.0,
     'L1_xattn_w3': 64.0,
     'L1_ffn_fc1_scales': 77.589,
     'L1_ffn_fc1_bias': 200.0,
     'L1_ffn_fc2_bias': 200.0}
    for name, (base, spread) in spreads.items():
        noise = np.random.default_rng([zlib.crc32(name.encode()), seed]).standard_normal(out[name].shape)
        drawn = base * np.exp(spread * noise) if base else spread * noise
        out[name] = jnp.asarray(drawn.astype(out[name].dtype))
    for name, factor in factors.items():
        out[name] = (out[name] * factor).astype(out[name].dtype)
    return out
```

```python
from contextlib import ExitStack

import concourse.bass as bass
from concourse import mybir

fp32 = mybir.dt.float32
ALU = mybir.AluOpType
ACT = mybir.ActivationFunctionType
AX = mybir.AxisListType.X

B, S, D = 32, 64, 128
E, SL = 8, 64
ES = E * SL
HID = 4 * D
HC = HID // 128
H, DK = 16, 8
MH = 64
T = 4
GB = 2 * T
GROUPS = B // GB
TOK = 128 * T
VW = 2 * DK + 2
DECAY = 0.9
EPS = 1e-5
LOG_T = 2.302585092994046

C_B1, C_G1, C_G2, C_BQ, C_BK, C_FB, C_LG, C_LB = 0, 32, 33, 34, 35, 36, 40, 41
NVEC = 42


def build(nc, a, out):
    with ExitStack() as ctx:
        def sb(name, *shape):
            return ctx.enter_context(nc.sbuf_tensor(name, [128, *shape], fp32))

        def sem(name):
            return ctx.enter_context(nc.semaphore(name))

        ident = sb("ident", 128)
        diag64 = sb("diag64", 64)
        same_batch = sb("same_batch", 128)
        head16 = sb("head16", H)
        head8 = sb("head8", H // 2)
        decay_step = sb("decay_step", 128)
        decayT = sb("decayT", 128)
        power = sb("power", 2 * T)
        vec_rows = sb("vec_rows", 128)
        vecs = sb("vecs", NVEC)
        g12 = sb("g12", 1)
        slot_rows = sb("slot_rows", 4, D)
        slot_sq = sb("slot_sq", 4, D)
        slot_n = sb("slot_n", 4)
        snT = sb("snT", ES)
        w1 = sb("w1", E, HID)
        w2 = sb("w2", E, HC, D)
        b2_all = sb("b2_all", E, D)
        w_rows = sb("w_rows", 4, D)
        wqT = sb("wqT", D)
        wkT = sb("wkT", D)
        woT = sb("woT", D)
        wv_half = sb("wv_half", 2, H // 2, VW)
        bv_row = sb("bv_row", D)
        v_bias = sb("v_bias", H // 2, VW)
        bo_all = sb("bo_all", D)
        m1_row = sb("m1_row", 3, MH)
        m1_half = sb("m1_half", 2, 3, MH)
        m_small = ctx.enter_context(nc.sbuf_tensor("m_small", [MH, 4], fp32))
        m2_rows = ctx.enter_context(nc.sbuf_tensor("m2_rows", [MH, MH], fp32))
        m2T = ctx.enter_context(nc.sbuf_tensor("m2T", [MH, MH], fp32))
        m3_wide = ctx.enter_context(nc.sbuf_tensor("m3_wide", [MH, 64], fp32))
        b3_all = sb("b3_all", 1)
        fc1_q = ctx.enter_context(nc.sbuf_tensor("fc1_q", [128, HID], mybir.dt.int32))
        fc2_q = ctx.enter_context(nc.sbuf_tensor("fc2_q", [128, HC, D], mybir.dt.int32))
        fc1_s = sb("fc1_s", HID)
        fc2_s = sb("fc2_s", HC, D)
        fc1 = sb("fc1", HID)
        fc2 = sb("fc2", HC, D)
        fb2_half = sb("fb2_half", D)

        x_in = sb("x_in", T, D)
        ctx_in = sb("ctx_in", T, D)
        kv = sb("kv", T, D)
        ctxT = sb("ctxT", TOK)
        stats = sb("stats", T, 6)
        mv = sb("mv", T, 2)
        pow_in = sb("pow_in", 2 * T)
        pow_out = sb("pow_out", 2 * T)
        small = sb("small", 8, T)
        y = sb("y", T, D)
        x1 = sb("x1", T, D)
        xn = sb("xn", T, D)
        xnT = sb("xnT", TOK)
        wait_pad = sb("wait_pad", 1)
        nmC = sb("nmC", T)
        diagC = sb("diagC", T, S)
        nmC_all = sb("nmC_all", T, S)
        nmD = sb("nmD", E, T)
        LD = sb("LD", E, T, S)
        CT = sb("CT", E, T, S)
        sumD = sb("sumD", E, T)
        lnD = sb("lnD", E, T)
        nlse = sb("nlse", E, T)
        diagD = sb("diagD", 2, E, SL)
        dispatch = sb("dispatch", 2, ES)
        slotsT = sb("slotsT", E, GB, SL)
        hT = sb("hT", 2, HC, TOK)
        eo = sb("eo", E, T, D + 1)
        rC = sb("rC", T)
        x2 = sb("x2", T, D)
        x2b = sb("x2b", T, D)
        y2T = sb("y2T", TOK)
        QT = sb("QT", TOK)
        KT = sb("KT", TOK)
        KM = sb("KM", GB, H // 2, S)
        sumQ = sb("sumQ", GB)
        sumK = sb("sumK", GB)
        qk_sum = sb("qk_sum", GB)
        mean_rows = sb("mean_rows", 2, T, H)
        V = sb("V", GB, H // 2, VW)
        mx = sb("mx", T, H)
        Dm = slotsT[:, :, :, :].rearrange("p e b k -> p (e b k)").rearrange("p (j h k) -> p j h k", j=T, h=H)
        exps = hT[:, :, :, :].rearrange("p i c t -> p (i c t)").rearrange("p (f i h k) -> p f i h k", f=2, i=2, h=H)
        e1, e2 = exps[:, 0], exps[:, 1]
        s1 = sb("s1", T, H)
        s2 = sb("s2", T, H)
        var = sb("var", T, H)
        h1 = ctx.enter_context(nc.sbuf_tensor("h1", [MH, 2 * T * H], fp32))
        h2 = ctx.enter_context(nc.sbuf_tensor("h2", [MH, 2 * T * H], fp32))
        zt = sb("zt", T, H)
        inv_t = sb("inv_t", T, H)
        P = LD[:, :, :, :].rearrange("p e j n -> p (e j n)").rearrange("p (i h k) -> p i h k", i=2, h=H)
        PT = CT[:, :, :, :].rearrange("p e j n -> p (e j n)").rearrange("p (i c q) -> p i c q", i=2, c=H // 2)
        den = sb("den", T, H)
        ao = sb("ao", T, D)
        aoT = sb("aoT", TOK)
        x3 = sb("x3", T, D)
        y3 = sb("y3", T, D)
        h3 = sb("h3", T, D)
        acc = sb("acc", T, D)
        h3T = sb("h3T", TOK)
        uT = hT[:, 0]
        res = sb("res", T, D)

        tr = [ctx.enter_context(nc.psum_tensor(f"tr{i}", [128, 512], fp32)) for i in range(2)]
        wide = [ctx.enter_context(nc.psum_tensor(f"wide{i}", [128, 1024], fp32)) for i in range(2)]
        low = ctx.enter_context(nc.psum_tensor("low", [128, 1024], fp32))
        quad = [wide[i // 2][:, 512 * (i % 2):512 * (i % 2) + 512] for i in range(4)]
        duo = [low[:, 0:512], low[:, 512:1024]]

        names = """consts_in weights_in cast_in pool_consts dve_consts consts_pe vecs_up
            x_in_ready ctx_in_ready  kv_ready r_ready ctxT_up ctxT_ready x1_ready
            pow_asked pow_ready xn_ready xnT_up xnT_ready L_up L_used diagC_ready mC_up nmC_ready
            LT_up LD_ready LC_ready expD_ready CT_ready sumD_ready lnD_ready diagD_ready D_up D_ready
            slots_up0 slots_up1 slots_out0 slots_out1 h_up h_ready eo_up eo_ready out_up out_used x2b_ready
            y2_ready y2T_up y2T_ready QK_up QT_ready KT_ready KM_ready V_up V_ready
            S_up Dm_ready e1_ready e2_ready e_used stats_ready hid1_up hid1_ready hid2_up hid2_ready
            t_up zt_ready inv_t_ready Dt_ready P_ready PT_up PT_dve PT_act av_up ao_ready
            aoT_up aoT_ready o_up x3_ready h3_ready h3T_up h3T_ready u_up u_ready z_up res_ready
            acc_ready y3_ready out_done dve_pre dve_step act_pre act_step pool_pre pool_step w_up pre_pow pre_pow_out slotT_up mean_ready""".split()
        s = {n: sem(n) for n in names}

        block = ctx.enter_context(nc.Block())

        def nth(g, per, n):
            return g * per + n

        NC = 16
        V_STEPS = 46
        @block.sync
        def _(sp):
            sp.dma_start(slot_rows[:, :, :], a["L0_ffn_slot_embeds"].rearrange("e s d -> (e s) d").rearrange("(c p) d -> p c d", p=128)).then_inc(s["consts_in"], 16)
            for r0, n, src in ((C_B1, 32, a["L0_ffn_b1"].rearrange("e (c p) -> (e c) p", p=128)),
                               (C_G1, 1, a["L0_ffn_norm_gamma"].rearrange("(a p) -> a p", a=1)),
                               (C_G2, 1, a["L0_ffn_slot_norm_gamma"].rearrange("(a p) -> a p", a=1)),
                               (C_BQ, 1, a["L1_xattn_bq"].rearrange("(a p) -> a p", a=1)),
                               (C_BK, 1, a["L1_xattn_bk"].rearrange("(a p) -> a p", a=1)),
                               (C_FB, 4, a["L1_ffn_fc1_bias"].rearrange("(a p) -> a p", p=128)),
                               (C_LG, 1, a["L1_ffn_ln_gamma"].rearrange("(a p) -> a p", a=1)),
                               (C_LB, 1, a["L1_ffn_ln_beta"].rearrange("(a p) -> a p", a=1))):
                sp.dma_start(vec_rows[r0:r0 + n, :], src).then_inc(s["consts_in"], 16)
            for k, src in enumerate((a["L1_xattn_Wq"], a["L1_xattn_Wk"], a["L1_xattn_Wv"], a["L1_xattn_Wo"])):
                sp.dma_start(w_rows[:, k, :], src).then_inc(s["consts_in"], 16)
            sp.dma_start(m2_rows[:, :], a["L1_xattn_w2"]).then_inc(s["consts_in"], 16)
            sp.dma_start(fc1_q[:, :], a["L1_ffn_fc1_q"]).then_inc(s["consts_in"], 16)
            sp.dma_start(fc2_q[:, :, :], a["L1_ffn_fc2_q"].rearrange("(c p) d -> p c d", p=128)).then_inc(s["consts_in"], 16)
            x_groups, ctx_groups = (t.rearrange("b n d -> (b n) d").rearrange("(g j p) d -> g p j d", j=T, p=128)
                                    for t in (a["x"], a["ctx_1024"]))
            sp.dma_start(x_in[:, :, :], x_groups[0]).then_inc(s["x_in_ready"], 16)
            sp.dma_start(ctx_in[:, :, :], ctx_groups[0]).then_inc(s["ctx_in_ready"], 16)
            with sp.Fori(1, GROUPS) as g:
                sp.wait_ge(s["x1_ready"], g)
                sp.dma_start(x_in[:, :, :], x_groups[bass.ds(g, 1)].rearrange("a p j d -> (a p) j d")).then_inc(s["x_in_ready"], 16)
                sp.wait_ge(s["kv_ready"], g)
                sp.wait_ge(s["ctxT_up"], g)
                sp.dma_start(ctx_in[:, :, :], ctx_groups[bass.ds(g, 1)].rearrange("a p j d -> (a p) j d")).then_inc(s["ctx_in_ready"], 16)

        @block.gpsimd
        def _(pool):
            steps = [0]

            def link(ins):
                steps[0] += 1
                ins.then_inc(s["pool_pre"], 1)
                pool.wait_ge(s["pool_pre"], steps[0])

            pool.memset(ident[:, :], 0.0)
            pool.memset(same_batch[:, :], 0.0)
            pool.memset(head16[:, :], 1.0)
            pool.memset(decay_step[:, :], DECAY)
            pool.memset(power[:, 0:T], -0.5)
            pool.memset(power[:, T:2 * T], 0.5)
            pool.memset(wv_half[:, :, :, :], 0.0)
            pool.memset(v_bias[:, :, :], 0.0)
            link(pool.memset(m1_half[:, :, :, :], 0.0))
            link(pool.memset(eo[:, :, :, D:D + 1], 1.0))
            link(pool.memset(same_batch[0:64, 0:64], 1.0))
            link(pool.memset(same_batch[64:128, 64:128], 1.0))
            link(pool.memset(v_bias[0:64, :, 2 * DK:2 * DK + 1], 1.0))
            link(pool.memset(v_bias[64:128, :, 2 * DK + 1:2 * DK + 2], 1.0))
            pool.memset(decay_step[:, 64:65], 0.0)
            pool.affine_select(out=ident[:, :], in_=ident[:, :], compare_op=ALU.not_equal, fill=1.0,
                               base=0, pattern=[[-1, 128]], channel_multiplier=1)
            link(pool.affine_select(out=head16[:, :], in_=head16[:, :], compare_op=ALU.is_ge, fill=0.0,
                                    base=0, pattern=[[-DK, H]], channel_multiplier=1))
            pool.affine_select(out=head16[:, :], in_=head16[:, :], compare_op=ALU.is_ge, fill=0.0,
                               base=DK - 1, pattern=[[DK, H]], channel_multiplier=-1).then_inc(s["pool_consts"], 1)
            pool.wait_ge(s["pre_pow"], 1)
            pool.tensor_tensor(slot_n[:, :], slot_n[:, :], power[:, T:2 * T], ALU.pow).then_inc(s["pre_pow_out"], 1)
            with pool.Fori(0, GROUPS) as g:
                def powers(n, w):
                    pool.wait_ge(s["pow_asked"], nth(g, 5, n))
                    pool.tensor_tensor(pow_out[:, 0:w], pow_in[:, 0:w], power[:, 0:w], ALU.pow).then_inc(s["pow_ready"], 1)

                powers(1, T)
                powers(2, 2 * T)
                powers(3, T)
                pool.wait_ge(s["out_used"], nth(g, T, T))
                pool.tensor_tensor(x2b[:, :, :], x2[:, :, :], bo_all[:, :].unsqueeze(1).to_broadcast([128, T, D]), ALU.add).then_inc(s["x2b_ready"], 1)
                powers(4, T)
                powers(5, T)
                pool.wait_ge(s["y3_ready"], nth(g, 1, 1))
                pool.tensor_tensor(acc[:, :, :], x3[:, :, :], y3[:, :, :], ALU.add).then_inc(s["pool_step"], 1)
                pool.wait_ge(s["pool_step"], nth(g, 1, 1))
                pool.tensor_tensor(acc[:, :, :], acc[:, :, :], fb2_half[:, :].unsqueeze(1).to_broadcast([128, T, D]), ALU.add).then_inc(s["acc_ready"], 1)

        def slots(pe, g, j):
            pe.wait_ge(s["D_ready"], nth(g, T, j + 1))
            if j == 0:
                pe.wait_ge(s["LC_ready"], nth(g, 4, 4))
            if j >= 2:
                pe.wait_ge(s["slots_out0"], nth(g, T, j - 1))
                pe.wait_ge(s["slots_out1"], nth(g, T, j - 1))
            for par in range(2):
                p = slice(64 * par, 64 * par + 64)
                pe.matmul(quad[2 * (j % 2) + par], xn[p, j, :], dispatch[p, j % 2, :], start=True, stop=True)\
                  .then_inc(s[f"slots_up{par}"], 1)

        def plain_wait(eng):
            eng.wait_ge(s["pool_consts"], 1)

        @block.tensor
        def _(pe):
            def transposes(psum, src, sem_name):
                for j in range(T):
                    ins = pe.transpose(psum[:, 128 * j:128 * j + 128], src[:, j, :], ident[:, :])
                ins.then_inc(s[sem_name], 1)

            pe.wait_ge(s["pool_consts"], 1)
            pe.wait_ge(s["consts_in"], 16 * NC)
            pe.transpose(tr[0][:, 0:NVEC], vec_rows[0:NVEC, :], ident[0:NVEC, 0:NVEC]).then_inc(s["vecs_up"], 1)
            transposes(quad[0], w_rows, "w_up")
            pe.transpose(tr[1][0:MH, 0:MH], m2_rows[:, :], ident[0:MH, 0:MH]).then_inc(s["w_up"], 1)
            pe.wait_ge(s["dve_consts"], 1)
            transposes(quad[1], slot_rows, "slotT_up")
            pe.wait_ge(s["dve_consts"], 2)
            with pe.Fori(0, GROUPS) as g:
                pe.wait_ge(s["kv_ready"], nth(g, 1, 1))
                pe.wait_ge(s["res_ready"], nth(g, 1, 1))
                pe.matmul(tr[0][:, :], decayT[:, :], kv[:, :, :], start=True, stop=True).then_inc(s["r_ready"], 1)
                pe.wait_ge(s["ctx_in_ready"], nth(g, 16, 16))
                transposes(tr[1], ctx_in, "ctxT_up")
                pe.wait_ge(s["xn_ready"], nth(g, 1, 1))
                pe.wait_ge(s["ctxT_ready"], nth(g, 1, 1))
                transposes(tr[1], xn, "xnT_up")
                pe.wait_ge(s["xnT_ready"], nth(g, 1, 1))
                for j in range(T):
                    if j >= 2:
                        pe.wait_ge(s["L_used"], nth(g, T, j - 1))
                    pe.matmul(duo[j % 2], xnT[:, 128 * j:128 * j + 128], snT[:, :], start=True, stop=True).then_inc(s["L_up"], 1)
                xT = xnT[:, :].rearrange("p (j a n) -> p a j n", j=T, a=2)
                for q in range(4):
                    for par in range(2):
                        for e in (2 * q, 2 * q + 1):
                            c = 256 * (e % 2)
                            ins = pe.matmul(quad[q][64 * par:64 * par + 64, c:c + 256], snT[:, SL * e:SL * e + SL],
                                            xT[:, par], start=True, stop=True)
                    ins.then_inc(s["LT_up"], 1)
                pe.wait_ge(s["diagC_ready"], nth(g, 1, 1))
                pe.matmul(tr[0][:, 0:256], same_batch[:, :], diagC[:, :, :], start=True, stop=True).then_inc(s["mC_up"], 1)
                for j in range(T):
                    pe.wait_ge(s["diagD_ready"], nth(g, T, j + 1))
                    if j == 0:
                        pe.wait_ge(s["L_used"], nth(g, T, T))
                    else:
                        pe.wait_ge(s["D_ready"], nth(g, T, j))
                    pe.matmul(duo[j % 2], xnT[:, 128 * j:128 * j + 128], snT[:, :], start=True, stop=False)
                    pe.matmul(duo[j % 2], same_batch[:, :], diagD[:, j % 2, :, :], start=False, stop=True).then_inc(s["D_up"], 1)
                    if j >= 1:
                        slots(pe, g, j - 1)
                slots(pe, g, T - 1)
                pe.wait_ge(s["slots_out0"], nth(g, T, T))
                pe.wait_ge(s["slots_out1"], nth(g, T, T))

                def second(e):
                    if e >= 2:
                        pe.wait_ge(s["eo_ready"], nth(g, E, e - 1))
                    for j in range(T):
                        for c in range(HC):
                            if j == 0:
                                pe.wait_ge(s["h_ready"], nth(g, HC * E, HC * e + c + 1))
                            ins = pe.matmul(duo[e % 2][:, 128 * j:128 * j + 128], hT[:, e % 2, c, 128 * j:128 * j + 128],
                                            w2[:, e, c, :], start=(c == 0), stop=(c == HC - 1))
                    ins.then_inc(s["eo_up"], 1)

                for e in range(E):
                    for c in range(HC):
                        if e >= 1:
                            pe.wait_ge(s["h_ready"], nth(g, HC * E, HC * (e - 1) + c + 1))
                        pe.matmul(quad[c], w1[:, e, 128 * c:128 * c + 128], slotsT[:, e, :, :],
                                  start=True, stop=True).then_inc(s["h_up"], 1)
                    if e >= 1:
                        second(e - 1)
                second(E - 1)
                pe.wait_ge(s["eo_ready"], nth(g, E, E))
                for j in range(T):
                    if j >= 2:
                        pe.wait_ge(s["V_ready"], nth(g, T, j - 1))
                    for par in range(2):
                        for half in range(2):
                            b = 2 * j + par
                            ins = pe.matmul(duo[j % 2][64 * half:64 * half + 64, 144 * par:144 * par + 144],
                                            ctxT[:, 64 * b:64 * b + 64], wv_half[:, half, :, :], start=True, stop=True)
                    ins.then_inc(s["V_up"], 1)
                plain_wait(pe)
                pe.wait_ge(s["CT_ready"], nth(g, 4, 4))
                for j in range(T):
                    if j >= 2:
                        plain_wait(pe)
                        pe.wait_ge(s["out_used"], nth(g, T, j - 1))
                    for par in range(2):
                        p = slice(64 * par, 64 * par + 64)
                        for e in range(E):
                            ins = pe.matmul(tr[j % 2][p, 0:D + 1], CT[p, e, j, :], eo[p, e, j, :],
                                            start=(e == 0), stop=(e == E - 1))
                    ins.then_inc(s["out_up"], 1)
                pe.matmul(quad[2], wkT[:, :], ctxT[:, :], start=True, stop=True).then_inc(s["QK_up"], 1)
                pe.wait_ge(s["y2_ready"], nth(g, 1, 1))
                transposes(tr[0], y, "y2T_up")
                pe.wait_ge(s["y2T_ready"], nth(g, 1, 1))
                pe.matmul(quad[3], wqT[:, :], y2T[:, :], start=True, stop=True).then_inc(s["QK_up"], 1)
                plain_wait(pe)
                pe.wait_ge(s["QT_ready"], nth(g, 1, 1))
                pe.wait_ge(s["KM_ready"], nth(g, 1, 1))
                for j in range(T):
                    if j >= 2:
                        plain_wait(pe)
                        pe.wait_ge(s["Dm_ready"], nth(g, T, j - 1))
                    for par in range(2):
                        b = 2 * j + par
                        for half in range(2):
                            r = slice(64 * half, 64 * half + 64)
                            ins = pe.matmul(wide[j % 2][64 * par:64 * par + 64, 512 * half:512 * half + 512],
                                            QT[r, 64 * b:64 * b + 64], KM[r, b, :, :], start=True, stop=True)
                    ins.then_inc(s["S_up"], 1)
                pe.wait_ge(s["mean_ready"], nth(g, 1, 1))
                pe.wait_ge(s["stats_ready"], nth(g, 1, 1))
                for par in range(2):
                    for f, rows in enumerate((mean_rows[:, par, :, :], mx[:, :, :], var[:, :, :])):
                        ins = pe.matmul(tr[1][0:MH, 64 * par:64 * par + 64], m1_row[:, 0, :] if f == 0 else m1_half[:, par, f, :],
                                        rows, start=(f == 0), stop=(f == 2))
                ins.then_inc(s["hid1_up"], 1)
                plain_wait(pe)
                pe.wait_ge(s["hid1_ready"], nth(g, 1, 1))
                pe.matmul(tr[0][0:MH, 0:128], m2T[:, :], h1[:, :], start=True, stop=True).then_inc(s["hid2_up"], 1)
                plain_wait(pe)
                pe.wait_ge(s["hid2_ready"], nth(g, 1, 1))
                for par in range(2):
                    ins = pe.matmul(tr[1][64 * par:64 * par + 64, 0:64], m3_wide[:, :], h2[:, 64 * par:64 * par + 64],
                                    start=True, stop=True)
                ins.then_inc(s["t_up"], 1)
                pe.wait_ge(s["V_ready"], nth(g, T, T))

                def turn(j):
                    pe.wait_ge(s["P_ready"], nth(g, T, j + 1))
                    if j >= 2:
                        pe.wait_ge(s["PT_dve"], nth(g, T, j - 1))
                        pe.wait_ge(s["PT_act"], nth(g, T, j - 1))
                    for c in range(H // 2):
                        ins = pe.transpose(wide[j % 2][:, 128 * c:128 * c + 128], P[:, j % 2, 2 * c:2 * c + 2, :], ident[:, :])
                    ins.then_inc(s["PT_up"], 1)

                def av(j):
                    pe.wait_ge(s["PT_dve"], nth(g, T, j + 1))
                    pe.wait_ge(s["PT_act"], nth(g, T, j + 1))
                    if j == 1:
                        pe.wait_ge(s["zt_ready"], nth(g, 1, 1))
                    if j >= 2:
                        pe.wait_ge(s["ao_ready"], nth(g, T, j - 1))
                    for par in range(2):
                        for c in range(H // 2):
                            ins = pe.matmul(tr[j % 2][64 * par:64 * par + 64, VW * c:VW * c + VW],
                                            PT[:, j % 2, c, 64 * par:64 * par + 64], V[:, 2 * j + par, c, :],
                                            start=True, stop=True)
                    ins.then_inc(s["av_up"], 1)

                for j in range(T):
                    turn(j)
                    if j >= 1:
                        av(j - 1)
                av(T - 1)
                pe.wait_ge(s["ao_ready"], nth(g, T, T))
                transposes(duo[0], ao, "aoT_up")
                pe.wait_ge(s["aoT_ready"], nth(g, 1, 1))
                for j in range(T):
                    ins = pe.matmul(duo[1][:, 128 * j:128 * j + 128], aoT[:, 128 * j:128 * j + 128], woT[:, :], start=True, stop=True)
                ins.then_inc(s["o_up"], 1)
                pe.wait_ge(s["h3_ready"], nth(g, 1, 1))
                transposes(tr[0], h3, "h3T_up")
                pe.wait_ge(s["h3T_ready"], nth(g, 1, 1))
                for c in range(HC):
                    pe.matmul(quad[c], fc1[:, 128 * c:128 * c + 128], h3T[:, :], start=True, stop=True).then_inc(s["u_up"], 1)
                pe.wait_ge(s["u_ready"], nth(g, HC, HC))
                for j in range(T):
                    for c in range(HC):
                        ins = pe.matmul(tr[1][:, 128 * j:128 * j + 128], uT[:, c, 128 * j:128 * j + 128], fc2[:, c, :],
                                        start=(c == 0), stop=(c == HC - 1))
                ins.then_inc(s["z_up"], 1)

        @block.scalar
        def _(act):
            act.dma_start(w1[:, :, :], a["L0_ffn_w1"].rearrange("e d h -> d e h")).then_inc(s["weights_in"], 16)
            act.dma_start(w2[:, :, :, :], a["L0_ffn_w2"].rearrange("e (c p) d -> p (e c) d", p=128).rearrange("p (e c) d -> p e c d", e=E)).then_inc(s["weights_in"], 16)

            def wide_row(dst, src, n):
                act.dma_start(dst, src.rearrange("(a n) -> a n", a=1).to_broadcast([n, src.shape[0]])).then_inc(s["cast_in"], 16)

            wide_row(b2_all[:, :, :].rearrange("p e d -> p (e d)"), a["L0_ffn_b2"].rearrange("e d -> (e d)"), 128)
            wide_row(bv_row[:, :], a["L1_xattn_bv"], 128)
            wide_row(bo_all[:, :], a["L1_xattn_bo"], 128)
            wide_row(b3_all[:, :], a["L1_xattn_b3"], 128)
            wide_row(fc1_s[:, :], a["L1_ffn_fc1_scales"].rearrange("a n -> (a n)"), 128)
            wide_row(fc2_s[:, :, :].rearrange("p c d -> p (c d)"), a["L1_ffn_fc2_scales"].rearrange("c d -> (c d)"), 128)
            wide_row(fb2_half[:, :], a["L1_ffn_fc2_bias"], 128)
            with nc.allow_non_contiguous_dma(reason="the small network's weights, once"):
                for f in range(3):
                    act.dma_start(m1_row[:, f, :], a["L1_xattn_w1"].rearrange("m f -> f m")[f:f + 1, :].to_broadcast([128, MH])).then_inc(s["cast_in"], 16)
                act.dma_start(m_small[:, 0:1], a["L1_xattn_b1"].rearrange("(m a) -> m a", a=1)).then_inc(s["cast_in"], 16)
                act.dma_start(m_small[:, 1:2], a["L1_xattn_b2"].rearrange("(m a) -> m a", a=1)).then_inc(s["cast_in"], 16)
                act.dma_start(m_small[:, 2:3], a["L1_xattn_w3"].rearrange("a m -> m a")).then_inc(s["cast_in"], 16)
            act.wait_ge(s["dve_consts"], 2)
            act.sem_inc(s["out_done"], 16)
            act.sem_inc(s["res_ready"], 1)

            with act.Fori(0, GROUPS) as g:
                act.wait_ge(s["ctx_in_ready"], nth(g, 16, 16))
                act.activation(kv[:, :, :], ctx_in[:, :, :], ACT.Square).then_inc(s["kv_ready"], 1)
                act.wait_ge(s["ctxT_up"], nth(g, 1, 1))
                act.activation(ctxT[:, :], tr[1][:, :], ACT.Copy).then_inc(s["ctxT_ready"], 1)
                act.wait_ge(s["xnT_up"], nth(g, 1, 1))
                act.activation(xnT[:, :], tr[1][:, :], ACT.Copy).then_inc(s["xnT_ready"], 1)
                act.wait_ge(s["mC_up"], nth(g, 1, 1))
                act.activation(nmC_all[:, :, :], tr[0][:, 0:256], ACT.Copy).then_inc(s["nmC_ready"], 1)
                for q in range(4):
                    e = slice(2 * q, 2 * q + 2)
                    act.wait_ge(s["LD_ready"], nth(g, 4, q + 1))
                    act.activation(LD[:, e, :, :], LD[:, e, :, :], ACT.Exp).then_inc(s["expD_ready"], 1)
                for q in range(4):
                    e = slice(2 * q, 2 * q + 2)
                    act.wait_ge(s["LC_ready"], nth(g, 4, q + 1))
                    act.activation(CT[:, e, :, :], CT[:, e, :, :], ACT.Exp).then_inc(s["CT_ready"], 1)
                act.wait_ge(s["sumD_ready"], nth(g, 1, 1))
                act.activation(lnD[:, :, :], sumD[:, :, :], ACT.Ln).then_inc(s["lnD_ready"], 1)

                def slots_out(j):
                    act.wait_ge(s["slots_up1"], nth(g, T, j + 1))
                    act.activation(slotsT[:, :, 2 * j + 1, :], quad[2 * (j % 2) + 1].rearrange("p (e k) -> p e k", e=E),
                                   ACT.Copy, scale=vecs[:, C_G1:C_G1 + 1]).then_inc(s["slots_out1"], 1)

                for j in range(T):
                    act.wait_ge(s["D_up"], nth(g, T, j + 1))
                    if j >= 2:
                        act.wait_ge(s["slots_up1"], nth(g, T, j - 1))
                    act.activation(dispatch[:, j % 2, :], duo[j % 2], ACT.Exp).then_inc(s["D_ready"], 1)
                    if j >= 1:
                        slots_out(j - 1)
                slots_out(T - 1)
                for e in range(E):
                    for c in range(HC):
                        act.wait_ge(s["h_up"], nth(g, HC * E, HC * e + c + 1))
                        if e >= 2:
                            act.wait_ge(s["eo_up"], nth(g, E, e - 1))
                        act.activation(hT[:, e % 2, c, :], quad[c], ACT.Gelu,
                                       bias=vecs[:, C_B1 + HC * e + c:C_B1 + HC * e + c + 1]).then_inc(s["h_ready"], 1)
                act.wait_ge(s["QK_up"], nth(g, 2, 1))
                act.activation(KT[:, :], quad[2], ACT.Identity, bias=vecs[:, C_BK:C_BK + 1]).then_inc(s["KT_ready"], 1)
                act.wait_ge(s["y2T_up"], nth(g, 1, 1))
                act.activation(y2T[:, :], tr[0][:, :], ACT.Copy).then_inc(s["y2T_ready"], 1)
                act.wait_ge(s["QK_up"], nth(g, 2, 2))
                act.activation(QT[:, :], quad[3], ACT.Identity, bias=vecs[:, C_BQ:C_BQ + 1]).then_inc(s["QT_ready"], 1)
                for j in range(T):
                    act.wait_ge(s["Dm_ready"], nth(g, T, j + 1))
                    if j >= 2:
                        act.wait_ge(s["e_used"], nth(g, T, j - 1))
                    act.activation(e1[:, j % 2, :, :], Dm[:, j, :, :], ACT.Exp, scale=DK ** -0.5).then_inc(s["e1_ready"], 1)
                    act.activation(e2[:, j % 2, :, :], Dm[:, j, :, :], ACT.Exp, scale=2 * DK ** -0.5).then_inc(s["e2_ready"], 1)
                act.wait_ge(s["hid1_up"], nth(g, 1, 1))
                act.activation(h1[:, :], tr[1][0:MH, 0:128], ACT.Gelu, bias=m_small[:, 0:1]).then_inc(s["hid1_ready"], 1)
                act.wait_ge(s["hid2_up"], nth(g, 1, 1))
                act.activation(h2[:, :], tr[0][0:MH, 0:128], ACT.Gelu, bias=m_small[:, 1:2]).then_inc(s["hid2_ready"], 1)
                act.wait_ge(s["zt_ready"], nth(g, 1, 1))
                act.activation(inv_t[:, :, :], zt[:, :, :], ACT.Exp, scale=-1.0).then_inc(s["inv_t_ready"], 1)

                def turned(j):
                    act.wait_ge(s["PT_up"], nth(g, T, j + 1))
                    if j >= 2:
                        act.wait_ge(s["av_up"], nth(g, T, j - 1))
                    act.activation(PT[:, j % 2, 4:8, :], wide[j % 2][:, 512:1024], ACT.Relu).then_inc(s["PT_act"], 1)

                for j in range(T):
                    act.wait_ge(s["Dt_ready"], nth(g, T, j + 1))
                    if j >= 2:
                        act.wait_ge(s["PT_up"], nth(g, T, j - 1))
                    act.activation(P[:, j % 2, :, :], Dm[:, j, :, :], ACT.Exp, scale=0.5).then_inc(s["P_ready"], 1)
                    if j >= 1:
                        turned(j - 1)
                turned(T - 1)
                act.wait_ge(s["aoT_up"], nth(g, 1, 1))
                act.activation(aoT[:, :], duo[0], ACT.Copy).then_inc(s["aoT_ready"], 1)
                for c in range(HC):
                    act.wait_ge(s["u_up"], nth(g, HC, c + 1))
                    act.activation(uT[:, c, :], quad[c], ACT.Silu, bias=vecs[:, C_FB + c:C_FB + c + 1]).then_inc(s["u_ready"], 1)
                act.wait_ge(s["res_ready"], nth(g, 1, 2))
                dst = out.rearrange("b n d -> (b n) d").rearrange("(g j p) d -> g p j d", j=T, p=128)
                act.dma_start(dst[bass.ds(g, 1)].rearrange("a p j d -> (a p) j d"), res[:, :, :]).then_inc(s["out_done"], 16)
            act.wait_ge(s["out_done"], 16 * (GROUPS + 1))

        @block.vector
        def _(dve):
            n = [0]

            def pre(ins):
                n[0] += 1
                ins.then_inc(s["dve_pre"], 1)
                dve.wait_ge(s["dve_pre"], n[0])

            dve.wait_ge(s["pool_consts"], 1)
            dve.tensor_tensor(diag64[:, :], ident[:, 0:64], ident[:, 64:128], ALU.add)
            dve.tensor_tensor(head8[:, :], head16[:, 0:8], head16[:, 8:16], ALU.add)
            dve.tensor_tensor_scan(decayT[:, :], decay_step[:, :], ident[:, :], 0.0, ALU.mult, ALU.add)
            dve.wait_ge(s["consts_in"], 16 * NC)
            pre(dve.tensor_tensor(slot_sq[:, :, :], slot_rows[:, :, :], slot_rows[:, :, :], ALU.mult))
            dve.tensor_reduce(slot_n[:, :], slot_sq[:, :, :], AX, ALU.add).then_inc(s["pre_pow"], 1)
            dve.wait_ge(s["pre_pow_out"], 1)
            pre(dve.tensor_scalar(slot_n[:, :], slot_n[:, :], 1e-12, None, ALU.max))
            pre(dve.reciprocal(slot_n[:, :], slot_n[:, :]))
            pre(dve.tensor_scalar(slot_n[:, :], slot_n[:, :], float(D) ** 0.5, None, ALU.mult))
            dve.tensor_tensor(slot_rows[:, :, :], slot_rows[:, :, :], slot_n[:, :].unsqueeze(2).to_broadcast([128, 4, D]),
                              ALU.mult).then_inc(s["dve_consts"], 1)
            dve.wait_ge(s["vecs_up"], 1)
            pre(dve.tensor_copy(vecs[:, :], tr[0][:, 0:NVEC]))
            pre(dve.tensor_tensor(g12[:, :], vecs[:, C_G1:C_G1 + 1], vecs[:, C_G2:C_G2 + 1], ALU.mult))
            dve.wait_ge(s["w_up"], 2)
            wT = quad[0].rearrange("p (k d) -> p k d", k=4)
            dve.tensor_copy(wqT[:, :], wT[:, 0, :])
            dve.tensor_copy(wkT[:, :], wT[:, 1, :])
            dve.tensor_copy(woT[:, :], wT[:, 3, :])
            wv = wT[:, 2, :].rearrange("p (c a k) -> p c a k", a=2, k=DK)
            for half in range(2):
                dve.tensor_copy(wv_half[:, half, :, DK * half:DK * half + DK], wv[:, :, half, :])
            dve.tensor_copy(m2T[:, :], tr[1][0:MH, 0:MH])
            dve.wait_ge(s["cast_in"], 16 * 13)
            bv = bv_row[:, :].rearrange("p (c a k) -> p c a k", a=2, k=DK)
            for half in range(2):
                p = slice(64 * half, 64 * half + 64)
                dve.tensor_copy(v_bias[p, :, DK * half:DK * half + DK], bv[p, :, half, :])
            pre(dve.tensor_scalar(m1_row[:, 0, :], m1_row[:, 0, :], DK ** -0.5 / (S * S), None, ALU.mult))
            for half in range(2):
                p = slice(64 * half, 64 * half + 64)
                dve.tensor_scalar(m1_half[p, half, 1, :], m1_row[p, 1, :], DK ** -0.5 / S, None, ALU.mult)
                dve.tensor_scalar(m1_half[p, half, 2, :], m1_row[p, 2, :], 1.0 / (S * (S - 1)), None, ALU.mult)
            dve.tensor_copy(m3_wide[:, :], m_small[:, 2:3].to_broadcast([MH, 64]))
            pre(dve.tensor_scalar(fb2_half[:, :], fb2_half[:, :], 0.5, None, ALU.mult))
            dve.tensor_scalar(fc1[:, :], fc1_q[:, :], -128.0, None, ALU.add)
            pre(dve.tensor_scalar(fc2[:, :, :], fc2_q[:, :, :], -128.0, None, ALU.add))
            dve.tensor_tensor(fc1[:, :], fc1[:, :], fc1_s[:, :], ALU.mult)
            dve.tensor_tensor(fc2[:, :, :], fc2[:, :, :], fc2_s[:, :, :], ALU.mult)
            dve.wait_ge(s["weights_in"], 32)
            dve.wait_ge(s["slotT_up"], 1)
            dve.tensor_scalar(snT[:, :], quad[1], g12[:, :], None, ALU.mult).then_inc(s["dve_consts"], 1)
            dve.wait_ge(s["dve_consts"], 2)

            with dve.Fori(0, GROUPS) as g:
                k = [0]

                def link(ins):
                    k[0] += 1
                    ins.then_inc(s["dve_step"], 1)
                    dve.wait_ge(s["dve_step"], nth(g, V_STEPS, k[0]))

                def moments(src):
                    for j in range(T):
                        ins = dve.bn_stats(stats[:, j, :], src[:, j, :])
                    link(ins)
                    dve.memset(wait_pad[:, :], 0.0)
                    for j in range(T):
                        ins = dve.bn_aggr(mv[:, j, :], stats[:, j, :])
                    link(ins)

                dve.wait_ge(s["x_in_ready"], nth(g, 16, 16))
                moments(x_in)
                dve.tensor_scalar(pow_in[:, 0:T], mv[:, :, 1], EPS, None, ALU.add).then_inc(s["pow_asked"], 1)
                dve.wait_ge(s["pow_ready"], nth(g, 5, 1))
                for j in range(T):
                    ins = dve.tensor_scalar(y[:, j, :], x_in[:, j, :], mv[:, j, 0:1], pow_out[:, j:j + 1], ALU.subtract, ALU.mult)
                link(ins)
                dve.wait_ge(s["r_ready"], nth(g, 1, 1))
                link(dve.tensor_tensor(y[:, :, :], y[:, :, :], tr[0][:, :].rearrange("p (j d) -> p j d", j=T), ALU.mult))
                dve.tensor_tensor(x1[:, :, :], x_in[:, :, :], y[:, :, :], ALU.add).then_inc(s["x1_ready"], 1)
                dve.wait_ge(s["x1_ready"], nth(g, 1, 1))
                moments(x1)
                dve.tensor_scalar(pow_in[:, 0:T], mv[:, :, 1], EPS, None, ALU.add)
                dve.tensor_scalar(pow_in[:, T:2 * T], mv[:, :, 1], float(D), None, ALU.mult).then_inc(s["pow_asked"], 1)
                dve.wait_ge(s["pow_ready"], nth(g, 5, 2))
                link(dve.tensor_tensor(small[:, 0, :], pow_out[:, 0:T], pow_out[:, T:2 * T], ALU.mult))
                link(dve.tensor_scalar(small[:, 1, :], small[:, 0, :], 1e-12, None, ALU.max))
                link(dve.reciprocal(small[:, 2, :], small[:, 1, :]))
                link(dve.scalar_tensor_tensor(small[:, 3, :], small[:, 2, :], float(D) ** 0.5, pow_out[:, 0:T], ALU.mult, ALU.mult))
                for j in range(T):
                    ins = dve.tensor_scalar(xn[:, j, :], x1[:, j, :], mv[:, j, 0:1], small[:, 3, j:j + 1], ALU.subtract, ALU.mult)
                ins.then_inc(s["xn_ready"], 1)
                for j in range(T):
                    dve.wait_ge(s["L_up"], nth(g, T, j + 1))
                    dve.tensor_reduce(nmC[:, j:j + 1], duo[j % 2], AX, ALU.max, negate=True).then_inc(s["L_used"], 1)
                dve.wait_ge(s["L_used"], nth(g, T, T))
                dve.tensor_tensor(diagC[:, :, :], diag64[:, :].unsqueeze(1).to_broadcast([128, T, S]),
                                  nmC[:, :].unsqueeze(2).to_broadcast([128, T, S]), ALU.mult).then_inc(s["diagC_ready"], 1)
                LT = [quad[q].rearrange("p (e j n) -> p e j n", e=2, j=T) for q in range(4)]
                for q in range(4):
                    e = slice(2 * q, 2 * q + 2)
                    dve.wait_ge(s["LT_up"], nth(g, 4, q + 1))
                    link(dve.tensor_reduce(nmD[:, e, :], LT[q], AX, ALU.max, negate=True))
                    dve.tensor_tensor(LD[:, e, :, :], LT[q], nmD[:, e, :].unsqueeze(3).to_broadcast([128, 2, T, S]), ALU.add).then_inc(s["LD_ready"], 1)
                dve.wait_ge(s["nmC_ready"], nth(g, 1, 1))
                for q in range(4):
                    dve.tensor_tensor(CT[:, 2 * q:2 * q + 2, :, :].rearrange("p e j n -> p e (j n)"), quad[q].rearrange("p (e t) -> p e t", e=2),
                                      nmC_all[:, :, :].rearrange("p j n -> p (j n)").unsqueeze(1).to_broadcast([128, 2, T * S]), ALU.add).then_inc(s["LC_ready"], 1)
                for q in range(4):
                    e = slice(2 * q, 2 * q + 2)
                    dve.wait_ge(s["expD_ready"], nth(g, 4, q + 1))
                    ins = dve.tensor_reduce(sumD[:, e, :], LD[:, e, :, :], AX, ALU.add)
                ins.then_inc(s["sumD_ready"], 1)
                dve.wait_ge(s["lnD_ready"], nth(g, 1, 1))
                link(dve.tensor_tensor(nlse[:, :, :], nmD[:, :, :], lnD[:, :, :], ALU.subtract))

                def slots_out(j):
                    dve.wait_ge(s["slots_up0"], nth(g, T, j + 1))
                    dve.tensor_scalar(slotsT[:, :, 2 * j, :], quad[2 * (j % 2)].rearrange("p (e k) -> p e k", e=E),
                                      vecs[:, C_G1:C_G1 + 1], None, ALU.mult).then_inc(s["slots_out0"], 1)

                for j in range(T):
                    if j >= 2:
                        dve.wait_ge(s["D_up"], nth(g, T, j - 1))
                    dve.tensor_tensor(diagD[:, j % 2, :, :], diag64[:, :].unsqueeze(1).to_broadcast([128, E, SL]),
                                      nlse[:, :, j].unsqueeze(2).to_broadcast([128, E, SL]), ALU.mult).then_inc(s["diagD_ready"], 1)
                    if j >= 2:
                        slots_out(j - 2)
                slots_out(T - 2)
                slots_out(T - 1)
                for e in range(E):
                    dve.wait_ge(s["eo_up"], nth(g, E, e + 1))
                    dve.tensor_tensor(eo[:, e, :, 0:D], duo[e % 2].rearrange("p (j d) -> p j d", j=T),
                                      b2_all[:, e, :].unsqueeze(1).to_broadcast([128, T, D]), ALU.add).then_inc(s["eo_ready"], 1)
                for j in range(T):
                    dve.wait_ge(s["V_up"], nth(g, T, j + 1))
                    dve.tensor_tensor(V[:, 2 * j:2 * j + 2, :, :].rearrange("p b c w -> p b (c w)"), duo[j % 2][:, 0:288].rearrange("p (b w) -> p b w", b=2),
                                      v_bias[:, :, :].rearrange("p c w -> p (c w)").unsqueeze(1).to_broadcast([128, 2, VW * H // 2]), ALU.add).then_inc(s["V_ready"], 1)
                for j in range(T):
                    dve.wait_ge(s["out_up"], nth(g, T, j + 1))
                    link(dve.reciprocal(rC[:, j:j + 1], tr[j % 2][:, D:D + 1]))
                    dve.scalar_tensor_tensor(x2[:, j, :], tr[j % 2][:, 0:D], rC[:, j:j + 1], x1[:, j, :], ALU.mult, ALU.add).then_inc(s["out_used"], 1)
                dve.wait_ge(s["out_used"], nth(g, T, T))
                moments(x2)
                dve.tensor_scalar(pow_in[:, 0:T], mv[:, :, 1], EPS, None, ALU.add).then_inc(s["pow_asked"], 1)
                dve.wait_ge(s["pow_ready"], nth(g, 5, 3))
                for j in range(T):
                    ins = dve.tensor_scalar(y[:, j, :], x2[:, j, :], mv[:, j, 0:1], pow_out[:, j:j + 1], ALU.subtract, ALU.mult)
                ins.then_inc(s["y2_ready"], 1)
                dve.wait_ge(s["KT_ready"], nth(g, 1, 1))
                for h in range(H // 2):
                    ins = dve.tensor_scalar(KM[:, :, h, :], KT[:, :].rearrange("p (b n) -> p b n", b=GB), head8[:, h:h + 1], None, ALU.mult)
                ins.then_inc(s["KM_ready"], 1)
                dve.tensor_reduce(sumK[:, :], KT[:, :].rearrange("p (b n) -> p b n", b=GB), AX, ALU.add)
                dve.wait_ge(s["QT_ready"], nth(g, 1, 1))
                link(dve.tensor_reduce(sumQ[:, :], QT[:, :].rearrange("p (b n) -> p b n", b=GB), AX, ALU.add))
                link(dve.tensor_tensor(qk_sum[:, :], sumQ[:, :], sumK[:, :], ALU.mult))
                for par in range(2):
                    ins = dve.tensor_tensor(mean_rows[:, par, :, :], head16[:, :].unsqueeze(1).to_broadcast([128, T, H]),
                                            qk_sum[:, par:GB:2].unsqueeze(2).to_broadcast([128, T, H]), ALU.mult)
                ins.then_inc(s["mean_ready"], 1)

                def sums(j):
                    dve.wait_ge(s["e1_ready"], nth(g, T, j + 1))
                    dve.tensor_reduce(s1[:, j, :], e1[:, j % 2, :, :], AX, ALU.add)
                    dve.wait_ge(s["e2_ready"], nth(g, T, j + 1))
                    dve.tensor_reduce(s2[:, j, :], e2[:, j % 2, :, :], AX, ALU.add).then_inc(s["e_used"], 1)

                for j in range(T):
                    sc = wide[j % 2][:, :].rearrange("p (h k) -> p h k", h=H)
                    dve.wait_ge(s["S_up"], nth(g, T, j + 1))
                    link(dve.tensor_reduce(mx[:, j, :], sc, AX, ALU.max))
                    dve.tensor_tensor(Dm[:, j, :, :], sc, mx[:, j, :].unsqueeze(2).to_broadcast([128, H, S]), ALU.subtract).then_inc(s["Dm_ready"], 1)
                    if j >= 1:
                        sums(j - 1)
                sums(T - 1)
                dve.wait_ge(s["e_used"], nth(g, T, T))
                link(dve.reciprocal(var[:, :, :], s1[:, :, :]))
                link(dve.tensor_tensor(var[:, :, :], var[:, :, :], var[:, :, :], ALU.mult))
                link(dve.tensor_tensor(var[:, :, :], var[:, :, :], s2[:, :, :], ALU.mult))
                dve.tensor_scalar(var[:, :, :], var[:, :, :], -1.0 / S, None, ALU.add).then_inc(s["stats_ready"], 1)
                dve.wait_ge(s["t_up"], nth(g, 1, 1))
                link(dve.tensor_scalar(zt[:, :, :], tr[1][:, 0:64].rearrange("p (j h) -> p j h", j=T), b3_all[:, :], -LOG_T, ALU.add, ALU.max))
                dve.tensor_scalar(zt[:, :, :], zt[:, :, :], LOG_T, None, ALU.min).then_inc(s["zt_ready"], 1)
                dve.wait_ge(s["inv_t_ready"], nth(g, 1, 1))

                def turned(j):
                    dve.wait_ge(s["PT_up"], nth(g, T, j + 1))
                    if j >= 2:
                        dve.wait_ge(s["av_up"], nth(g, T, j - 1))
                    dve.tensor_scalar(PT[:, j % 2, 0:4, :], wide[j % 2][:, 0:512].rearrange("p (c q) -> p c q", c=4), 0.0, None, ALU.max).then_inc(s["PT_dve"], 1)

                def normalise(j):
                    dve.wait_ge(s["av_up"], nth(g, T, j + 1))
                    av = tr[j % 2][:, 0:VW * H // 2].rearrange("p (c w) -> p c w", c=H // 2)
                    dj = den[:, j, :].rearrange("p (c a) -> p c a", a=2)
                    link(dve.tensor_scalar(dj, av[:, :, 2 * DK:VW], 1e-30, None, ALU.max))
                    link(dve.reciprocal(den[:, j, :], den[:, j, :]))
                    dve.tensor_tensor(ao[:, j, :].rearrange("p (c a k) -> p c a k", a=2, k=DK), av[:, :, 0:2 * DK].rearrange("p c (a k) -> p c a k", a=2),
                                      dj.unsqueeze(3).to_broadcast([128, H // 2, 2, DK]), ALU.mult).then_inc(s["ao_ready"], 1)

                for j in range(T):
                    dve.tensor_tensor(Dm[:, j, :, :], Dm[:, j, :, :], inv_t[:, j, :].unsqueeze(2).to_broadcast([128, H, S]), ALU.mult).then_inc(s["Dt_ready"], 1)
                    if j >= 1:
                        turned(j - 1)
                    if j >= 2:
                        normalise(j - 2)
                turned(T - 1)
                normalise(T - 2)
                normalise(T - 1)
                dve.wait_ge(s["o_up"], nth(g, 1, 1))
                dve.wait_ge(s["x2b_ready"], nth(g, 1, 1))
                link(dve.tensor_tensor(x3[:, :, :], x2b[:, :, :], duo[1].rearrange("p (j d) -> p j d", j=T), ALU.add))
                moments(x3)
                dve.tensor_scalar(pow_in[:, 0:T], mv[:, :, 1], EPS, None, ALU.add).then_inc(s["pow_asked"], 1)
                dve.wait_ge(s["pow_ready"], nth(g, 5, 4))
                link(dve.tensor_copy(small[:, 4, :], pow_out[:, 0:T]))
                link(dve.tensor_tensor(small[:, 5, :], small[:, 4, :], small[:, 4, :], ALU.mult))
                link(dve.tensor_tensor(small[:, 6, :], small[:, 5, :], mv[:, :, 1], ALU.mult))
                dve.tensor_scalar(pow_in[:, 0:T], small[:, 6, :], EPS, None, ALU.add).then_inc(s["pow_asked"], 1)
                dve.wait_ge(s["pow_ready"], nth(g, 5, 5))
                link(dve.tensor_tensor(small[:, 7, :], small[:, 4, :], pow_out[:, 0:T], ALU.mult))
                for j in range(T):
                    ins = dve.tensor_scalar(h3[:, j, :], x3[:, j, :], mv[:, j, 0:1], small[:, 7, j:j + 1], ALU.subtract, ALU.mult)
                ins.then_inc(s["h3_ready"], 1)
                for j in range(T):
                    ins = dve.tensor_scalar(y3[:, j, :], x3[:, j, :], mv[:, j, 0:1], small[:, 4, j:j + 1], ALU.subtract, ALU.mult)
                ins.then_inc(s["y3_ready"], 1)
                dve.wait_ge(s["h3T_up"], nth(g, 1, 1))
                dve.tensor_scalar(h3T[:, :], tr[0][:, :], vecs[:, C_LG:C_LG + 1], vecs[:, C_LB:C_LB + 1], ALU.mult, ALU.add).then_inc(s["h3T_ready"], 1)
                dve.wait_ge(s["z_up"], nth(g, 1, 1))
                dve.wait_ge(s["acc_ready"], nth(g, 1, 1))
                dve.wait_ge(s["out_done"], nth(g, 16, 16))
                dve.scalar_tensor_tensor(res[:, :, :].rearrange("p j d -> p (j d)"), tr[1][:, :], 0.5, acc[:, :, :].rearrange("p j d -> p (j d)"), ALU.mult, ALU.add).then_inc(s["res_ready"], 1)
                assert k[0] == V_STEPS, k[0]


_INS = ['x', 'ctx_1024', 'L0_ffn_norm_gamma', 'L0_ffn_slot_norm_gamma', 'L0_ffn_slot_embeds', 'L0_ffn_w1', 'L0_ffn_b1',
        'L0_ffn_w2', 'L0_ffn_b2', 'L1_xattn_Wq', 'L1_xattn_bq', 'L1_xattn_Wk', 'L1_xattn_bk', 'L1_xattn_Wv', 'L1_xattn_bv',
        'L1_xattn_Wo', 'L1_xattn_bo', 'L1_xattn_w1', 'L1_xattn_b1', 'L1_xattn_w2', 'L1_xattn_b2', 'L1_xattn_w3',
        'L1_xattn_b3', 'L1_ffn_ln_gamma', 'L1_ffn_ln_beta', 'L1_ffn_fc1_q', 'L1_ffn_fc1_scales', 'L1_ffn_fc1_bias',
        'L1_ffn_fc2_q', 'L1_ffn_fc2_scales', 'L1_ffn_fc2_bias']


def kernel(**inputs):
    import numpy as _np
    import concourse.bacc as _bacc
    from concourse import mybir as _mybir
    from concourse.bass_utils import run_bass_kernel_spmd as _run

    nc = _bacc.Bacc("TRN2", target_bir_lowering=False, num_devices=1)
    arrays, args = {}, {}
    for name in _INS:
        v = _np.ascontiguousarray(inputs[name])
        arrays[f"in_{name}"] = v
        args[name] = nc.dram_tensor(f"in_{name}", v.shape, _mybir.dt.from_np(v.dtype), kind="ExternalInput").ap()
    out = nc.dram_tensor("out_0", (32, 64, 128), _mybir.dt.float32, kind="ExternalOutput").ap()
    build(nc, args, out)
    r = _run(nc, [arrays], core_ids=[0])
    return r.results[0]["out_0"]
```

```python
from contextlib import ExitStack

import concourse.bass as bass
from concourse import mybir

fp32 = mybir.dt.float32
ALU = mybir.AluOpType
ACT = mybir.ActivationFunctionType
AX = mybir.AxisListType.X

B, S, D = 32, 64, 128
E, SL = 8, 64
ES = E * SL
EP = E // 2
HID = 4 * D
HC = HID // 128
H, DK = 16, 8
HP = H // 2
MH = 64
T = 2
GB = 2 * T
GROUPS = B // GB
TOK = 128 * T
TH = T * H
VW = 2 * DK + 2
DECAY = 0.9
EPS = 1e-5
LOG_T = 2.302585092994046

C_B1, C_G1, C_G2, C_BQ, C_BK, C_FB, C_LG, C_LB = 0, 32, 33, 34, 35, 36, 40, 41
NVEC = 42

FIRSTS = 2 * E
ORDER = []
for _p in range(EP):
    ORDER += [("first", n) for n in range(4 * _p + (_p > 0), 4 * _p + 4)]
    if _p < EP - 1:
        ORDER.append(("first", 4 * _p + 4))
    ORDER += [("second", _p, b) for b in range(GB)]
PIECES = len(ORDER)
STEPS_AT = {
    "attend": (1, 3, 5, 7, 13, 15, 15, 18, 20, 21, 22, 22, 23, 24, 24, 26, 28, 30, 31),
    "feed": (1, 3, 6, 8),
    "turn": (2,),
    "first_consts": (3, 9, 11),
    "later_consts": (2, 16),
    "route": (3, 6, 9, 13, 17, 17, 22, 24, 24, 27, 30, 31),
}


def nth(g, per, n):
    return g * per + n


def before(g):
    return not isinstance(g, int) or g > 0


def iteration(it, experts, stages, steps_first):
    running = []
    for name, shift in (("attend", -1), ("feed", -2), ("turn", 0), ("route", 1)):
        g = it + shift
        if not isinstance(g, int) or 0 <= g < GROUPS:
            running.append((stages[name](g), STEPS_AT[name]))
    for name, when in (("first_consts", -1), ("later_consts", 0)):
        if isinstance(it, int) and it == when:
            running.append((stages[name](), STEPS_AT[name]))
    pieces = not isinstance(it, int) or 0 <= it < GROUPS
    for i in range(PIECES):
        if pieces and not steps_first:
            experts(it, i)
        for stage, at in running:
            for _ in range(at.count(i)):
                next(stage)
        if pieces and steps_first:
            experts(it, i)
    if pieces:
        experts(it, PIECES)


def all_iterations(eng, experts, stages, steps_first=False):
    for it in (-1, 0, 1):
        iteration(it, experts, stages, steps_first)
    with eng.Fori(2, GROUPS - 2) as it:
        iteration(it, experts, stages, steps_first)
    for it in range(GROUPS - 2, GROUPS + 2):
        iteration(it, experts, stages, steps_first)


def build(nc, a, out):
    with ExitStack() as ctx:
        def sb(name, *shape):
            return ctx.enter_context(nc.sbuf_tensor(name, [128, *shape], fp32))

        ident = sb("ident", 128)
        head16 = sb("head16", H)
        head8 = sb("head8", HP)
        decay_step = sb("decay_step", 128)
        decayT = sb("decayT", 128)
        power = sb("power", 2 * T)
        half_power = sb("half_power", 4)
        vec_rows = sb("vec_rows", 128)
        vecs = sb("vecs", NVEC)
        g12 = sb("g12", 1)
        slot_rows = sb("slot_rows", 4, D)
        slot_sq = sb("slot_sq", 4, D)
        slot_n = sb("slot_n", 4)
        snT = sb("snT", ES)
        w1 = sb("w1", E, HID)
        w2 = sb("w2", E, HC, D)
        b2_pair = sb("b2_pair", EP, D)
        w_rows = sb("w_rows", 4, D)
        wqT = sb("wqT", D)
        wkT = sb("wkT", D)
        woT = sb("woT", D)
        wv_half = sb("wv_half", 2, HP, VW)
        bv_row = sb("bv_row", D)
        v_bias = sb("v_bias", HP, VW)
        bo_all = sb("bo_all", D)
        m1_row = sb("m1_row", 3, MH)
        m1_half = sb("m1_half", 2, 3, MH)
        m_small = ctx.enter_context(nc.sbuf_tensor("m_small", [MH, 4], fp32))
        m2_rows = ctx.enter_context(nc.sbuf_tensor("m2_rows", [MH, MH], fp32))
        m2T = ctx.enter_context(nc.sbuf_tensor("m2T", [MH, MH], fp32))
        m3_wide = ctx.enter_context(nc.sbuf_tensor("m3_wide", [MH, 64], fp32))
        b3_all = sb("b3_all", 1)
        fc1_q = ctx.enter_context(nc.sbuf_tensor("fc1_q", [128, HID], mybir.dt.int32))
        fc2_q = ctx.enter_context(nc.sbuf_tensor("fc2_q", [128, HC, D], mybir.dt.int32))
        fc1_s = sb("fc1_s", HID)
        fc2_s = sb("fc2_s", HC, D)
        fc1 = sb("fc1", HID)
        fc2 = sb("fc2", HC, D)
        fb2_half = sb("fb2_half", D)

        x_in = sb("x_in", T, D)
        ctx_in = sb("ctx_in", T, D)
        kv = sb("kv", T, D)
        ctxT = sb("ctxT", TOK)
        r_stats = sb("r_stats", T, 6)
        r_mv = sb("r_mv", T, 2)
        r_pow_in = sb("r_pow_in", 2 * T)
        r_pow = sb("r_pow", 2 * T)
        r_small = sb("r_small", 4, T)
        wait_pad = sb("wait_pad", 1)
        pool_pad = sb("pool_pad", 1)
        y1 = sb("y1", T, D)
        x1 = sb("x1", T, D)
        xn = sb("xn", T, D)
        xnT = sb("xnT", TOK)
        nmC = sb("nmC", T)
        C = sb("C", T, ES)
        sumC = sb("sumC", T)
        nmD = sb("nmD", EP, GB)
        DT = sb("DT", EP, TOK)
        sumD = sb("sumD", EP, GB)
        Dw = sb("Dw", T, ES)
        slotsT = sb("slotsT", E, GB, SL)
        CT = sb("CT", EP, TOK)
        x1b = sb("x1b", T, D)
        rC = sb("rC", T)
        hT = sb("hT", 2, 2, HC, TOK)
        eo = sb("eo", EP, GB, D)
        x2 = sb("x2", T, D)
        a_stats = sb("a_stats", T, 6)
        a_mv = sb("a_mv", T, 2)
        a_pow_in = sb("a_pow_in", T)
        a_pow = sb("a_pow", T)
        ctxT_kept = sb("ctxT_kept", TOK)
        x2b = sb("x2b", T, D)
        y2 = sb("y2", T, D)
        y2T = sb("y2T", TOK)
        QT = sb("QT", TOK)
        KT = sb("KT", TOK)
        KM = sb("KM", GB, HP, S)
        sumQ = sb("sumQ", GB)
        sumK = sb("sumK", GB)
        qk_sum = sb("qk_sum", GB)
        mean_rows = sb("mean_rows", 2, T, H)
        V = sb("V", GB, HP, VW)
        mx = sb("mx", T, H)
        Dm = sb("Dm", T, H, S)
        e1 = sb("e1", T, H, S)
        e2 = sb("e2", T, H, S)
        s1 = sb("s1", T, H)
        s2 = sb("s2", T, H)
        var = sb("var", T, H)
        h1 = ctx.enter_context(nc.sbuf_tensor("h1", [MH, 2 * TH], fp32))
        h2 = ctx.enter_context(nc.sbuf_tensor("h2", [MH, 2 * TH], fp32))
        zt = sb("zt", T, H)
        inv_t = sb("inv_t", T, H)
        P = sb("P", T, H, S)
        PT = sb("PT", T, HP, 128)
        den = sb("den", T, H)
        ao = sb("ao", T, D)
        aoT = sb("aoT", TOK)
        x3 = sb("x3", T, D)
        f_stats = sb("f_stats", T, 6)
        f_mv = sb("f_mv", T, 2)
        f_pow_in = sb("f_pow_in", T)
        f_pow = sb("f_pow", T)
        f_small = sb("f_small", 4, T)
        y3 = sb("y3", T, D)
        h3 = sb("h3", T, D)
        acc = sb("acc", T, D)
        h3T = sb("h3T", TOK)
        uT = sb("uT", HC, TOK)
        res = sb("res", T, D)

        def bank(name, n=1):
            return ctx.enter_context(nc.psum_tensor(name, [128, 512 * n], fp32))

        hid = [bank("hid0"), bank("hid1")]
        pair = bank("pair")
        mix = bank("mix")
        ra = [bank("ra0"), bank("ra1")]
        slot_banks = [ra, hid]
        at2 = bank("at", 2)
        at = [at2[:, 0:512], at2[:, 512:1024]]

        names = """vecs_in slots_in mats_in weights0_in weights1_in weights2_in weights3_in cast_in pool_consts dve_consts pool_pre dve_pre pre_pow pre_pow_out
            vecs_up w_up slotT_up later_consts
            x_in_ready ctx_in_ready kv_ready r_up ctxT_up ctxT_ready x1_ready xn_ready xnT_up xnT_ready
            L_up nmC_ready C_ready LT_up LD_ready expD_ready DT_ready D_up D_dve D_act
            slots_up slots_dve slots_act r_pow_asked r_pow_ready route_step
            CT_up CT_dve CT_act rC_ready x1b_ready kept_ready h_up h_ready eo_up eo_ready out_up x2_ready
            V_up V_ready K_up KT_ready KM_ready x2b_ready y2_ready y2T_up y2T_ready Q_up QT_ready mean_ready
            S_up Dm0_ready Dm1_ready e1_ready e2_ready stats_ready hid1_up hid1_ready hid2_up hid2_ready t_up zt_ready
            inv_t_ready Dt_ready P_ready PT_up PT_dve PT_act av_up ao_ready aoT_up aoT_ready o_up x3_ready
            a_pow_asked a_pow_ready attend_step f_pow_asked f_pow_ready feed_step
            h3_ready y3_ready h3T_up h3T_ready u_up u_ready z_up acc_step acc_ready res_ready out_done""".split()
        s = {n: ctx.enter_context(nc.semaphore(n)) for n in names}
        block = ctx.enter_context(nc.Block())
        VECS, MATS, CASTS = 8, 7, 14
        ROUTE_STEPS, ATTEND_STEPS, FEED_STEPS = 14, 17, 5

        def none(g=None):
            while True:
                yield

        @block.sync
        def _(sp):
            x_groups, ctx_groups, out_groups = (t.rearrange("b n d -> (b n) d").rearrange("(g j p) d -> g p j d", j=T, p=128)
                                                for t in (a["x"], a["ctx_1024"], out))

            def group(t, g):
                return t[g] if isinstance(g, int) else t[bass.ds(g, 1)].rearrange("a p j d -> (a p) j d")

            def load(g):
                if before(g):
                    sp.wait_ge(s["x1_ready"], nth(g, 1, 0))
                sp.dma_start(x_in[:, :, :], group(x_groups, g)).then_inc(s["x_in_ready"], 16)
                if before(g):
                    sp.wait_ge(s["kv_ready"], nth(g, 1, 0))
                    sp.wait_ge(s["ctxT_up"], nth(g, 1, 0))
                sp.dma_start(ctx_in[:, :, :], group(ctx_groups, g)).then_inc(s["ctx_in_ready"], 16)

            load(0)
            sp.dma_start(slot_rows[:, :, :], a["L0_ffn_slot_embeds"].rearrange("e s d -> (e s) d").rearrange("(c p) d -> p c d", p=128)).then_inc(s["slots_in"], 16)
            for r0, n, src in ((C_B1, 32, a["L0_ffn_b1"].rearrange("e (c p) -> (e c) p", p=128)),
                               (C_G1, 1, a["L0_ffn_norm_gamma"].rearrange("(a p) -> a p", a=1)),
                               (C_G2, 1, a["L0_ffn_slot_norm_gamma"].rearrange("(a p) -> a p", a=1)),
                               (C_BQ, 1, a["L1_xattn_bq"].rearrange("(a p) -> a p", a=1)),
                               (C_BK, 1, a["L1_xattn_bk"].rearrange("(a p) -> a p", a=1)),
                               (C_FB, 4, a["L1_ffn_fc1_bias"].rearrange("(a p) -> a p", p=128)),
                               (C_LG, 1, a["L1_ffn_ln_gamma"].rearrange("(a p) -> a p", a=1)),
                               (C_LB, 1, a["L1_ffn_ln_beta"].rearrange("(a p) -> a p", a=1))):
                sp.dma_start(vec_rows[r0:r0 + n, :], src).then_inc(s["vecs_in"], 16)
            w1_in = a["L0_ffn_w1"].rearrange("e d h -> d e h")
            w2_in = a["L0_ffn_w2"].rearrange("e (c p) d -> p (e c) d", p=128).rearrange("p (e c) d -> p e c d", e=E)
            for p in range(EP):
                e = slice(2 * p, 2 * p + 2)
                sp.dma_start(w1[:, e, :], w1_in[:, e, :]).then_inc(s[f"weights{p}_in"], 16)
                sp.dma_start(w2[:, e, :, :], w2_in[:, e, :, :]).then_inc(s[f"weights{p}_in"], 16)
            for k, src in enumerate((a["L1_xattn_Wq"], a["L1_xattn_Wk"], a["L1_xattn_Wv"], a["L1_xattn_Wo"])):
                sp.dma_start(w_rows[:, k, :], src).then_inc(s["mats_in"], 16)
            sp.dma_start(m2_rows[:, :], a["L1_xattn_w2"]).then_inc(s["mats_in"], 16)
            sp.dma_start(fc1_q[:, :], a["L1_ffn_fc1_q"]).then_inc(s["mats_in"], 16)
            sp.dma_start(fc2_q[:, :, :], a["L1_ffn_fc2_q"].rearrange("(c p) d -> p c d", p=128)).then_inc(s["mats_in"], 16)

            def wide_row(dst, src, n=128):
                sp.dma_start(dst, src.rearrange("(a n) -> a n", a=1).to_broadcast([n, src.shape[0]])).then_inc(s["cast_in"], 16)

            for k in range(2):
                sp.dma_start(b2_pair[64 * k:64 * k + 64, :, :],
                              a["L0_ffn_b2"].rearrange("(c k) d -> k c d", k=2)[k:k + 1].to_broadcast([64, EP, D])).then_inc(s["cast_in"], 16)
            wide_row(bv_row[:, :], a["L1_xattn_bv"])
            wide_row(bo_all[:, :], a["L1_xattn_bo"])
            wide_row(b3_all[:, :], a["L1_xattn_b3"])
            wide_row(fc1_s[:, :], a["L1_ffn_fc1_scales"].rearrange("a n -> (a n)"))
            wide_row(fc2_s[:, :, :].rearrange("p c d -> p (c d)"), a["L1_ffn_fc2_scales"].rearrange("c d -> (c d)"))
            wide_row(fb2_half[:, :], a["L1_ffn_fc2_bias"])
            with nc.allow_non_contiguous_dma(reason="the small network's weights, once"):
                for f in range(3):
                    sp.dma_start(m1_row[:, f, :], a["L1_xattn_w1"].rearrange("m f -> f m")[f:f + 1, :].to_broadcast([128, MH])).then_inc(s["cast_in"], 16)
                sp.dma_start(m_small[:, 0:1], a["L1_xattn_b1"].rearrange("(m a) -> m a", a=1)).then_inc(s["cast_in"], 16)
                sp.dma_start(m_small[:, 1:2], a["L1_xattn_b2"].rearrange("(m a) -> m a", a=1)).then_inc(s["cast_in"], 16)
                sp.dma_start(m_small[:, 2:3], a["L1_xattn_w3"].rearrange("a m -> m a")).then_inc(s["cast_in"], 16)

            def experts(g, i):
                pass

            def route(g):
                if not isinstance(g, int) or g + 1 < GROUPS:
                    load(g + 1)
                yield from none(g)

            def feed(g):
                yield
                yield
                yield
                sp.wait_ge(s["res_ready"], nth(g, 1, 2))
                sp.dma_start(group(out_groups, g), res[:, :, :]).then_inc(s["out_done"], 16)
                yield

            all_iterations(sp, experts, {"attend": none, "feed": feed, "turn": none, "route": route, "first_consts": none, "later_consts": none})
            sp.wait_ge(s["out_done"], 16 * (GROUPS + 1))

        @block.gpsimd
        def _(pool):
            steps = [0]

            def link(ins):
                steps[0] += 1
                ins.then_inc(s["pool_pre"], 1)
                pool.wait_ge(s["pool_pre"], steps[0])

            pool.memset(ident[:, :], 0.0)
            pool.memset(head16[:, :], 1.0)
            pool.memset(decay_step[:, :], DECAY)
            pool.memset(power[:, 0:T], -0.5)
            pool.memset(power[:, T:2 * T], 0.5)
            pool.memset(half_power[:, :], 0.5)
            pool.memset(wv_half[:, :, :, :], 0.0)
            pool.memset(v_bias[:, :, :], 0.0)
            link(pool.memset(m1_half[:, :, :, :], 0.0))
            link(pool.memset(v_bias[0:64, :, 2 * DK:2 * DK + 1], 1.0))
            link(pool.memset(v_bias[64:128, :, 2 * DK + 1:2 * DK + 2], 1.0))
            pool.memset(decay_step[:, 64:65], 0.0)
            pool.affine_select(out=ident[:, :], in_=ident[:, :], compare_op=ALU.not_equal, fill=1.0,
                               base=0, pattern=[[-1, 128]], channel_multiplier=1)
            link(pool.affine_select(out=head16[:, :], in_=head16[:, :], compare_op=ALU.is_ge, fill=0.0,
                                    base=0, pattern=[[-DK, H]], channel_multiplier=1))
            pool.affine_select(out=head16[:, :], in_=head16[:, :], compare_op=ALU.is_ge, fill=0.0,
                               base=DK - 1, pattern=[[DK, H]], channel_multiplier=-1).then_inc(s["pool_consts"], 1)

            def first_consts():
                yield
                pool.wait_ge(s["pre_pow"], 1)
                pool.tensor_tensor(slot_n[:, :], slot_n[:, :], half_power[:, :], ALU.pow).then_inc(s["pre_pow_out"], 1)
                yield
                yield

            def later_consts():
                yield
                pool.wait_ge(s["later_consts"], 1)
                yield

            def plain_wait():
                pool.wait_ge(s["pool_consts"], 1)

            def experts(g, i):
                pass

            def route(g):
                pool.wait_ge(s["r_pow_asked"], nth(g, 2, 1))
                pool.tensor_tensor(r_pow[:, 0:T], r_pow_in[:, 0:T], power[:, 0:T], ALU.pow).then_inc(s["r_pow_ready"], 1)
                yield
                pool.wait_ge(s["r_pow_asked"], nth(g, 2, 2))
                pool.tensor_tensor(r_pow[:, :], r_pow_in[:, :], power[:, :], ALU.pow).then_inc(s["r_pow_ready"], 1)
                yield from none(g)

            def turn(g):
                if before(g):
                    pool.wait_ge(s["x2_ready"], nth(g, 1, 0))
                pool.wait_ge(s["x1_ready"], nth(g, 1, 1))
                pool.tensor_tensor(pool_pad[:, :], power[:, 0:1], power[:, 0:1], ALU.add)
                pool.tensor_copy(x1b[:, :, :], x1[:, :, :]).then_inc(s["x1b_ready"], 1)
                plain_wait()
                if before(g):
                    pool.wait_ge(s["K_up"], nth(g, 1, 0))
                pool.wait_ge(s["ctxT_ready"], nth(g, 1, 1))
                pool.tensor_copy(ctxT_kept[:, :], ctxT[:, :]).then_inc(s["kept_ready"], 1)
                yield

            def attend(g):
                pool.wait_ge(s["a_pow_asked"], nth(g, 1, 1))
                pool.tensor_tensor(a_pow[:, :], a_pow_in[:, :], power[:, 0:T], ALU.pow).then_inc(s["a_pow_ready"], 1)
                if before(g):
                    pool.wait_ge(s["x3_ready"], nth(g, 1, 0))
                pool.wait_ge(s["x2_ready"], nth(g, 1, 1))
                pool.tensor_tensor(x2b[:, :, :], x2[:, :, :], bo_all[:, :].unsqueeze(1).to_broadcast([128, T, D]), ALU.add).then_inc(s["x2b_ready"], 1)
                for _ in STEPS_AT["attend"][1:]:
                    yield
                pool.wait_ge(s["f_pow_asked"], nth(g, 2, 1))
                pool.tensor_tensor(f_pow[:, :], f_pow_in[:, :], power[:, 0:T], ALU.pow).then_inc(s["f_pow_ready"], 1)
                yield

            def feed(g):
                pool.wait_ge(s["f_pow_asked"], nth(g, 2, 2))
                pool.tensor_tensor(f_pow[:, :], f_pow_in[:, :], power[:, 0:T], ALU.pow).then_inc(s["f_pow_ready"], 1)
                pool.wait_ge(s["y3_ready"], nth(g, 1, 1))
                if before(g):
                    pool.wait_ge(s["res_ready"], nth(g, 1, 1))
                pool.tensor_tensor(acc[:, :, :], x3[:, :, :], y3[:, :, :], ALU.add).then_inc(s["acc_step"], 1)
                pool.wait_ge(s["acc_step"], nth(g, 1, 1))
                pool.tensor_tensor(acc[:, :, :], acc[:, :, :], fb2_half[:, :].unsqueeze(1).to_broadcast([128, T, D]), ALU.add).then_inc(s["acc_ready"], 1)
                yield from none(g)

            all_iterations(pool, experts, {"attend": attend, "feed": feed, "turn": turn, "route": route,
                                 "first_consts": first_consts, "later_consts": later_consts})

        @block.tensor
        def _(pe):
            def plain_wait():
                pe.wait_ge(s["pool_consts"], 1)

            def transposes(psum, src, done, n=T):
                for j in range(n):
                    ins = pe.transpose(psum[:, 128 * j:128 * j + 128], src[:, j, :], ident[:, :])
                ins.then_inc(s[done], 1)

            pe.wait_ge(s["dve_consts"], 1)

            def first_consts():
                pe.wait_ge(s["vecs_in"], 16 * VECS)
                pe.transpose(mix[:, 0:NVEC], vec_rows[0:NVEC, :], ident[0:NVEC, 0:NVEC]).then_inc(s["vecs_up"], 1)
                yield
                yield
                pe.wait_ge(s["dve_consts"], 2)
                transposes(at[1], slot_rows, "slotT_up", 4)
                pe.wait_ge(s["dve_consts"], 3)
                yield

            def later_consts():
                pe.wait_ge(s["mats_in"], 16 * MATS)
                transposes(at[0], w_rows, "w_up", 4)
                pe.transpose(mix[0:MH, 0:MH], m2_rows[:, :], ident[0:MH, 0:MH]).then_inc(s["w_up"], 1)
                yield
                pe.wait_ge(s["later_consts"], 1)
                yield

            def experts(g, i):
                if i == PIECES:
                    pe.wait_ge(s["CT_dve"], nth(g, 1, 1))
                    pe.wait_ge(s["CT_act"], nth(g, 1, 1))
                    if before(g):
                        pe.wait_ge(s["ao_ready"], nth(g, T, 0))
                    for j in range(T):
                        for c in range(EP):
                            if j == 0:
                                pe.wait_ge(s["eo_ready"], nth(g, EP, c + 1))
                            for par in range(2):
                                b = 2 * j + par
                                ins = pe.matmul(mix[64 * par:64 * par + 64, 128 * j:128 * j + 128], CT[:, c, 64 * b:64 * b + 64],
                                                eo[:, c, b, :], start=(c == 0), stop=(c == EP - 1))
                    ins.then_inc(s["out_up"], 1)
                elif ORDER[i][0] == "first":
                    n = ORDER[i][1]
                    e, half = n // 2, n % 2
                    if isinstance(g, int) and g == 0 and n % 4 == 0:
                        pe.wait_ge(s[f"weights{n // 4}_in"], 32)
                    if n == 0:
                        pe.wait_ge(s["slots_dve"], nth(g, T, T))
                        pe.wait_ge(s["slots_act"], nth(g, T, T))
                    if n >= 2 or before(g):
                        pe.wait_ge(s["h_ready"], nth(g, FIRSTS, n - 1))
                    for c in range(2 * half, 2 * half + 2):
                        ins = pe.matmul(hid[half][:, TOK * (c % 2):TOK * (c % 2) + TOK], w1[:, e, 128 * c:128 * c + 128],
                                        slotsT[:, e, :, :], start=True, stop=True)
                    ins.then_inc(s["h_up"], 1)
                else:
                    _, p, b = ORDER[i]
                    if b == 0:
                        pe.wait_ge(s["h_ready"], nth(g, FIRSTS, 4 * p + 4))
                        if p >= 1 or before(g):
                            pe.wait_ge(s["eo_ready"], nth(g, EP, p))
                    for c in range(HC):
                        for k in range(2):
                            ins = pe.matmul(pair[64 * k:64 * k + 64, 128 * b:128 * b + 128], hT[:, p % 2, k, c, 64 * b:64 * b + 64],
                                            w2[:, 2 * p + k, c, :], start=(c == 0), stop=(c == HC - 1))
                    if b == GB - 1:
                        ins.then_inc(s["eo_up"], 1)

            def route(g):
                yield
                pe.wait_ge(s["kv_ready"], nth(g, 1, 1))
                if before(g):
                    pe.wait_ge(s["CT_dve"], nth(g, 1, 0))
                    pe.wait_ge(s["CT_act"], nth(g, 1, 0))
                pe.matmul(ra[0][:, 0:TOK], decayT[:, :], kv[:, :, :], start=True, stop=True).then_inc(s["r_up"], 1)
                pe.wait_ge(s["ctx_in_ready"], nth(g, 16, 16))
                transposes(ra[1], ctx_in, "ctxT_up")
                yield
                yield
                pe.wait_ge(s["xn_ready"], nth(g, 1, 1))
                transposes(ra[0], xn, "xnT_up")
                yield
                pe.wait_ge(s["xnT_ready"], nth(g, 1, 1))
                pe.wait_ge(s["ctxT_ready"], nth(g, 1, 1))
                for j in range(T):
                    pe.matmul(ra[j][:, :], xnT[:, 128 * j:128 * j + 128], snT[:, :], start=True, stop=True).then_inc(s["L_up"], 1)
                yield
                if not isinstance(g, int) or g >= 2:
                    pe.wait_ge(s["Dm1_ready"], nth(g - 2, 1, 1))
                for c in range(EP):
                    ins = pe.matmul(at[c // 2][:, TOK * (c % 2):TOK * (c % 2) + TOK], snT[:, 128 * c:128 * c + 128], xnT[:, :],
                                    start=True, stop=True)
                    if c % 2:
                        ins.then_inc(s["LT_up"], 1)
                yield
                yield
                yield
                yield
                pe.wait_ge(s["DT_ready"], nth(g, 1, 1))
                for j in range(T):
                    pe.wait_ge(s["C_ready"], nth(g, T, j + 1))
                    for c in range(EP):
                        ins = pe.transpose(ra[j][:, 128 * c:128 * c + 128], DT[:, c, 128 * j:128 * j + 128], ident[:, :])
                    ins.then_inc(s["D_up"], 1)
                yield
                for j in range(T):
                    if j == 0:
                        pe.wait_ge(s["D_dve"], nth(g, 1, 1))
                        pe.wait_ge(s["D_act"], nth(g, 1, 1))
                    elif before(g):
                        pe.wait_ge(s["h_ready"], nth(g, FIRSTS, 0))
                    for par in range(2):
                        p = slice(64 * par, 64 * par + 64)
                        pe.matmul(slot_banks[j][par][:, :], xn[p, j, :], Dw[p, j, :], start=True, stop=True).then_inc(s["slots_up"], 1)
                    yield

            def turn(g):
                pe.wait_ge(s["slots_dve"], nth(g, T, T))
                pe.wait_ge(s["slots_act"], nth(g, T, T))
                pe.wait_ge(s["C_ready"], nth(g, T, T))
                for j in range(T):
                    for c in range(EP):
                        ins = pe.transpose(ra[j][:, 128 * c:128 * c + 128], C[:, j, 128 * c:128 * c + 128], ident[:, :])
                    ins.then_inc(s["CT_up"], 1)
                yield

            def attend(g):
                pe.wait_ge(s["kept_ready"], nth(g, 1, 1))
                if before(g):
                    pe.wait_ge(s["x3_ready"], nth(g, 1, 0))
                else:
                    pe.wait_ge(s["LD_ready"], nth(g + 1, T, T))
                for b in range(GB):
                    for half in range(2):
                        ins = pe.matmul(at[b // 2][64 * half:64 * half + 64, 144 * (b % 2):144 * (b % 2) + 144],
                                        ctxT_kept[:, 64 * b:64 * b + 64], wv_half[:, half, :, :], start=True, stop=True)
                    if b % 2:
                        ins.then_inc(s["V_up"], 1)
                pe.wait_ge(s["x2_ready"], nth(g, 1, 1))
                pe.matmul(mix[:, 0:TOK], wkT[:, :], ctxT_kept[:, :], start=True, stop=True).then_inc(s["K_up"], 1)
                yield
                pe.wait_ge(s["y2_ready"], nth(g, 1, 1))
                pe.wait_ge(s["KT_ready"], nth(g, 1, 1))
                transposes(mix, y2, "y2T_up")
                yield
                pe.wait_ge(s["y2T_ready"], nth(g, 1, 1))
                if before(g):
                    pe.wait_ge(s["res_ready"], nth(g - 1, 1, 1))
                pe.matmul(mix[:, TOK:2 * TOK], wqT[:, :], y2T[:, :], start=True, stop=True).then_inc(s["Q_up"], 1)
                yield
                for j in range(T):
                    plain_wait()
                    if j == 0:
                        pe.wait_ge(s["QT_ready"], nth(g, 1, 1))
                        pe.wait_ge(s["KM_ready"], nth(g, 1, 1))
                        if before(g):
                            pe.wait_ge(s["u_ready"], nth(g, T, 0))
                    else:
                        pe.wait_ge(s["Dm0_ready"], nth(g, 1, 1))
                    for half in range(2):
                        r = slice(64 * half, 64 * half + 64)
                        for par in range(2):
                            b = 2 * j + par
                            ins = pe.matmul(at[half][64 * par:64 * par + 64, :], QT[r, 64 * b:64 * b + 64], KM[r, b, :, :],
                                            start=True, stop=True)
                    ins.then_inc(s["S_up"], 1)
                    yield
                yield
                yield
                pe.wait_ge(s["mean_ready"], nth(g, 1, 1))
                pe.wait_ge(s["stats_ready"], nth(g, 1, 1))
                for par in range(2):
                    for f, rows in enumerate((mean_rows[:, par, :, :], mx[:, :, :], var[:, :, :])):
                        ins = pe.matmul(mix[0:MH, TH * par:TH * par + TH], m1_row[:, 0, :] if f == 0 else m1_half[:, par, f, :],
                                        rows, start=(f == 0), stop=(f == 2))
                ins.then_inc(s["hid1_up"], 1)
                yield
                plain_wait()
                pe.wait_ge(s["hid1_ready"], nth(g, 1, 1))
                pe.matmul(mix[0:MH, 128:128 + 2 * TH], m2T[:, :], h1[:, :], start=True, stop=True).then_inc(s["hid2_up"], 1)
                yield
                plain_wait()
                pe.wait_ge(s["hid2_ready"], nth(g, 1, 1))
                for par in range(2):
                    ins = pe.matmul(mix[64 * par:64 * par + 64, 192:192 + TH], m3_wide[:, :], h2[:, TH * par:TH * par + TH],
                                    start=True, stop=True)
                ins.then_inc(s["t_up"], 1)
                yield
                yield
                yield
                yield
                yield

                def turned(j):
                    pe.wait_ge(s["P_ready"], nth(g, T, j + 1))
                    for c in range(HP):
                        ins = pe.transpose(at2[:, 128 * c:128 * c + 128], P[:, j, 2 * c:2 * c + 2, :], ident[:, :])
                    ins.then_inc(s["PT_up"], 1)

                def values(j):
                    for c in range(HP):
                        for par in range(2):
                            ins = pe.matmul(mix[64 * par:64 * par + 64, 144 * j + VW * c:144 * j + VW * c + VW],
                                            PT[:, j, c, 64 * par:64 * par + 64], V[:, 2 * j + par, c, :], start=True, stop=True)
                    ins.then_inc(s["av_up"], 1)

                pe.wait_ge(s["Dm1_ready"], nth(g, 1, 1))
                if not isinstance(g, int) or g + 2 < GROUPS:
                    pe.wait_ge(s["LD_ready"], nth(g + 2, T, T))
                turned(0)
                yield
                pe.wait_ge(s["PT_dve"], nth(g, T, 1))
                pe.wait_ge(s["PT_act"], nth(g, T, 1))
                turned(1)
                pe.wait_ge(s["zt_ready"], nth(g, 1, 1))
                pe.wait_ge(s["res_ready"], nth(g, 1, 1))
                values(0)
                yield
                pe.wait_ge(s["PT_dve"], nth(g, T, 2))
                pe.wait_ge(s["PT_act"], nth(g, T, 2))
                pe.wait_ge(s["ao_ready"], nth(g, T, 1))
                values(1)
                yield
                pe.wait_ge(s["ao_ready"], nth(g, T, T))
                transposes(at[0], ao, "aoT_up")
                yield
                pe.wait_ge(s["aoT_ready"], nth(g, 1, 1))
                for j in range(T):
                    ins = pe.matmul(at[1][:, 128 * j:128 * j + 128], aoT[:, 128 * j:128 * j + 128], woT[:, :], start=True, stop=True)
                ins.then_inc(s["o_up"], 1)
                yield

            def feed(g):
                yield
                pe.wait_ge(s["h3_ready"], nth(g, 1, 1))
                if not isinstance(g, int) or g + 1 < GROUPS:
                    pe.wait_ge(s["V_ready"], nth(g + 1, T, T))
                transposes(at[0], h3, "h3T_up")
                yield
                pe.wait_ge(s["h3T_ready"], nth(g, 1, 1))
                for c in range(HC):
                    ins = pe.matmul(at[c // 2][:, TOK * (c % 2):TOK * (c % 2) + TOK], fc1[:, 128 * c:128 * c + 128], h3T[:, :],
                                    start=True, stop=True)
                    if c % 2:
                        ins.then_inc(s["u_up"], 1)
                yield
                pe.wait_ge(s["u_ready"], nth(g, T, T))
                if not isinstance(g, int) or g + 1 < GROUPS:
                    pe.wait_ge(s["QT_ready"], nth(g + 1, 1, 1))
                for j in range(T):
                    for c in range(HC):
                        ins = pe.matmul(mix[:, TOK + 128 * j:TOK + 128 * j + 128], uT[:, c, 128 * j:128 * j + 128], fc2[:, c, :],
                                        start=(c == 0), stop=(c == HC - 1))
                ins.then_inc(s["z_up"], 1)
                yield

            all_iterations(pe, experts, {"attend": attend, "feed": feed, "turn": turn, "route": route,
                                 "first_consts": first_consts, "later_consts": later_consts}, steps_first=True)

        @block.scalar
        def _(act):
            act.sem_inc(s["out_done"], 16)
            act.sem_inc(s["res_ready"], 1)

            def first_consts():
                yield
                yield
                act.wait_ge(s["dve_consts"], 3)
                yield

            def later_consts():
                yield
                act.wait_ge(s["later_consts"], 1)
                yield

            def experts(g, i):
                if i < PIECES and ORDER[i][0] == "first":
                    n = ORDER[i][1]
                    e, half = n // 2, n % 2
                    act.wait_ge(s["h_up"], nth(g, FIRSTS, n + 1))
                    for c in range(2 * half, 2 * half + 2):
                        ins = act.activation(hT[:, e // 2 % 2, e % 2, c, :], hid[half][:, TOK * (c % 2):TOK * (c % 2) + TOK], ACT.Gelu,
                                             bias=vecs[:, C_B1 + HC * e + c:C_B1 + HC * e + c + 1])
                    ins.then_inc(s["h_ready"], 1)

            def route(g):
                act.wait_ge(s["ctx_in_ready"], nth(g, 16, 16))
                act.activation(kv[:, :, :], ctx_in[:, :, :], ACT.Square).then_inc(s["kv_ready"], 1)
                yield
                act.wait_ge(s["ctxT_up"], nth(g, 1, 1))
                if before(g):
                    act.wait_ge(s["kept_ready"], nth(g, 1, 0))
                act.activation(ctxT[:, :], ra[1][:, 0:TOK], ACT.Copy).then_inc(s["ctxT_ready"], 1)
                yield
                yield
                act.wait_ge(s["xnT_up"], nth(g, 1, 1))
                act.activation(xnT[:, :], ra[0][:, 0:TOK], ACT.Copy).then_inc(s["xnT_ready"], 1)
                yield
                yield
                yield
                if before(g):
                    act.wait_ge(s["CT_up"], nth(g, T, 0))
                    act.wait_ge(s["rC_ready"], nth(g, 1, 0))
                for j in range(T):
                    act.wait_ge(s["nmC_ready"], nth(g, T, j + 1))
                    act.activation(C[:, j, :], ra[j][:, :], ACT.Exp, bias=nmC[:, j:j + 1], accum_out=sumC[:, j:j + 1]).then_inc(s["C_ready"], 1)
                yield
                for q in range(2):
                    act.wait_ge(s["LD_ready"], nth(g, 2, q + 1))
                    act.activation(DT[:, 2 * q:2 * q + 2, :], DT[:, 2 * q:2 * q + 2, :], ACT.Exp).then_inc(s["expD_ready"], 1)
                yield
                yield
                act.wait_ge(s["D_up"], nth(g, T, 2))
                act.activation(Dw[:, 1, :], ra[1][:, :], ACT.Copy).then_inc(s["D_act"], 1)
                yield
                for j in range(T):
                    if j == 0 and before(g):
                        act.wait_ge(s["h_up"], nth(g, FIRSTS, 0))
                    act.wait_ge(s["slots_up"], nth(g, 2 * T, 2 * j + 2))
                    act.activation(slotsT[:, :, 2 * j + 1, :], slot_banks[j][1][:, :].rearrange("p (e k) -> p e k", e=E),
                                   ACT.Copy, scale=vecs[:, C_G1:C_G1 + 1]).then_inc(s["slots_act"], 1)
                    yield

            def turn(g):
                act.wait_ge(s["CT_up"], nth(g, T, 2))
                if before(g):
                    act.wait_ge(s["out_up"], nth(g, 1, 0))
                act.activation(CT[:, :, 128:256], ra[1][:, :].rearrange("p (c t) -> p c t", c=EP), ACT.Copy).then_inc(s["CT_act"], 1)
                yield

            def attend(g):
                act.wait_ge(s["K_up"], nth(g, 1, 1))
                if before(g):
                    act.wait_ge(s["mean_ready"], nth(g, 1, 0))
                act.activation(KT[:, :], mix[:, 0:TOK], ACT.Identity, bias=vecs[:, C_BK:C_BK + 1]).then_inc(s["KT_ready"], 1)
                yield
                act.wait_ge(s["y2T_up"], nth(g, 1, 1))
                act.activation(y2T[:, :], mix[:, 0:TOK], ACT.Copy).then_inc(s["y2T_ready"], 1)
                yield
                act.wait_ge(s["Q_up"], nth(g, 1, 1))
                act.activation(QT[:, :], mix[:, TOK:2 * TOK], ACT.Identity, bias=vecs[:, C_BQ:C_BQ + 1]).then_inc(s["QT_ready"], 1)
                yield
                yield
                yield
                for j in range(T):
                    if j == 0 and before(g):
                        act.wait_ge(s["stats_ready"], nth(g, 1, 0))
                    act.wait_ge(s[f"Dm{j}_ready"], nth(g, 1, 1))
                    act.activation(e1[:, j, :, :], Dm[:, j, :, :], ACT.Exp, scale=DK ** -0.5).then_inc(s["e1_ready"], 1)
                    act.activation(e2[:, j, :, :], Dm[:, j, :, :], ACT.Exp, scale=2 * DK ** -0.5).then_inc(s["e2_ready"], 1)
                    yield
                act.wait_ge(s["hid1_up"], nth(g, 1, 1))
                act.activation(h1[:, :], mix[0:MH, 0:2 * TH], ACT.Gelu, bias=m_small[:, 0:1]).then_inc(s["hid1_ready"], 1)
                yield
                act.wait_ge(s["hid2_up"], nth(g, 1, 1))
                act.activation(h2[:, :], mix[0:MH, 128:128 + 2 * TH], ACT.Gelu, bias=m_small[:, 1:2]).then_inc(s["hid2_ready"], 1)
                yield
                yield
                act.wait_ge(s["zt_ready"], nth(g, 1, 1))
                act.activation(inv_t[:, :, :], zt[:, :, :], ACT.Exp, scale=-1.0).then_inc(s["inv_t_ready"], 1)
                yield
                yield
                for j in range(T):
                    act.wait_ge(s["Dt_ready"], nth(g, T, j + 1))
                    act.activation(P[:, j, :, :], Dm[:, j, :, :], ACT.Exp, scale=0.5).then_inc(s["P_ready"], 1)
                    yield
                for j in range(T):
                    act.wait_ge(s["PT_up"], nth(g, T, j + 1))
                    act.activation(PT[:, j, 4:8, :], at[1], ACT.Relu).then_inc(s["PT_act"], 1)
                    yield
                yield
                act.wait_ge(s["aoT_up"], nth(g, 1, 1))
                act.activation(aoT[:, :], at[0][:, 0:TOK], ACT.Copy).then_inc(s["aoT_ready"], 1)
                yield
                yield

            def feed(g):
                yield
                yield
                for c in range(HC):
                    act.wait_ge(s["u_up"], nth(g, 2, c // 2 + 1))
                    ins = act.activation(uT[:, c, :], at[c // 2][:, TOK * (c % 2):TOK * (c % 2) + TOK], ACT.Silu,
                                         bias=vecs[:, C_FB + c:C_FB + c + 1])
                    if c % 2:
                        ins.then_inc(s["u_ready"], 1)
                yield
                yield

            all_iterations(act, experts, {"attend": attend, "feed": feed, "turn": turn, "route": route,
                                 "first_consts": first_consts, "later_consts": later_consts})

        @block.vector
        def _(dve):
            n = [0]

            def pre(ins):
                n[0] += 1
                ins.then_inc(s["dve_pre"], 1)
                dve.wait_ge(s["dve_pre"], n[0])

            dve.wait_ge(s["pool_consts"], 1)
            dve.tensor_tensor(head8[:, :], head16[:, 0:8], head16[:, 8:16], ALU.add)
            dve.tensor_tensor_scan(decayT[:, :], decay_step[:, :], ident[:, :], 0.0, ALU.mult, ALU.add).then_inc(s["dve_consts"], 1)

            def first_consts():
                yield
                dve.wait_ge(s["slots_in"], 16)
                pre(dve.tensor_tensor(slot_sq[:, :, :], slot_rows[:, :, :], slot_rows[:, :, :], ALU.mult))
                dve.tensor_reduce(slot_n[:, :], slot_sq[:, :, :], AX, ALU.add).then_inc(s["pre_pow"], 1)
                dve.wait_ge(s["pre_pow_out"], 1)
                pre(dve.tensor_scalar(slot_n[:, :], slot_n[:, :], 1e-12, None, ALU.max))
                pre(dve.reciprocal(slot_n[:, :], slot_n[:, :]))
                pre(dve.tensor_scalar(slot_n[:, :], slot_n[:, :], float(D) ** 0.5, None, ALU.mult))
                dve.tensor_tensor(slot_rows[:, :, :], slot_rows[:, :, :], slot_n[:, :].unsqueeze(2).to_broadcast([128, 4, D]),
                                  ALU.mult).then_inc(s["dve_consts"], 1)
                dve.wait_ge(s["vecs_up"], 1)
                pre(dve.tensor_copy(vecs[:, :], mix[:, 0:NVEC]))
                pre(dve.tensor_tensor(g12[:, :], vecs[:, C_G1:C_G1 + 1], vecs[:, C_G2:C_G2 + 1], ALU.mult))
                yield
                dve.wait_ge(s["slotT_up"], 1)
                dve.tensor_scalar(snT[:, :], at[1], g12[:, :], None, ALU.mult).then_inc(s["dve_consts"], 1)
                yield

            def later_consts():
                dve.wait_ge(s["w_up"], 2)
                wT = at[0].rearrange("p (k d) -> p k d", k=4)
                dve.tensor_copy(wqT[:, :], wT[:, 0, :])
                dve.tensor_copy(wkT[:, :], wT[:, 1, :])
                dve.tensor_copy(woT[:, :], wT[:, 3, :])
                wv = wT[:, 2, :].rearrange("p (c a k) -> p c a k", a=2, k=DK)
                for half in range(2):
                    dve.tensor_copy(wv_half[:, half, :, DK * half:DK * half + DK], wv[:, :, half, :])
                dve.tensor_copy(m2T[:, :], mix[0:MH, 0:MH])
                dve.wait_ge(s["cast_in"], 16 * CASTS)
                bv = bv_row[:, :].rearrange("p (c a k) -> p c a k", a=2, k=DK)
                for half in range(2):
                    p = slice(64 * half, 64 * half + 64)
                    dve.tensor_copy(v_bias[p, :, DK * half:DK * half + DK], bv[p, :, half, :])
                pre(dve.tensor_scalar(m1_row[:, 0, :], m1_row[:, 0, :], DK ** -0.5 / (S * S), None, ALU.mult))
                for half in range(2):
                    p = slice(64 * half, 64 * half + 64)
                    dve.tensor_scalar(m1_half[p, half, 1, :], m1_row[p, 1, :], DK ** -0.5 / S, None, ALU.mult)
                    dve.tensor_scalar(m1_half[p, half, 2, :], m1_row[p, 2, :], 1.0 / (S * (S - 1)), None, ALU.mult)
                dve.tensor_copy(m3_wide[:, :], m_small[:, 2:3].to_broadcast([MH, 64]))
                pre(dve.tensor_scalar(fb2_half[:, :], fb2_half[:, :], 0.5, None, ALU.mult))
                dve.tensor_scalar(fc1[:, :], fc1_q[:, :], -128.0, None, ALU.add)
                pre(dve.tensor_scalar(fc2[:, :, :], fc2_q[:, :, :], -128.0, None, ALU.add))
                dve.tensor_tensor(fc1[:, :], fc1[:, :], fc1_s[:, :], ALU.mult)
                dve.tensor_tensor(fc2[:, :, :], fc2[:, :, :], fc2_s[:, :, :], ALU.mult).then_inc(s["later_consts"], 1)
                dve.wait_ge(s["later_consts"], 1)
                yield
                yield

            def linker(name, per, g):
                k = [0]

                def link(ins):
                    k[0] += 1
                    ins.then_inc(s[name], 1)
                    dve.wait_ge(s[name], nth(g, per, k[0]))

                return link, k

            def moments(link, src, stats, mv):
                for j in range(T):
                    ins = dve.bn_stats(stats[:, j, :], src[:, j, :])
                link(ins)
                dve.memset(wait_pad[:, :], 0.0)
                for j in range(T):
                    ins = dve.bn_aggr(mv[:, j, :], stats[:, j, :])
                link(ins)

            def centred(dst, src, mv, scale):
                for j in range(T):
                    ins = dve.tensor_scalar(dst[:, j, :], src[:, j, :], mv[:, j, 0:1], scale[:, j:j + 1], ALU.subtract, ALU.mult)
                return ins

            def experts(g, i):
                if i == PIECES:
                    dve.wait_ge(s["out_up"], nth(g, 1, 1))
                    dve.wait_ge(s["x1b_ready"], nth(g, 1, 1))
                    dve.wait_ge(s["rC_ready"], nth(g, 1, 1))
                    if before(g):
                        dve.wait_ge(s["x2b_ready"], nth(g, 1, 0))
                    for j in range(T):
                        ins = dve.scalar_tensor_tensor(x2[:, j, :], mix[:, 128 * j:128 * j + 128], rC[:, j:j + 1], x1b[:, j, :], ALU.mult, ALU.add)
                    ins.then_inc(s["x2_ready"], 1)
                elif ORDER[i][0] == "second" and ORDER[i][2] == GB - 1:
                    p = ORDER[i][1]
                    dve.wait_ge(s["eo_up"], nth(g, EP, p + 1))
                    dve.tensor_tensor(eo[:, p, :, :], pair[:, :].rearrange("p (b d) -> p b d", b=GB),
                                      b2_pair[:, p, :].unsqueeze(1).to_broadcast([128, GB, D]), ALU.add).then_inc(s["eo_ready"], 1)

            def route(g):
                link, k = linker("route_step", ROUTE_STEPS, g)
                dve.wait_ge(s["x_in_ready"], nth(g, 16, 16))
                moments(link, x_in, r_stats, r_mv)
                dve.tensor_scalar(r_pow_in[:, 0:T], r_mv[:, :, 1], EPS, None, ALU.add).then_inc(s["r_pow_asked"], 1)
                yield
                dve.wait_ge(s["r_pow_ready"], nth(g, 2, 1))
                link(centred(y1, x_in, r_mv, r_pow))
                dve.wait_ge(s["r_up"], nth(g, 1, 1))
                link(dve.tensor_tensor(y1[:, :, :], y1[:, :, :], ra[0][:, 0:TOK].rearrange("p (j d) -> p j d", j=T), ALU.mult))
                if before(g):
                    dve.wait_ge(s["x1b_ready"], nth(g, 1, 0))
                dve.tensor_tensor(x1[:, :, :], x_in[:, :, :], y1[:, :, :], ALU.add).then_inc(s["x1_ready"], 1)
                dve.wait_ge(s["x1_ready"], nth(g, 1, 1))
                moments(link, x1, r_stats, r_mv)
                dve.tensor_scalar(r_pow_in[:, 0:T], r_mv[:, :, 1], EPS, None, ALU.add)
                dve.tensor_scalar(r_pow_in[:, T:2 * T], r_mv[:, :, 1], float(D), None, ALU.mult).then_inc(s["r_pow_asked"], 1)
                yield
                dve.wait_ge(s["r_pow_ready"], nth(g, 2, 2))
                link(dve.tensor_tensor(r_small[:, 0, :], r_pow[:, 0:T], r_pow[:, T:2 * T], ALU.mult))
                link(dve.tensor_scalar(r_small[:, 1, :], r_small[:, 0, :], 1e-12, None, ALU.max))
                link(dve.reciprocal(r_small[:, 2, :], r_small[:, 1, :]))
                link(dve.scalar_tensor_tensor(r_small[:, 3, :], r_small[:, 2, :], float(D) ** 0.5, r_pow[:, 0:T], ALU.mult, ALU.mult))
                centred(xn, x1, r_mv, r_small[:, 3]).then_inc(s["xn_ready"], 1)
                yield
                yield
                for j in range(T):
                    dve.wait_ge(s["L_up"], nth(g, T, j + 1))
                    dve.tensor_reduce(nmC[:, j:j + 1], ra[j][:, :], AX, ALU.max, negate=True).then_inc(s["nmC_ready"], 1)
                yield
                if before(g):
                    dve.wait_ge(s["D_up"], nth(g, T, 0))
                for q in range(2):
                    c = slice(2 * q, 2 * q + 2)
                    LT = at[q].rearrange("p (c b n) -> p c b n", c=2, b=GB)
                    dve.wait_ge(s["LT_up"], nth(g, 2, q + 1))
                    link(dve.tensor_reduce(nmD[:, c, :], LT, AX, ALU.max, negate=True))
                    dve.tensor_tensor(DT[:, c, :].rearrange("p c (b n) -> p c b n", b=GB), LT,
                                      nmD[:, c, :].unsqueeze(3).to_broadcast([128, 2, GB, S]), ALU.add).then_inc(s["LD_ready"], 1)
                yield
                yield
                yield
                DT4 = DT[:, :, :].rearrange("p c (b n) -> p c b n", b=GB)
                for q in range(2):
                    dve.wait_ge(s["expD_ready"], nth(g, 2, q + 1))
                    ins = dve.tensor_reduce(sumD[:, 2 * q:2 * q + 2, :], DT4[:, 2 * q:2 * q + 2], AX, ALU.add)
                link(ins)
                link(dve.reciprocal(sumD[:, :, :], sumD[:, :, :]))
                dve.tensor_tensor(DT4, DT4, sumD[:, :, :].unsqueeze(3).to_broadcast([128, EP, GB, S]), ALU.mult).then_inc(s["DT_ready"], 1)
                yield
                dve.wait_ge(s["D_up"], nth(g, T, 1))
                dve.tensor_copy(Dw[:, 0, :], ra[0][:, :]).then_inc(s["D_dve"], 1)
                yield
                for j in range(T):
                    if j == 0 and before(g):
                        dve.wait_ge(s["h_up"], nth(g, FIRSTS, 0))
                    dve.wait_ge(s["slots_up"], nth(g, 2 * T, 2 * j + 1))
                    dve.tensor_scalar(slotsT[:, :, 2 * j, :], slot_banks[j][0][:, :].rearrange("p (e k) -> p e k", e=E),
                                      vecs[:, C_G1:C_G1 + 1], None, ALU.mult).then_inc(s["slots_dve"], 1)
                    if j == T - 1:
                        dve.wait_ge(s["slots_up"], nth(g, 2 * T, 2 * T))
                        assert k[0] == ROUTE_STEPS, k[0]
                    yield

            def turn(g):
                dve.wait_ge(s["C_ready"], nth(g, T, T))
                dve.reciprocal(rC[:, :], sumC[:, :]).then_inc(s["rC_ready"], 1)
                dve.wait_ge(s["CT_up"], nth(g, T, 1))
                dve.tensor_copy(CT[:, :, 0:128], ra[0][:, :].rearrange("p (c t) -> p c t", c=EP)).then_inc(s["CT_dve"], 1)
                yield

            def attend(g):
                link, k = linker("attend_step", ATTEND_STEPS, g)
                dve.wait_ge(s["x2_ready"], nth(g, 1, 1))
                moments(link, x2, a_stats, a_mv)
                dve.tensor_scalar(a_pow_in[:, :], a_mv[:, :, 1], EPS, None, ALU.add).then_inc(s["a_pow_asked"], 1)
                for q in range(2):
                    dve.wait_ge(s["V_up"], nth(g, 2, q + 1))
                    dve.tensor_tensor(V[:, 2 * q:2 * q + 2, :, :].rearrange("p b c w -> p b (c w)"), at[q][:, 0:288].rearrange("p (b w) -> p b w", b=2),
                                      v_bias[:, :, :].rearrange("p c w -> p (c w)").unsqueeze(1).to_broadcast([128, 2, VW * HP]), ALU.add).then_inc(s["V_ready"], 1)
                dve.wait_ge(s["a_pow_ready"], nth(g, 1, 1))
                centred(y2, x2, a_mv, a_pow).then_inc(s["y2_ready"], 1)
                yield
                dve.wait_ge(s["KT_ready"], nth(g, 1, 1))
                for h in range(HP):
                    ins = dve.tensor_scalar(KM[:, :, h, :], KT[:, :].rearrange("p (b n) -> p b n", b=GB), head8[:, h:h + 1], None, ALU.mult)
                ins.then_inc(s["KM_ready"], 1)
                dve.tensor_reduce(sumK[:, :], KT[:, :].rearrange("p (b n) -> p b n", b=GB), AX, ALU.add)
                yield
                dve.wait_ge(s["QT_ready"], nth(g, 1, 1))
                link(dve.tensor_reduce(sumQ[:, :], QT[:, :].rearrange("p (b n) -> p b n", b=GB), AX, ALU.add))
                link(dve.tensor_tensor(qk_sum[:, :], sumQ[:, :], sumK[:, :], ALU.mult))
                for par in range(2):
                    ins = dve.tensor_tensor(mean_rows[:, par, :, :], head16[:, :].unsqueeze(1).to_broadcast([128, T, H]),
                                            qk_sum[:, par:GB:2].unsqueeze(2).to_broadcast([128, T, H]), ALU.mult)
                ins.then_inc(s["mean_ready"], 1)
                yield
                sc = at2[:, :].rearrange("p (h k) -> p h k", h=H)
                for j in range(T):
                    if j == 0 and before(g):
                        dve.wait_ge(s["P_ready"], nth(g, T, 0))
                    dve.wait_ge(s["S_up"], nth(g, T, j + 1))
                    link(dve.tensor_reduce(mx[:, j, :], sc, AX, ALU.max))
                    dve.tensor_tensor(Dm[:, j, :, :], sc, mx[:, j, :].unsqueeze(2).to_broadcast([128, H, S]), ALU.subtract).then_inc(s[f"Dm{j}_ready"], 1)
                    yield
                for j in range(T):
                    dve.wait_ge(s["e1_ready"], nth(g, T, j + 1))
                    dve.tensor_reduce(s1[:, j, :], e1[:, j, :, :], AX, ALU.add)
                    dve.wait_ge(s["e2_ready"], nth(g, T, j + 1))
                    ins = dve.tensor_reduce(s2[:, j, :], e2[:, j, :, :], AX, ALU.add)
                    if j == T - 1:
                        link(ins)
                        link(dve.reciprocal(var[:, :, :], s1[:, :, :]))
                        link(dve.tensor_tensor(var[:, :, :], var[:, :, :], var[:, :, :], ALU.mult))
                        link(dve.tensor_tensor(var[:, :, :], var[:, :, :], s2[:, :, :], ALU.mult))
                        dve.tensor_scalar(var[:, :, :], var[:, :, :], -1.0 / S, None, ALU.add).then_inc(s["stats_ready"], 1)
                    yield
                yield
                yield
                dve.wait_ge(s["t_up"], nth(g, 1, 1))
                link(dve.tensor_scalar(zt[:, :, :], mix[:, 192:192 + TH].rearrange("p (j h) -> p j h", j=T), b3_all[:, :], -LOG_T, ALU.add, ALU.max))
                dve.tensor_scalar(zt[:, :, :], zt[:, :, :], LOG_T, None, ALU.min).then_inc(s["zt_ready"], 1)
                yield
                yield
                dve.wait_ge(s["inv_t_ready"], nth(g, 1, 1))
                for j in range(T):
                    dve.tensor_tensor(Dm[:, j, :, :], Dm[:, j, :, :], inv_t[:, j, :].unsqueeze(2).to_broadcast([128, H, S]), ALU.mult).then_inc(s["Dt_ready"], 1)
                yield
                yield
                yield

                def turned(j):
                    dve.wait_ge(s["PT_up"], nth(g, T, j + 1))
                    dve.tensor_scalar(PT[:, j, 0:4, :], at[0].rearrange("p (c q) -> p c q", c=4), 0.0, None, ALU.max).then_inc(s["PT_dve"], 1)

                def normalise(j):
                    dve.wait_ge(s["av_up"], nth(g, T, j + 1))
                    av = mix[:, 144 * j:144 * j + 144].rearrange("p (c w) -> p c w", c=HP)
                    dj = den[:, j, :].rearrange("p (c a) -> p c a", a=2)
                    link(dve.tensor_scalar(dj, av[:, :, 2 * DK:VW], 1e-30, None, ALU.max))
                    link(dve.reciprocal(den[:, j, :], den[:, j, :]))
                    dve.tensor_tensor(ao[:, j, :].rearrange("p (c a k) -> p c a k", a=2, k=DK), av[:, :, 0:2 * DK].rearrange("p c (a k) -> p c a k", a=2),
                                      dj.unsqueeze(3).to_broadcast([128, HP, 2, DK]), ALU.mult).then_inc(s["ao_ready"], 1)

                turned(0)
                yield
                turned(1)
                normalise(0)
                yield
                normalise(1)
                yield
                yield
                dve.wait_ge(s["o_up"], nth(g, 1, 1))
                dve.wait_ge(s["x2b_ready"], nth(g, 1, 1))
                if before(g):
                    dve.wait_ge(s["acc_ready"], nth(g, 1, 0))
                dve.tensor_tensor(x3[:, :, :], x2b[:, :, :], at[1][:, 0:TOK].rearrange("p (j d) -> p j d", j=T), ALU.add).then_inc(s["x3_ready"], 1)
                dve.wait_ge(s["x3_ready"], nth(g, 1, 1))
                moments(link, x3, f_stats, f_mv)
                dve.tensor_scalar(f_pow_in[:, :], f_mv[:, :, 1], EPS, None, ALU.add).then_inc(s["f_pow_asked"], 1)
                assert k[0] == ATTEND_STEPS, k[0]
                yield

            def feed(g):
                link, k = linker("feed_step", FEED_STEPS, g)
                dve.wait_ge(s["f_pow_ready"], nth(g, 2, 1))
                link(dve.tensor_copy(f_small[:, 0, :], f_pow[:, :]))
                link(dve.tensor_tensor(f_small[:, 1, :], f_small[:, 0, :], f_small[:, 0, :], ALU.mult))
                link(dve.tensor_tensor(f_small[:, 2, :], f_small[:, 1, :], f_mv[:, :, 1], ALU.mult))
                dve.tensor_scalar(f_pow_in[:, :], f_small[:, 2, :], EPS, None, ALU.add).then_inc(s["f_pow_asked"], 1)
                link(centred(y3, x3, f_mv, f_small[:, 0]))
                dve.wait_ge(s["f_pow_ready"], nth(g, 2, 2))
                link(dve.tensor_tensor(f_small[:, 3, :], f_small[:, 0, :], f_pow[:, :], ALU.mult))
                ins = centred(h3, x3, f_mv, f_small[:, 3])
                ins.then_inc(s["h3_ready"], 1)
                dve.memset(wait_pad[:, :], 0.0).then_inc(s["y3_ready"], 1)
                yield
                dve.wait_ge(s["h3T_up"], nth(g, 1, 1))
                dve.tensor_scalar(h3T[:, :], at[0][:, 0:TOK], vecs[:, C_LG:C_LG + 1], vecs[:, C_LB:C_LB + 1], ALU.mult, ALU.add).then_inc(s["h3T_ready"], 1)
                yield
                yield
                dve.wait_ge(s["z_up"], nth(g, 1, 1))
                dve.wait_ge(s["acc_ready"], nth(g, 1, 1))
                dve.wait_ge(s["out_done"], nth(g, 16, 16))
                dve.scalar_tensor_tensor(res[:, :, :].rearrange("p j d -> p (j d)"), mix[:, TOK:2 * TOK], 0.5,
                                         acc[:, :, :].rearrange("p j d -> p (j d)"), ALU.mult, ALU.add).then_inc(s["res_ready"], 1)
                assert k[0] == FEED_STEPS, k[0]
                yield

            all_iterations(dve, experts, {"attend": attend, "feed": feed, "turn": turn, "route": route,
                                 "first_consts": first_consts, "later_consts": later_consts}, steps_first=True)


_INS = ['x', 'ctx_1024', 'L0_ffn_norm_gamma', 'L0_ffn_slot_norm_gamma', 'L0_ffn_slot_embeds', 'L0_ffn_w1', 'L0_ffn_b1',
        'L0_ffn_w2', 'L0_ffn_b2', 'L1_xattn_Wq', 'L1_xattn_bq', 'L1_xattn_Wk', 'L1_xattn_bk', 'L1_xattn_Wv', 'L1_xattn_bv',
        'L1_xattn_Wo', 'L1_xattn_bo', 'L1_xattn_w1', 'L1_xattn_b1', 'L1_xattn_w2', 'L1_xattn_b2', 'L1_xattn_w3',
        'L1_xattn_b3', 'L1_ffn_ln_gamma', 'L1_ffn_ln_beta', 'L1_ffn_fc1_q', 'L1_ffn_fc1_scales', 'L1_ffn_fc1_bias',
        'L1_ffn_fc2_q', 'L1_ffn_fc2_scales', 'L1_ffn_fc2_bias']


def kernel(**inputs):
    import numpy as _np
    import concourse.bacc as _bacc
    from concourse import mybir as _mybir
    from concourse.bass_utils import run_bass_kernel_spmd as _run

    nc = _bacc.Bacc("TRN2", target_bir_lowering=False, num_devices=1)
    arrays, args = {}, {}
    for name in _INS:
        v = _np.ascontiguousarray(inputs[name])
        arrays[f"in_{name}"] = v
        args[name] = nc.dram_tensor(f"in_{name}", v.shape, _mybir.dt.from_np(v.dtype), kind="ExternalInput").ap()
    out = nc.dram_tensor("out_0", (32, 64, 128), _mybir.dt.float32, kind="ExternalOutput").ap()
    build(nc, args, out)
    r = _run(nc, [arrays], core_ids=[0])
    return r.results[0]["out_0"]
```

```python
from contextlib import ExitStack

import numpy as np

import concourse.bass as bass
from concourse import mybir

fp32 = mybir.dt.float32
fp22 = mybir.dt.float32r
ALU = mybir.AluOpType
ACT = mybir.ActivationFunctionType
AX = mybir.AxisListType.X

B, S, D = 32, 64, 128
E, SL = 8, 64
ES = E * SL
EP = E // 2
HID = 4 * D
HC = HID // 128
H, DK = 16, 8
HP = H // 2
MH = 64
T = 2
GB = 2 * T
GROUPS = B // GB
TOK = 128 * T
TH = T * H
VW = 2 * DK + 2
DECAY = 0.9
EPS = 1e-5
LOG_T = 2.302585092994046

C_B1, C_G1, C_G2, C_BQ, C_BK, C_FB, C_LG, C_LB, C_B2 = 0, 32, 33, 34, 35, 36, 40, 41, 42
NVEC = 50

FIRSTS = 2 * E
ORDER = []
for _p in range(EP):
    ORDER += [("first", n) for n in range(4 * _p + (_p > 0), 4 * _p + 4)]
    if _p > 0:
        ORDER.insert(len(ORDER) - 1, ("turned", _p - 1))
    if _p < EP - 1:
        ORDER.append(("first", 4 * _p + 4))
    ORDER += [("second", _p, q) for q in range(HC)]
ORDER.append(("turned", EP - 1))
PIECES = len(ORDER)
STEPS_AT = {
    "route": (3, 8, 13, 16, 18, 18, 25, 26, 26, 29, 31, 33),
    "turn": (4,),
    "attend": (1, 3, 5, 9, 14, 16, 17, 20, 23, 23, 25, 26, 26, 26, 26, 27, 31, 35, 36),
    "feed": (1, 4, 5, 8),
    "last_feed": (3, 14, 17, 30),
    "first_consts": (3, 4, 10),
    "later_consts": (9, 18),
    "split_first": (22, 28),
    "split_later": (8, 8),
}


def nth(g, per, n):
    return g * per + n


def before(g):
    return not isinstance(g, int) or g > 0


def iteration(it, experts, stages, steps_first):
    running = []
    for name, shift in (("attend", -1), ("feed", -2), ("turn", 0), ("route", 1)):
        g = it + shift
        if not isinstance(g, int) or 0 <= g < GROUPS:
            at = "last_feed" if name == "feed" and isinstance(it, int) and it == GROUPS else name
            running.append((stages[name](g), STEPS_AT[at]))
    for name, when in (("first_consts", -1), ("split_first", -1), ("later_consts", 0), ("split_later", 0)):
        if isinstance(it, int) and it == when:
            running.append((stages[name](), STEPS_AT[name]))
    pieces = not isinstance(it, int) or 0 <= it < GROUPS
    for i in range(PIECES + 1):
        if pieces and not steps_first:
            experts(it, i)
        for stage, at in running:
            for _ in range(at.count(i)):
                next(stage)
        if pieces and steps_first:
            experts(it, i)


def all_iterations(eng, experts, stages, steps_first=False):
    for it in (-1, 0, 1):
        iteration(it, experts, stages, steps_first)
    with eng.Fori(2, GROUPS - 2) as it:
        iteration(it, experts, stages, steps_first)
    for it in range(GROUPS - 2, GROUPS + 2):
        iteration(it, experts, stages, steps_first)


def build(nc, a, out):
    with ExitStack() as ctx:
        def sb(name, *shape, dtype=fp32):
            return ctx.enter_context(nc.sbuf_tensor(name, [128, *shape], dtype))

        def split(name, *shape):
            return sb(name + "_hi", *shape, dtype=fp22), sb(name + "_lo", *shape, dtype=fp22)

        def places(name, n, *earlier):
            space, at, views = sb(name, n), 0, []
            for shape, dtype in earlier:
                size = int(np.prod(shape))
                v = space[:, at:at + size]
                v = v if dtype == fp32 else v.bitcast(dtype)
                views.append(v if len(shape) == 1 else v.rearrange("p (a b) -> p a b", a=shape[0]))
                at += size
            return space, *views

        exps, w1 = places("exps", 2 * T * H * S, ((E, HID), fp32))
        e1 = exps[:, 0:T * H * S].rearrange("p (j h k) -> p j h k", j=T, h=H)
        e2 = exps[:, T * H * S:].rearrange("p (j h k) -> p j h k", j=T, h=H)
        P, fc1_q, fc2_q, fc1_s, fc2_s = places("P", T * H * S, ((HID,), mybir.dt.int32), ((HC, D), mybir.dt.int32),
                                               ((HID,), fp32), ((HC, D), fp32))
        P = P[:, :].rearrange("p (j h k) -> p j h k", j=T, h=H)
        PT, w_rows, slot_rows, slot_sq, snT = places("PT", T * HP * 128, ((4, D), fp32), ((4, D), fp32), ((4, D), fp32), ((ES,), fp32))
        PT = PT[:, :].rearrange("p (j c q) -> p j c q", j=T, c=HP)

        ident = sb("ident", 128)
        head16 = sb("head16", H)
        head8 = sb("head8", HP)
        decay_step = sb("decay_step", 128)
        decayT = sb("decayT", 128)
        power = sb("power", 2 * T)
        half_power = sb("half_power", 4)
        vec_rows = sb("vec_rows", 128)
        vecs = sb("vecs", NVEC)
        g12 = sb("g12", 1)
        slot_n = sb("slot_n", 4)
        snT_hi, snT_lo = split("snT", ES)
        w1_hi, w1_lo = split("w1", E, HID)
        w2 = sb("w2", E, HC, D)
        wqT = sb("wqT", D)
        wkT = sb("wkT", D)
        woT = sb("woT", D)
        wv_half = sb("wv_half", 2, HP, VW)
        bv_row = sb("bv_row", D)
        v_bias = sb("v_bias", HP, VW)
        bo_all = sb("bo_all", D)
        m1_row = sb("m1_row", 3, MH)
        m1_half = sb("m1_half", 2, 3, MH)
        m_small = ctx.enter_context(nc.sbuf_tensor("m_small", [MH, 4], fp32))
        m2_rows = ctx.enter_context(nc.sbuf_tensor("m2_rows", [MH, MH], fp32))
        m2T = ctx.enter_context(nc.sbuf_tensor("m2T", [MH, MH], fp32))
        m3_wide = ctx.enter_context(nc.sbuf_tensor("m3_wide", [MH, 64], fp32))
        b3_all = sb("b3_all", 1)
        fc1 = sb("fc1", HID)
        fc2 = sb("fc2", HC, D)
        fb2_half = sb("fb2_half", D)

        x_in = sb("x_in", T, D)
        ctx_in = sb("ctx_in", T, D)
        kv = sb("kv", T, D)
        ctxT = sb("ctxT", TOK)
        r_stats = sb("r_stats", T, 6)
        r_mv = sb("r_mv", T, 2)
        r_pow_in = sb("r_pow_in", 2 * T)
        r_pow = sb("r_pow", 2 * T)
        r_small = sb("r_small", 4, T)
        wait_pad = sb("wait_pad", 1)
        pool_pad = sb("pool_pad", 1)
        y1 = sb("y1", T, D)
        x1 = sb("x1", T, D)
        xn = sb("xn", T, D)
        xnT_hi, xnT_lo = split("xnT", TOK)
        nmC = sb("nmC", T)
        C = sb("C", T, ES)
        sumC = sb("sumC", T)
        nmD = sb("nmD", EP, GB)
        DT = sb("DT", EP, TOK)
        sumD = sb("sumD", EP, GB)
        Dw = sb("Dw", T, ES)
        slotsT_hi, slotsT_lo = split("slotsT", E, GB, SL)
        CT = sb("CT", EP, TOK)
        x1b = sb("x1b", T, D)
        rC = sb("rC", T)
        hT = sb("hT", 2, 2, HC, TOK)
        eoT = sb("eoT", GB, 2, SL)
        eo = sb("eo", EP, GB, D)
        x2 = sb("x2", T, D)
        a_stats = sb("a_stats", T, 6)
        a_mv = sb("a_mv", T, 2)
        a_pow_in = sb("a_pow_in", T)
        a_pow = sb("a_pow", T)
        ctxT_kept = sb("ctxT_kept", TOK)
        x2b = sb("x2b", T, D)
        y2 = sb("y2", T, D)
        y2T = sb("y2T", TOK)
        QT = sb("QT", TOK)
        KT = sb("KT", TOK)
        KM = sb("KM", GB, HP, S)
        sumQ = sb("sumQ", GB)
        sumK = sb("sumK", GB)
        qk_sum = sb("qk_sum", GB)
        mean_rows = sb("mean_rows", 2, T, H)
        V = sb("V", GB, HP, VW)
        mx = sb("mx", T, H)
        Dm = sb("Dm", T, H, S)
        s1 = sb("s1", T, H)
        s2 = sb("s2", T, H)
        var = sb("var", T, H)
        h1 = ctx.enter_context(nc.sbuf_tensor("h1", [MH, 2 * TH], fp32))
        h2 = ctx.enter_context(nc.sbuf_tensor("h2", [MH, 2 * TH], fp32))
        zt = sb("zt", T, H)
        inv_t = sb("inv_t", T, H)
        den = sb("den", T, H)
        ao = sb("ao", T, D)
        aoT = sb("aoT", TOK)
        x3 = sb("x3", T, D)
        f_stats = sb("f_stats", T, 6)
        f_mv = sb("f_mv", T, 2)
        f_pow_in = sb("f_pow_in", T)
        f_pow = sb("f_pow", T)
        f_small = sb("f_small", 4, T)
        y3 = sb("y3", T, D)
        h3 = sb("h3", T, D)
        acc = sb("acc", T, D)
        h3T = sb("h3T", TOK)
        uT = sb("uT", HC, TOK)
        res = sb("res", T, D)

        def bank(name, n=1):
            return ctx.enter_context(nc.psum_tensor(name, [128, 512 * n], fp32))

        hid = [bank("hid0"), bank("hid1")]
        pair = bank("pair")
        mix = bank("mix")
        ra2 = bank("ra", 2)
        ra = [ra2[:, 0:512], ra2[:, 512:1024]]
        slot_banks = [ra, [hid[0][:, :], hid[1][:, :]]]

        def last(g):
            return isinstance(g, int) and g == GROUPS - 1

        def ended(g):
            return isinstance(g, int) and g >= GROUPS - 2

        at2 = bank("at", 2)
        at = [at2[:, 0:512], at2[:, 512:1024]]

        def tile_banks(g, j):
            return ra2 if last(g) and j == 1 else at2

        def value_bank(g, j):
            return ra2 if last(g) and j == 1 else mix

        def feed_banks(g):
            return (hid[0][:, :], hid[1][:, :], pair[:, 0:TOK]) if ended(g) else (at[0], at[1], mix[:, TOK:2 * TOK])

        names = """vecs_in slots_in mats_in cast_in weights0_in weights1_in weights2_in weights3_in
            pool_consts dve_consts pool_pre dve_pre pre_pow pre_pow_out w1_hi_ready w1_lo_ready
            vecs_up w_up slotT_up later_consts
            x_in_ready ctx_in_ready kv_ready r_up ctxT_up ctxT_ready x1_ready xn_ready xnT_up xnT_hi_ready xnT_lo_ready
            L_up nmC_ready C_ready LT_up LD_ready expD_ready DT_ready D_up D_dve D_act
            slots_up slots_dve slots_act slots_lo_ready r_pow_asked r_pow_ready route_step
            CT_up CT_dve CT_act rC_ready x1b_ready kept_ready h_up h_ready eoT_up eoT_ready eo_up eo_ready out_up x2_ready
            V_up V_ready K_up KT_ready KM_ready x2b_ready y2_ready y2T_up y2T_ready Q_up QT_ready mean_ready
            S_up Dm0_ready Dm1_ready e1_ready e2_ready stats_ready hid1_up hid1_ready hid2_up hid2_ready t_up zt_ready
            inv_t_ready Dt_ready P_ready PT_up PT_dve PT_act av_up ao_ready aoT_up aoT_ready o_up x3_ready
            a_pow_asked a_pow_ready attend_step f_pow_asked f_pow_ready feed_step
            h3_ready y3_ready h3T_up h3T_ready u_up u_ready z_up acc_step acc_ready res_ready out_done""".split()
        s = {n: ctx.enter_context(nc.semaphore(n)) for n in names}
        block = ctx.enter_context(nc.Block())
        VECS, MATS, CASTS = 9, 7, 12
        ROUTE_STEPS, ATTEND_STEPS, FEED_STEPS = 14, 17, 5

        def none(g=None):
            while True:
                yield

        @block.sync
        def _(sp):
            x_groups, ctx_groups, out_groups = (t.rearrange("b n d -> (b n) d").rearrange("(g j p) d -> g p j d", j=T, p=128)
                                                for t in (a["x"], a["ctx_1024"], out))

            def group(t, g):
                return t[g] if isinstance(g, int) else t[bass.ds(g, 1)].rearrange("a p j d -> (a p) j d")

            def load(g):
                if before(g):
                    sp.wait_ge(s["x1_ready"], nth(g, 1, 0))
                sp.dma_start(x_in[:, :, :], group(x_groups, g)).then_inc(s["x_in_ready"], 16)
                if before(g):
                    sp.wait_ge(s["kv_ready"], nth(g, 1, 0))
                    sp.wait_ge(s["ctxT_up"], nth(g, 1, 0))
                sp.dma_start(ctx_in[:, :, :], group(ctx_groups, g)).then_inc(s["ctx_in_ready"], 16)

            load(0)
            sp.dma_start(slot_rows[:, :, :], a["L0_ffn_slot_embeds"].rearrange("e s d -> (e s) d").rearrange("(c p) d -> p c d", p=128)).then_inc(s["slots_in"], 16)
            for r0, n, src in ((C_B1, 32, a["L0_ffn_b1"].rearrange("e (c p) -> (e c) p", p=128)),
                               (C_B2, E, a["L0_ffn_b2"]),
                               (C_G1, 1, a["L0_ffn_norm_gamma"].rearrange("(a p) -> a p", a=1)),
                               (C_G2, 1, a["L0_ffn_slot_norm_gamma"].rearrange("(a p) -> a p", a=1)),
                               (C_BQ, 1, a["L1_xattn_bq"].rearrange("(a p) -> a p", a=1)),
                               (C_BK, 1, a["L1_xattn_bk"].rearrange("(a p) -> a p", a=1)),
                               (C_FB, 4, a["L1_ffn_fc1_bias"].rearrange("(a p) -> a p", p=128)),
                               (C_LG, 1, a["L1_ffn_ln_gamma"].rearrange("(a p) -> a p", a=1)),
                               (C_LB, 1, a["L1_ffn_ln_beta"].rearrange("(a p) -> a p", a=1))):
                sp.dma_start(vec_rows[r0:r0 + n, :], src).then_inc(s["vecs_in"], 16)
            w1_in = a["L0_ffn_w1"].rearrange("e d h -> d e h")
            w2_in = a["L0_ffn_w2"].rearrange("e (c p) d -> p (e c) d", p=128).rearrange("p (e c) d -> p e c d", e=E)
            for p in range(EP):
                e = slice(2 * p, 2 * p + 2)
                sp.dma_start(w1[:, e, :], w1_in[:, e, :]).then_inc(s[f"weights{p}_in"], 16)
                sp.dma_start(w2[:, e, :, :], w2_in[:, e, :, :]).then_inc(s[f"weights{p}_in"], 16)
            for k, src in enumerate((a["L1_xattn_Wq"], a["L1_xattn_Wk"], a["L1_xattn_Wv"], a["L1_xattn_Wo"])):
                sp.dma_start(w_rows[:, k, :], src).then_inc(s["mats_in"], 16)
            sp.dma_start(m2_rows[:, :], a["L1_xattn_w2"]).then_inc(s["mats_in"], 16)
            sp.dma_start(fc1_q[:, :], a["L1_ffn_fc1_q"]).then_inc(s["mats_in"], 16)
            sp.dma_start(fc2_q[:, :, :], a["L1_ffn_fc2_q"].rearrange("(c p) d -> p c d", p=128)).then_inc(s["mats_in"], 16)

            def wide_row(dst, src, n=128):
                sp.dma_start(dst, src.rearrange("(a n) -> a n", a=1).to_broadcast([n, src.shape[0]])).then_inc(s["cast_in"], 16)

            wide_row(bv_row[:, :], a["L1_xattn_bv"])
            wide_row(bo_all[:, :], a["L1_xattn_bo"])
            wide_row(b3_all[:, :], a["L1_xattn_b3"])
            wide_row(fc1_s[:, :], a["L1_ffn_fc1_scales"].rearrange("a n -> (a n)"))
            wide_row(fc2_s[:, :, :].rearrange("p c d -> p (c d)"), a["L1_ffn_fc2_scales"].rearrange("c d -> (c d)"))
            wide_row(fb2_half[:, :], a["L1_ffn_fc2_bias"])
            with nc.allow_non_contiguous_dma(reason="the small network's weights, once"):
                for f in range(3):
                    sp.dma_start(m1_row[:, f, :], a["L1_xattn_w1"].rearrange("m f -> f m")[f:f + 1, :].to_broadcast([128, MH])).then_inc(s["cast_in"], 16)
                sp.dma_start(m_small[:, 0:1], a["L1_xattn_b1"].rearrange("(m a) -> m a", a=1)).then_inc(s["cast_in"], 16)
                sp.dma_start(m_small[:, 1:2], a["L1_xattn_b2"].rearrange("(m a) -> m a", a=1)).then_inc(s["cast_in"], 16)
                sp.dma_start(m_small[:, 2:3], a["L1_xattn_w3"].rearrange("a m -> m a")).then_inc(s["cast_in"], 16)

            def experts(g, i):
                pass

            def route(g):
                if not isinstance(g, int) or g + 1 < GROUPS:
                    load(g + 1)
                yield from none(g)

            def feed(g):
                yield
                yield
                yield
                sp.wait_ge(s["res_ready"], nth(g, 1, 2))
                sp.dma_start(group(out_groups, g), res[:, :, :]).then_inc(s["out_done"], 16)
                yield

            all_iterations(sp, experts, {"attend": none, "feed": feed, "turn": none, "route": route, "first_consts": none, "later_consts": none,
                                "split_first": none, "split_later": none})
            sp.wait_ge(s["out_done"], 16 * (GROUPS + 1))

        @block.gpsimd
        def _(pool):
            steps = [0]

            def link(ins):
                steps[0] += 1
                ins.then_inc(s["pool_pre"], 1)
                pool.wait_ge(s["pool_pre"], steps[0])

            pool.memset(ident[:, :], 0.0)
            pool.memset(head16[:, :], 1.0)
            pool.memset(decay_step[:, :], DECAY)
            pool.memset(power[:, 0:T], -0.5)
            pool.memset(power[:, T:2 * T], 0.5)
            pool.memset(half_power[:, :], 0.5)
            pool.memset(wv_half[:, :, :, :], 0.0)
            pool.memset(v_bias[:, :, :], 0.0)
            link(pool.memset(m1_half[:, :, :, :], 0.0))
            link(pool.memset(v_bias[0:64, :, 2 * DK:2 * DK + 1], 1.0))
            link(pool.memset(v_bias[64:128, :, 2 * DK + 1:2 * DK + 2], 1.0))
            pool.memset(decay_step[:, 64:65], 0.0)
            pool.affine_select(out=ident[:, :], in_=ident[:, :], compare_op=ALU.not_equal, fill=1.0,
                               base=0, pattern=[[-1, 128]], channel_multiplier=1)
            link(pool.affine_select(out=head16[:, :], in_=head16[:, :], compare_op=ALU.is_ge, fill=0.0,
                                    base=0, pattern=[[-DK, H]], channel_multiplier=1))
            pool.affine_select(out=head16[:, :], in_=head16[:, :], compare_op=ALU.is_ge, fill=0.0,
                               base=DK - 1, pattern=[[DK, H]], channel_multiplier=-1).then_inc(s["pool_consts"], 1)

            def first_consts():
                yield
                pool.wait_ge(s["pre_pow"], 1)
                pool.tensor_tensor(slot_n[:, :], slot_n[:, :], half_power[:, :], ALU.pow).then_inc(s["pre_pow_out"], 1)
                yield
                yield

            def later_consts():
                yield
                pool.wait_ge(s["later_consts"], 1)
                yield

            def plain_wait():
                pool.wait_ge(s["pool_consts"], 1)

            def experts(g, i):
                pass

            def route(g):
                pool.wait_ge(s["r_pow_asked"], nth(g, 2, 1))
                pool.tensor_tensor(r_pow[:, 0:T], r_pow_in[:, 0:T], power[:, 0:T], ALU.pow).then_inc(s["r_pow_ready"], 1)
                yield
                pool.wait_ge(s["r_pow_asked"], nth(g, 2, 2))
                pool.tensor_tensor(r_pow[:, :], r_pow_in[:, :], power[:, :], ALU.pow).then_inc(s["r_pow_ready"], 1)
                yield from none(g)

            def turn(g):
                if before(g):
                    pool.wait_ge(s["x2_ready"], nth(g, 1, 0))
                pool.wait_ge(s["x1_ready"], nth(g, 1, 1))
                pool.tensor_tensor(pool_pad[:, :], power[:, 0:1], power[:, 0:1], ALU.add)
                pool.tensor_copy(x1b[:, :, :], x1[:, :, :]).then_inc(s["x1b_ready"], 1)
                plain_wait()
                if before(g):
                    pool.wait_ge(s["K_up"], nth(g, 1, 0))
                pool.wait_ge(s["ctxT_ready"], nth(g, 1, 1))
                pool.tensor_copy(ctxT_kept[:, :], ctxT[:, :]).then_inc(s["kept_ready"], 1)
                yield

            def attend(g):
                pool.wait_ge(s["a_pow_asked"], nth(g, 1, 1))
                pool.tensor_tensor(a_pow[:, :], a_pow_in[:, :], power[:, 0:T], ALU.pow).then_inc(s["a_pow_ready"], 1)
                if before(g):
                    pool.wait_ge(s["x3_ready"], nth(g, 1, 0))
                pool.wait_ge(s["x2_ready"], nth(g, 1, 1))
                pool.tensor_tensor(x2b[:, :, :], x2[:, :, :], bo_all[:, :].unsqueeze(1).to_broadcast([128, T, D]), ALU.add).then_inc(s["x2b_ready"], 1)
                yield
                if not last(g):
                    if before(g):
                        pool.wait_ge(s["S_up"], nth(g, T, 0))
                    pool.wait_ge(s["KT_ready"], nth(g, 1, 1))
                    pool.tensor_tensor(KM[:, :, :, :], KT[:, :].rearrange("p (b n) -> p b n", b=GB).unsqueeze(2).to_broadcast([128, GB, HP, S]),
                                       head8[:, :].unsqueeze(1).unsqueeze(3).to_broadcast([128, GB, HP, S]), ALU.mult).then_inc(s["KM_ready"], 1)
                for _ in STEPS_AT["attend"][2:]:
                    yield
                pool.wait_ge(s["f_pow_asked"], nth(g, 2, 1))
                pool.tensor_tensor(f_pow[:, :], f_pow_in[:, :], power[:, 0:T], ALU.pow).then_inc(s["f_pow_ready"], 1)
                yield

            def feed(g):
                pool.wait_ge(s["f_pow_asked"], nth(g, 2, 2))
                pool.tensor_tensor(f_pow[:, :], f_pow_in[:, :], power[:, 0:T], ALU.pow).then_inc(s["f_pow_ready"], 1)
                pool.wait_ge(s["y3_ready"], nth(g, 1, 1))
                if before(g):
                    pool.wait_ge(s["res_ready"], nth(g, 1, 1))
                pool.tensor_tensor(acc[:, :, :], x3[:, :, :], y3[:, :, :], ALU.add).then_inc(s["acc_step"], 1)
                pool.wait_ge(s["acc_step"], nth(g, 1, 1))
                pool.tensor_tensor(acc[:, :, :], acc[:, :, :], fb2_half[:, :].unsqueeze(1).to_broadcast([128, T, D]), ALU.add).then_inc(s["acc_ready"], 1)
                yield from none(g)

            all_iterations(pool, experts, {"attend": attend, "feed": feed, "turn": turn, "route": route,
                                 "first_consts": first_consts, "later_consts": later_consts,
                                 "split_first": none, "split_later": none})

        @block.tensor
        def _(pe):
            def plain_wait():
                pe.wait_ge(s["pool_consts"], 1)

            def transposes(psum, src, done, n=T):
                for j in range(n):
                    ins = pe.transpose(psum[:, 128 * j:128 * j + 128], src[:, j, :], ident[:, :])
                ins.then_inc(s[done], 1)

            def product(out, lhsT, rhs):
                pe.matmul(out, lhsT[0], rhs[0], start=True, stop=False)
                pe.matmul(out, lhsT[0], rhs[1], start=False, stop=False)
                return pe.matmul(out, lhsT[1], rhs[0], start=False, stop=True)

            pe.wait_ge(s["dve_consts"], 1)

            def first_consts():
                yield
                pe.wait_ge(s["vecs_in"], 16 * VECS)
                pe.transpose(mix[:, 0:NVEC], vec_rows[0:NVEC, :], ident[0:NVEC, 0:NVEC]).then_inc(s["vecs_up"], 1)
                yield
                pe.wait_ge(s["dve_consts"], 2)
                transposes(at[1], slot_rows, "slotT_up", 4)
                pe.wait_ge(s["dve_consts"], 3)
                yield

            def later_consts():
                pe.wait_ge(s["mats_in"], 16 * MATS)
                transposes(at[0], w_rows, "w_up", 4)
                pe.transpose(mix[0:MH, 0:MH], m2_rows[:, :], ident[0:MH, 0:MH]).then_inc(s["w_up"], 1)
                yield
                pe.wait_ge(s["later_consts"], 1)
                yield

            def experts(g, i):
                if i == PIECES:
                    pe.wait_ge(s["CT_dve"], nth(g, 1, 1))
                    pe.wait_ge(s["CT_act"], nth(g, 1, 1))
                    if before(g):
                        pe.wait_ge(s["ao_ready"], nth(g, T, 0))
                    for j in range(T):
                        for c in range(EP):
                            if j == 0:
                                pe.wait_ge(s["eo_ready"], nth(g, EP, c + 1))
                            for par in range(2):
                                b = 2 * j + par
                                ins = pe.matmul(mix[64 * par:64 * par + 64, 128 * j:128 * j + 128], CT[:, c, 64 * b:64 * b + 64],
                                                eo[:, c, b, :], start=(c == 0), stop=(c == EP - 1))
                    ins.then_inc(s["out_up"], 1)
                elif ORDER[i][0] == "first":
                    n = ORDER[i][1]
                    e, half = n // 2, n % 2
                    if isinstance(g, int) and g == 0 and n % 4 == 0:
                        pe.wait_ge(s[f"weights{n // 4}_in"], 32)
                        pe.wait_ge(s["w1_lo_ready"], n // 4 + 1)
                    if n == 0:
                        pe.wait_ge(s["slots_dve"], nth(g, T, T))
                        pe.wait_ge(s["slots_act"], nth(g, T, T))
                        pe.wait_ge(s["slots_lo_ready"], nth(g, 1, 1))
                    if n >= 2 or before(g):
                        pe.wait_ge(s["h_ready"], nth(g, FIRSTS, n - 1))
                    for c in range(2 * half, 2 * half + 2):
                        chunk = slice(128 * c, 128 * c + 128)
                        ins = product(hid[half][:, TOK * (c % 2):TOK * (c % 2) + TOK], (w1_hi[:, e, chunk], w1_lo[:, e, chunk]),
                                      (slotsT_hi[:, e, :, :], slotsT_lo[:, e, :, :]))
                    ins.then_inc(s["h_up"], 1)
                elif ORDER[i][0] == "second":
                    _, p, q = ORDER[i]
                    k = q // 2
                    if q == 0:
                        pe.wait_ge(s["h_ready"], nth(g, FIRSTS, 4 * p + 4))
                        if p >= 1 or before(g):
                            pe.wait_ge(s["eo_ready"], nth(g, EP, p))
                    for c in range(HC // 2 * (q % 2), HC // 2 * (q % 2) + HC // 2):
                        ins = pe.matmul(pair[:, TOK * k:TOK * k + TOK], w2[:, 2 * p + k, c, :], hT[:, p % 2, k, c, :],
                                        start=(c == 0), stop=(c == HC - 1))
                    if q == 3:
                        ins.then_inc(s["eoT_up"], 1)
                else:
                    p = ORDER[i][1]
                    pe.wait_ge(s["eoT_ready"], nth(g, EP, p + 1))
                    for b in range(GB):
                        ins = pe.transpose(pair[:, 128 * b:128 * b + 128], eoT[:, b, :, :].rearrange("p k n -> p (k n)"), ident[:, :])
                    ins.then_inc(s["eo_up"], 1)

            def route(g):
                yield
                pe.wait_ge(s["kv_ready"], nth(g, 1, 1))
                if before(g):
                    pe.wait_ge(s["CT_dve"], nth(g, 1, 0))
                    pe.wait_ge(s["CT_act"], nth(g, 1, 0))
                pe.matmul(ra[0][:, 0:TOK], decayT[:, :], kv[:, :, :], start=True, stop=True).then_inc(s["r_up"], 1)
                pe.wait_ge(s["ctx_in_ready"], nth(g, 16, 16))
                transposes(ra[1], ctx_in, "ctxT_up")
                yield
                yield
                pe.wait_ge(s["xn_ready"], nth(g, 1, 1))
                transposes(ra[0], xn, "xnT_up")
                yield
                pe.wait_ge(s["xnT_hi_ready"], nth(g, 1, 1))
                pe.wait_ge(s["xnT_lo_ready"], nth(g, 1, 1))
                pe.wait_ge(s["ctxT_ready"], nth(g, 1, 1))
                for j in range(T):
                    t = slice(128 * j, 128 * j + 128)
                    product(ra[j], (xnT_hi[:, t], xnT_lo[:, t]), (snT_hi[:, :], snT_lo[:, :])).then_inc(s["L_up"], 1)
                yield
                if not isinstance(g, int) or g >= 2:
                    pe.wait_ge(s["Dm1_ready"], nth(g - 2, 1, 1))
                for c in range(EP):
                    slots = slice(128 * c, 128 * c + 128)
                    ins = product(at[c // 2][:, TOK * (c % 2):TOK * (c % 2) + TOK], (snT_hi[:, slots], snT_lo[:, slots]),
                                  (xnT_hi[:, :], xnT_lo[:, :]))
                    if c % 2:
                        ins.then_inc(s["LT_up"], 1)
                yield
                yield
                yield
                yield
                pe.wait_ge(s["DT_ready"], nth(g, 1, 1))
                for j in range(T):
                    pe.wait_ge(s["C_ready"], nth(g, T, j + 1))
                    for c in range(EP):
                        ins = pe.transpose(ra[j][:, 128 * c:128 * c + 128], DT[:, c, 128 * j:128 * j + 128], ident[:, :])
                    ins.then_inc(s["D_up"], 1)
                yield
                for j in range(T):
                    if j == 0:
                        pe.wait_ge(s["D_dve"], nth(g, 1, 1))
                        pe.wait_ge(s["D_act"], nth(g, 1, 1))
                    elif before(g):
                        pe.wait_ge(s["h_ready"], nth(g, FIRSTS, 0))
                    for par in range(2):
                        p = slice(64 * par, 64 * par + 64)
                        pe.matmul(slot_banks[j][par], xn[p, j, :], Dw[p, j, :], start=True, stop=True).then_inc(s["slots_up"], 1)
                    yield

            def turn(g):
                pe.wait_ge(s["slots_dve"], nth(g, T, T))
                pe.wait_ge(s["slots_act"], nth(g, T, T))
                pe.wait_ge(s["C_ready"], nth(g, T, T))
                for j in range(T):
                    for c in range(EP):
                        ins = pe.transpose(ra[j][:, 128 * c:128 * c + 128], C[:, j, 128 * c:128 * c + 128], ident[:, :])
                    ins.then_inc(s["CT_up"], 1)
                yield

            def attend(g):
                pe.wait_ge(s["kept_ready"], nth(g, 1, 1))
                if before(g):
                    pe.wait_ge(s["x3_ready"], nth(g, 1, 0))
                else:
                    pe.wait_ge(s["LD_ready"], nth(g + 1, T, T))
                for b in range(GB):
                    for half in range(2):
                        ins = pe.matmul(at[b // 2][64 * half:64 * half + 64, 144 * (b % 2):144 * (b % 2) + 144],
                                        ctxT_kept[:, 64 * b:64 * b + 64], wv_half[:, half, :, :], start=True, stop=True)
                    if b % 2:
                        ins.then_inc(s["V_up"], 1)
                pe.wait_ge(s["x2_ready"], nth(g, 1, 1))
                pe.matmul(mix[:, 0:TOK], wkT[:, :], ctxT_kept[:, :], start=True, stop=True).then_inc(s["K_up"], 1)
                yield
                pe.wait_ge(s["y2_ready"], nth(g, 1, 1))
                pe.wait_ge(s["KT_ready"], nth(g, 1, 1))
                transposes(mix, y2, "y2T_up")
                yield
                pe.wait_ge(s["y2T_ready"], nth(g, 1, 1))
                if before(g):
                    pe.wait_ge(s["res_ready"], nth(g - 1, 1, 1))
                pe.matmul(mix[:, TOK:2 * TOK], wqT[:, :], y2T[:, :], start=True, stop=True).then_inc(s["Q_up"], 1)
                yield
                for j in range(T):
                    plain_wait()
                    if j == 0:
                        pe.wait_ge(s["QT_ready"], nth(g, 1, 1))
                        pe.wait_ge(s["KM_ready"], nth(g, 1, 1))
                        if ended(g - 1):
                            pe.wait_ge(s["u_ready"], nth(g - 1, T, 0))
                        elif before(g):
                            pe.wait_ge(s["u_ready"], nth(g, T, 0))
                    elif not last(g):
                        pe.wait_ge(s["Dm0_ready"], nth(g, 1, 1))
                    for half in range(2):
                        r = slice(64 * half, 64 * half + 64)
                        for par in range(2):
                            b = 2 * j + par
                            ins = pe.matmul(tile_banks(g, j)[64 * par:64 * par + 64, 512 * half:512 * half + 512], QT[r, 64 * b:64 * b + 64], KM[r, b, :, :],
                                            start=True, stop=True)
                    ins.then_inc(s["S_up"], 1)
                    yield
                yield
                yield
                pe.wait_ge(s["mean_ready"], nth(g, 1, 1))
                pe.wait_ge(s["stats_ready"], nth(g, 1, 1))
                for par in range(2):
                    for f, rows in enumerate((mean_rows[:, par, :, :], mx[:, :, :], var[:, :, :])):
                        ins = pe.matmul(mix[0:MH, TH * par:TH * par + TH], m1_row[:, 0, :] if f == 0 else m1_half[:, par, f, :],
                                        rows, start=(f == 0), stop=(f == 2))
                ins.then_inc(s["hid1_up"], 1)
                yield
                plain_wait()
                pe.wait_ge(s["hid1_ready"], nth(g, 1, 1))
                pe.matmul(mix[0:MH, 128:128 + 2 * TH], m2T[:, :], h1[:, :], start=True, stop=True).then_inc(s["hid2_up"], 1)
                yield
                plain_wait()
                pe.wait_ge(s["hid2_ready"], nth(g, 1, 1))
                for par in range(2):
                    ins = pe.matmul(mix[64 * par:64 * par + 64, 192:192 + TH], m3_wide[:, :], h2[:, TH * par:TH * par + TH],
                                    start=True, stop=True)
                ins.then_inc(s["t_up"], 1)
                yield
                yield
                yield
                yield
                yield

                def turned(j):
                    pe.wait_ge(s["P_ready"], nth(g, T, j + 1))
                    for c in range(HP):
                        ins = pe.transpose(tile_banks(g, j)[:, 128 * c:128 * c + 128], P[:, j, 2 * c:2 * c + 2, :], ident[:, :])
                    ins.then_inc(s["PT_up"], 1)

                def values(j):
                    for c in range(HP):
                        for par in range(2):
                            ins = pe.matmul(value_bank(g, j)[64 * par:64 * par + 64, 144 * j + VW * c:144 * j + VW * c + VW],
                                            PT[:, j, c, 64 * par:64 * par + 64], V[:, 2 * j + par, c, :], start=True, stop=True)
                    ins.then_inc(s["av_up"], 1)

                pe.wait_ge(s["Dm1_ready"], nth(g, 1, 1))
                if not isinstance(g, int) or g + 2 < GROUPS:
                    pe.wait_ge(s["LD_ready"], nth(g + 2, T, T))
                turned(0)
                yield
                if last(g):
                    turned(1)
                pe.wait_ge(s["PT_dve"], nth(g, T, 1))
                pe.wait_ge(s["PT_act"], nth(g, T, 1))
                if not last(g):
                    turned(1)
                pe.wait_ge(s["zt_ready"], nth(g, 1, 1))
                if not ended(g - 1):
                    pe.wait_ge(s["res_ready"], nth(g, 1, 1))
                values(0)
                yield
                pe.wait_ge(s["PT_dve"], nth(g, T, 2))
                pe.wait_ge(s["PT_act"], nth(g, T, 2))
                if not last(g):
                    pe.wait_ge(s["ao_ready"], nth(g, T, 1))
                values(1)
                yield
                pe.wait_ge(s["ao_ready"], nth(g, T, T))
                transposes(at[0], ao, "aoT_up")
                yield
                pe.wait_ge(s["aoT_ready"], nth(g, 1, 1))
                for j in range(T):
                    ins = pe.matmul(at[1][:, 128 * j:128 * j + 128], aoT[:, 128 * j:128 * j + 128], woT[:, :], start=True, stop=True)
                ins.then_inc(s["o_up"], 1)
                yield

            def feed(g):
                yield
                b0, b1, bz = feed_banks(g)
                pe.wait_ge(s["h3_ready"], nth(g, 1, 1))
                if ended(g):
                    pe.wait_ge(s["h_ready"], nth(GROUPS, FIRSTS, 0))
                else:
                    pe.wait_ge(s["V_ready"], nth(g + 1, T, T))
                transposes(b0, h3, "h3T_up")
                yield
                pe.wait_ge(s["h3T_ready"], nth(g, 1, 1))
                for c in range(HC):
                    ins = pe.matmul((b0, b1)[c // 2][:, TOK * (c % 2):TOK * (c % 2) + TOK], fc1[:, 128 * c:128 * c + 128], h3T[:, :],
                                    start=True, stop=True)
                    if c % 2:
                        ins.then_inc(s["u_up"], 1)
                yield
                pe.wait_ge(s["u_ready"], nth(g, T, T))
                if ended(g):
                    pe.wait_ge(s["eo_ready"], nth(GROUPS, EP, 0))
                else:
                    pe.wait_ge(s["QT_ready"], nth(g + 1, 1, 1))
                for j in range(T):
                    for c in range(HC):
                        ins = pe.matmul(bz[:, 128 * j:128 * j + 128], uT[:, c, 128 * j:128 * j + 128], fc2[:, c, :],
                                        start=(c == 0), stop=(c == HC - 1))
                ins.then_inc(s["z_up"], 1)
                yield

            all_iterations(pe, experts, {"attend": attend, "feed": feed, "turn": turn, "route": route,
                                 "first_consts": first_consts, "later_consts": later_consts,
                                 "split_first": none, "split_later": none}, steps_first=True)

        @block.scalar
        def _(act):
            act.sem_inc(s["out_done"], 16)
            act.sem_inc(s["res_ready"], 1)

            def first_consts():
                yield
                yield
                act.wait_ge(s["dve_consts"], 3)
                yield

            def split_w1(first):
                for p in (first, first + 1):
                    act.wait_ge(s[f"weights{p}_in"], 32)
                    act.activation(w1_hi[:, 2 * p:2 * p + 2, :], w1[:, 2 * p:2 * p + 2, :], ACT.Copy).then_inc(s["w1_hi_ready"], 1)
                    yield

            def later_consts():
                yield
                act.wait_ge(s["later_consts"], 1)
                yield

            def experts(g, i):
                if i < PIECES and ORDER[i][0] == "first":
                    n = ORDER[i][1]
                    e, half = n // 2, n % 2
                    act.wait_ge(s["h_up"], nth(g, FIRSTS, n + 1))
                    for c in range(2 * half, 2 * half + 2):
                        ins = act.activation(hT[:, e // 2 % 2, e % 2, c, :], hid[half][:, TOK * (c % 2):TOK * (c % 2) + TOK], ACT.Gelu,
                                             bias=vecs[:, C_B1 + HC * e + c:C_B1 + HC * e + c + 1])
                    ins.then_inc(s["h_ready"], 1)

            def route(g):
                act.wait_ge(s["ctx_in_ready"], nth(g, 16, 16))
                act.activation(kv[:, :, :], ctx_in[:, :, :], ACT.Square).then_inc(s["kv_ready"], 1)
                yield
                act.wait_ge(s["ctxT_up"], nth(g, 1, 1))
                if before(g):
                    act.wait_ge(s["kept_ready"], nth(g, 1, 0))
                act.activation(ctxT[:, :], ra[1][:, 0:TOK], ACT.Copy).then_inc(s["ctxT_ready"], 1)
                yield
                yield
                act.wait_ge(s["xnT_up"], nth(g, 1, 1))
                act.activation(xnT_hi[:, :], ra[0][:, 0:TOK], ACT.Copy).then_inc(s["xnT_hi_ready"], 1)
                yield
                yield
                yield
                if before(g):
                    act.wait_ge(s["CT_up"], nth(g, T, 0))
                    act.wait_ge(s["rC_ready"], nth(g, 1, 0))
                for j in range(T):
                    act.wait_ge(s["nmC_ready"], nth(g, T, j + 1))
                    act.activation(C[:, j, :], ra[j], ACT.Exp, bias=nmC[:, j:j + 1], accum_out=sumC[:, j:j + 1]).then_inc(s["C_ready"], 1)
                yield
                for q in range(2):
                    act.wait_ge(s["LD_ready"], nth(g, 2, q + 1))
                    act.activation(DT[:, 2 * q:2 * q + 2, :], DT[:, 2 * q:2 * q + 2, :], ACT.Exp).then_inc(s["expD_ready"], 1)
                yield
                yield
                act.wait_ge(s["D_up"], nth(g, T, 2))
                act.activation(Dw[:, 1, :], ra[1], ACT.Copy).then_inc(s["D_act"], 1)
                yield
                for j in range(T):
                    if j == 0 and before(g):
                        act.wait_ge(s["h_up"], nth(g, FIRSTS, 0))
                    act.wait_ge(s["slots_up"], nth(g, 2 * T, 2 * j + 2))
                    act.activation(slotsT_hi[:, :, 2 * j + 1, :], slot_banks[j][1].rearrange("p (e k) -> p e k", e=E),
                                   ACT.Copy, scale=vecs[:, C_G1:C_G1 + 1]).then_inc(s["slots_act"], 1)
                    yield

            def turn(g):
                act.wait_ge(s["CT_up"], nth(g, T, 2))
                if before(g):
                    act.wait_ge(s["out_up"], nth(g, 1, 0))
                act.activation(CT[:, :, 128:256], ra[1].rearrange("p (c t) -> p c t", c=EP), ACT.Copy).then_inc(s["CT_act"], 1)
                yield

            def attend(g):
                act.wait_ge(s["K_up"], nth(g, 1, 1))
                if before(g):
                    act.wait_ge(s["mean_ready"], nth(g, 1, 0))
                act.activation(KT[:, :], mix[:, 0:TOK], ACT.Identity, bias=vecs[:, C_BK:C_BK + 1]).then_inc(s["KT_ready"], 1)
                yield
                act.wait_ge(s["y2T_up"], nth(g, 1, 1))
                act.activation(y2T[:, :], mix[:, 0:TOK], ACT.Copy).then_inc(s["y2T_ready"], 1)
                yield
                act.wait_ge(s["Q_up"], nth(g, 1, 1))
                act.activation(QT[:, :], mix[:, TOK:2 * TOK], ACT.Identity, bias=vecs[:, C_BQ:C_BQ + 1]).then_inc(s["QT_ready"], 1)
                yield
                yield
                yield
                for j in range(T):
                    if j == 0 and before(g):
                        act.wait_ge(s["stats_ready"], nth(g, 1, 0))
                    act.wait_ge(s[f"Dm{j}_ready"], nth(g, 1, 1))
                    act.activation(e1[:, j, :, :], Dm[:, j, :, :], ACT.Exp, scale=DK ** -0.5).then_inc(s["e1_ready"], 1)
                    act.activation(e2[:, j, :, :], Dm[:, j, :, :], ACT.Exp, scale=2 * DK ** -0.5).then_inc(s["e2_ready"], 1)
                    yield
                act.wait_ge(s["hid1_up"], nth(g, 1, 1))
                act.activation(h1[:, :], mix[0:MH, 0:2 * TH], ACT.Gelu, bias=m_small[:, 0:1]).then_inc(s["hid1_ready"], 1)
                yield
                act.wait_ge(s["hid2_up"], nth(g, 1, 1))
                act.activation(h2[:, :], mix[0:MH, 128:128 + 2 * TH], ACT.Gelu, bias=m_small[:, 1:2]).then_inc(s["hid2_ready"], 1)
                yield
                yield
                act.wait_ge(s["zt_ready"], nth(g, 1, 1))
                act.activation(inv_t[:, :, :], zt[:, :, :], ACT.Exp, scale=-1.0).then_inc(s["inv_t_ready"], 1)
                yield
                yield
                for j in range(T):
                    act.wait_ge(s["Dt_ready"], nth(g, T, j + 1))
                    act.activation(P[:, j, :, :], Dm[:, j, :, :], ACT.Exp, scale=0.5).then_inc(s["P_ready"], 1)
                    yield
                for j in range(T):
                    act.wait_ge(s["PT_up"], nth(g, T, j + 1))
                    act.activation(PT[:, j, 4:8, :], tile_banks(g, j)[:, 512:1024], ACT.Relu).then_inc(s["PT_act"], 1)
                    yield
                yield
                act.wait_ge(s["aoT_up"], nth(g, 1, 1))
                act.activation(aoT[:, :], at[0][:, 0:TOK], ACT.Copy).then_inc(s["aoT_ready"], 1)
                yield
                yield

            def feed(g):
                yield
                yield
                for c in range(HC):
                    act.wait_ge(s["u_up"], nth(g, 2, c // 2 + 1))
                    ins = act.activation(uT[:, c, :], feed_banks(g)[c // 2][:, TOK * (c % 2):TOK * (c % 2) + TOK], ACT.Silu,
                                         bias=vecs[:, C_FB + c:C_FB + c + 1])
                    if c % 2:
                        ins.then_inc(s["u_ready"], 1)
                yield
                yield

            all_iterations(act, experts, {"attend": attend, "feed": feed, "turn": turn, "route": route,
                                 "first_consts": first_consts, "later_consts": later_consts,
                                 "split_first": lambda: split_w1(0), "split_later": lambda: split_w1(2)})

        @block.vector
        def _(dve):
            n = [0]

            def pre(ins):
                n[0] += 1
                ins.then_inc(s["dve_pre"], 1)
                dve.wait_ge(s["dve_pre"], n[0])

            dve.wait_ge(s["pool_consts"], 1)
            dve.tensor_tensor(head8[:, :], head16[:, 0:8], head16[:, 8:16], ALU.add)
            dve.tensor_tensor_scan(decayT[:, :], decay_step[:, :], ident[:, :], 0.0, ALU.mult, ALU.add).then_inc(s["dve_consts"], 1)

            def first_consts():
                yield
                dve.wait_ge(s["slots_in"], 16)
                pre(dve.tensor_tensor(slot_sq[:, :, :], slot_rows[:, :, :], slot_rows[:, :, :], ALU.mult))
                dve.tensor_reduce(slot_n[:, :], slot_sq[:, :, :], AX, ALU.add).then_inc(s["pre_pow"], 1)
                dve.wait_ge(s["pre_pow_out"], 1)
                pre(dve.tensor_scalar(slot_n[:, :], slot_n[:, :], 1e-12, None, ALU.max))
                pre(dve.reciprocal(slot_n[:, :], slot_n[:, :]))
                pre(dve.tensor_scalar(slot_n[:, :], slot_n[:, :], float(D) ** 0.5, None, ALU.mult))
                dve.tensor_tensor(slot_rows[:, :, :], slot_rows[:, :, :], slot_n[:, :].unsqueeze(2).to_broadcast([128, 4, D]),
                                  ALU.mult).then_inc(s["dve_consts"], 1)
                dve.wait_ge(s["vecs_up"], 1)
                pre(dve.tensor_copy(vecs[:, :], mix[:, 0:NVEC]))
                pre(dve.tensor_tensor(g12[:, :], vecs[:, C_G1:C_G1 + 1], vecs[:, C_G2:C_G2 + 1], ALU.mult))
                yield
                dve.wait_ge(s["slotT_up"], 1)
                pre(dve.tensor_scalar(snT[:, :], at[1], g12[:, :], None, ALU.mult))
                pre(dve.tensor_copy(snT_hi[:, :], snT[:, :]))
                dve.tensor_tensor(snT_lo[:, :], snT[:, :], snT_hi[:, :], ALU.subtract).then_inc(s["dve_consts"], 1)
                yield

            def split_w1(first):
                for p in (first, first + 1):
                    e = slice(2 * p, 2 * p + 2)
                    dve.wait_ge(s[f"weights{p}_in"], 32)
                    dve.wait_ge(s["w1_hi_ready"], p + 1)
                    dve.tensor_tensor(w1_lo[:, e, :], w1[:, e, :], w1_hi[:, e, :], ALU.subtract).then_inc(s["w1_lo_ready"], 1)
                    yield

            def later_consts():
                dve.wait_ge(s["w_up"], 2)
                wT = at[0].rearrange("p (k d) -> p k d", k=4)
                dve.tensor_copy(wqT[:, :], wT[:, 0, :])
                dve.tensor_copy(wkT[:, :], wT[:, 1, :])
                dve.tensor_copy(woT[:, :], wT[:, 3, :])
                wv = wT[:, 2, :].rearrange("p (c a k) -> p c a k", a=2, k=DK)
                for half in range(2):
                    dve.tensor_copy(wv_half[:, half, :, DK * half:DK * half + DK], wv[:, :, half, :])
                dve.tensor_copy(m2T[:, :], mix[0:MH, 0:MH])
                dve.wait_ge(s["cast_in"], 16 * CASTS)
                bv = bv_row[:, :].rearrange("p (c a k) -> p c a k", a=2, k=DK)
                for half in range(2):
                    p = slice(64 * half, 64 * half + 64)
                    dve.tensor_copy(v_bias[p, :, DK * half:DK * half + DK], bv[p, :, half, :])
                pre(dve.tensor_scalar(m1_row[:, 0, :], m1_row[:, 0, :], DK ** -0.5 / (S * S), None, ALU.mult))
                for half in range(2):
                    p = slice(64 * half, 64 * half + 64)
                    dve.tensor_scalar(m1_half[p, half, 1, :], m1_row[p, 1, :], DK ** -0.5 / S, None, ALU.mult)
                    dve.tensor_scalar(m1_half[p, half, 2, :], m1_row[p, 2, :], 1.0 / (S * (S - 1)), None, ALU.mult)
                dve.tensor_copy(m3_wide[:, :], m_small[:, 2:3].to_broadcast([MH, 64]))
                pre(dve.tensor_scalar(fb2_half[:, :], fb2_half[:, :], 0.5, None, ALU.mult))
                dve.tensor_scalar(fc1[:, :], fc1_q[:, :], -128.0, None, ALU.add)
                pre(dve.tensor_scalar(fc2[:, :, :], fc2_q[:, :, :], -128.0, None, ALU.add))
                dve.tensor_tensor(fc1[:, :], fc1[:, :], fc1_s[:, :], ALU.mult)
                dve.tensor_tensor(fc2[:, :, :], fc2[:, :, :], fc2_s[:, :, :], ALU.mult).then_inc(s["later_consts"], 1)
                dve.wait_ge(s["later_consts"], 1)
                yield
                yield

            def linker(name, per, g):
                k = [0]

                def link(ins):
                    k[0] += 1
                    ins.then_inc(s[name], 1)
                    dve.wait_ge(s[name], nth(g, per, k[0]))

                return link, k

            def moments(link, src, stats, mv):
                for j in range(T):
                    ins = dve.bn_stats(stats[:, j, :], src[:, j, :])
                link(ins)
                dve.memset(wait_pad[:, :], 0.0)
                for j in range(T):
                    ins = dve.bn_aggr(mv[:, j, :], stats[:, j, :])
                link(ins)

            def centred(dst, src, mv, scale):
                for j in range(T):
                    ins = dve.tensor_scalar(dst[:, j, :], src[:, j, :], mv[:, j, 0:1], scale[:, j:j + 1], ALU.subtract, ALU.mult)
                return ins

            def experts(g, i):
                if i == PIECES:
                    dve.wait_ge(s["out_up"], nth(g, 1, 1))
                    dve.wait_ge(s["x1b_ready"], nth(g, 1, 1))
                    dve.wait_ge(s["rC_ready"], nth(g, 1, 1))
                    if before(g):
                        dve.wait_ge(s["x2b_ready"], nth(g, 1, 0))
                    for j in range(T):
                        ins = dve.scalar_tensor_tensor(x2[:, j, :], mix[:, 128 * j:128 * j + 128], rC[:, j:j + 1], x1b[:, j, :], ALU.mult, ALU.add)
                    ins.then_inc(s["x2_ready"], 1)
                elif ORDER[i][0] == "second" and ORDER[i][2] == 3:
                    p = ORDER[i][1]
                    dve.wait_ge(s["eoT_up"], nth(g, EP, p + 1))
                    dve.tensor_tensor(eoT[:, :, :, :].rearrange("p b k n -> p k b n"), pair[:, :].rearrange("p (k b n) -> p k b n", k=2, b=GB),
                                      vecs[:, C_B2 + 2 * p:C_B2 + 2 * p + 2].unsqueeze(2).unsqueeze(3).to_broadcast([128, 2, GB, SL]), ALU.add).then_inc(s["eoT_ready"], 1)
                elif ORDER[i][0] == "turned":
                    p = ORDER[i][1]
                    dve.wait_ge(s["eo_up"], nth(g, EP, p + 1))
                    dve.tensor_copy(eo[:, p, :, :], pair[:, :].rearrange("p (b d) -> p b d", b=GB)).then_inc(s["eo_ready"], 1)

            def route(g):
                link, k = linker("route_step", ROUTE_STEPS, g)
                dve.wait_ge(s["x_in_ready"], nth(g, 16, 16))
                moments(link, x_in, r_stats, r_mv)
                dve.tensor_scalar(r_pow_in[:, 0:T], r_mv[:, :, 1], EPS, None, ALU.add).then_inc(s["r_pow_asked"], 1)
                yield
                dve.wait_ge(s["r_pow_ready"], nth(g, 2, 1))
                link(centred(y1, x_in, r_mv, r_pow))
                dve.wait_ge(s["r_up"], nth(g, 1, 1))
                link(dve.tensor_tensor(y1[:, :, :], y1[:, :, :], ra[0][:, 0:TOK].rearrange("p (j d) -> p j d", j=T), ALU.mult))
                if before(g):
                    dve.wait_ge(s["x1b_ready"], nth(g, 1, 0))
                dve.tensor_tensor(x1[:, :, :], x_in[:, :, :], y1[:, :, :], ALU.add).then_inc(s["x1_ready"], 1)
                dve.wait_ge(s["x1_ready"], nth(g, 1, 1))
                moments(link, x1, r_stats, r_mv)
                dve.tensor_scalar(r_pow_in[:, 0:T], r_mv[:, :, 1], EPS, None, ALU.add)
                dve.tensor_scalar(r_pow_in[:, T:2 * T], r_mv[:, :, 1], float(D), None, ALU.mult).then_inc(s["r_pow_asked"], 1)
                yield
                dve.wait_ge(s["r_pow_ready"], nth(g, 2, 2))
                link(dve.tensor_tensor(r_small[:, 0, :], r_pow[:, 0:T], r_pow[:, T:2 * T], ALU.mult))
                link(dve.tensor_scalar(r_small[:, 1, :], r_small[:, 0, :], 1e-12, None, ALU.max))
                link(dve.reciprocal(r_small[:, 2, :], r_small[:, 1, :]))
                link(dve.scalar_tensor_tensor(r_small[:, 3, :], r_small[:, 2, :], float(D) ** 0.5, r_pow[:, 0:T], ALU.mult, ALU.mult))
                centred(xn, x1, r_mv, r_small[:, 3]).then_inc(s["xn_ready"], 1)
                yield
                dve.wait_ge(s["xnT_hi_ready"], nth(g, 1, 1))
                dve.tensor_tensor(xnT_lo[:, :], ra[0][:, 0:TOK], xnT_hi[:, :], ALU.subtract).then_inc(s["xnT_lo_ready"], 1)
                yield
                for j in range(T):
                    dve.wait_ge(s["L_up"], nth(g, T, j + 1))
                    dve.tensor_reduce(nmC[:, j:j + 1], ra[j], AX, ALU.max, negate=True).then_inc(s["nmC_ready"], 1)
                yield
                if before(g):
                    dve.wait_ge(s["D_up"], nth(g, T, 0))
                for q in range(2):
                    c = slice(2 * q, 2 * q + 2)
                    LT = at[q].rearrange("p (c b n) -> p c b n", c=2, b=GB)
                    dve.wait_ge(s["LT_up"], nth(g, 2, q + 1))
                    link(dve.tensor_reduce(nmD[:, c, :], LT, AX, ALU.max, negate=True))
                    dve.tensor_tensor(DT[:, c, :].rearrange("p c (b n) -> p c b n", b=GB), LT,
                                      nmD[:, c, :].unsqueeze(3).to_broadcast([128, 2, GB, S]), ALU.add).then_inc(s["LD_ready"], 1)
                yield
                yield
                yield
                DT4 = DT[:, :, :].rearrange("p c (b n) -> p c b n", b=GB)
                for q in range(2):
                    dve.wait_ge(s["expD_ready"], nth(g, 2, q + 1))
                    ins = dve.tensor_reduce(sumD[:, 2 * q:2 * q + 2, :], DT4[:, 2 * q:2 * q + 2], AX, ALU.add)
                link(ins)
                link(dve.reciprocal(sumD[:, :, :], sumD[:, :, :]))
                dve.tensor_tensor(DT4, DT4, sumD[:, :, :].unsqueeze(3).to_broadcast([128, EP, GB, S]), ALU.mult).then_inc(s["DT_ready"], 1)
                yield
                dve.wait_ge(s["D_up"], nth(g, T, 1))
                dve.tensor_copy(Dw[:, 0, :], ra[0]).then_inc(s["D_dve"], 1)
                yield
                for j in range(T):
                    if j == 0 and before(g):
                        dve.wait_ge(s["h_up"], nth(g, FIRSTS, 0))
                    dve.wait_ge(s["slots_up"], nth(g, 2 * T, 2 * j + 1))
                    dve.tensor_scalar(slotsT_hi[:, :, 2 * j, :], slot_banks[j][0].rearrange("p (e k) -> p e k", e=E),
                                      vecs[:, C_G1:C_G1 + 1], None, ALU.mult).then_inc(s["slots_dve"], 1)
                    for par in range(2):
                        if par == 0:
                            dve.wait_ge(s["slots_dve"], nth(g, T, j + 1))
                        else:
                            dve.wait_ge(s["slots_act"], nth(g, T, j + 1))
                        b = 2 * j + par
                        ins = dve.scalar_tensor_tensor(slotsT_lo[:, :, b, :], slot_banks[j][par].rearrange("p (e k) -> p e k", e=E),
                                                       vecs[:, C_G1:C_G1 + 1], slotsT_hi[:, :, b, :], ALU.mult, ALU.subtract)
                    if j == T - 1:
                        ins.then_inc(s["slots_lo_ready"], 1)
                        assert k[0] == ROUTE_STEPS, k[0]
                    yield

            def turn(g):
                dve.wait_ge(s["C_ready"], nth(g, T, T))
                dve.reciprocal(rC[:, :], sumC[:, :]).then_inc(s["rC_ready"], 1)
                dve.wait_ge(s["CT_up"], nth(g, T, 1))
                dve.tensor_copy(CT[:, :, 0:128], ra[0].rearrange("p (c t) -> p c t", c=EP)).then_inc(s["CT_dve"], 1)
                yield

            def attend(g):
                link, k = linker("attend_step", ATTEND_STEPS, g)
                dve.wait_ge(s["x2_ready"], nth(g, 1, 1))
                moments(link, x2, a_stats, a_mv)
                dve.tensor_scalar(a_pow_in[:, :], a_mv[:, :, 1], EPS, None, ALU.add).then_inc(s["a_pow_asked"], 1)
                for q in range(2):
                    dve.wait_ge(s["V_up"], nth(g, 2, q + 1))
                    dve.tensor_tensor(V[:, 2 * q:2 * q + 2, :, :].rearrange("p b c w -> p b (c w)"), at[q][:, 0:288].rearrange("p (b w) -> p b w", b=2),
                                      v_bias[:, :, :].rearrange("p c w -> p (c w)").unsqueeze(1).to_broadcast([128, 2, VW * HP]), ALU.add).then_inc(s["V_ready"], 1)
                dve.wait_ge(s["a_pow_ready"], nth(g, 1, 1))
                centred(y2, x2, a_mv, a_pow).then_inc(s["y2_ready"], 1)
                yield
                dve.wait_ge(s["KT_ready"], nth(g, 1, 1))
                if last(g):
                    for h in range(HP):
                        ins = dve.tensor_scalar(KM[:, :, h, :], KT[:, :].rearrange("p (b n) -> p b n", b=GB), head8[:, h:h + 1], None, ALU.mult)
                    ins.then_inc(s["KM_ready"], 1)
                dve.tensor_reduce(sumK[:, :], KT[:, :].rearrange("p (b n) -> p b n", b=GB), AX, ALU.add)
                yield
                dve.wait_ge(s["QT_ready"], nth(g, 1, 1))
                link(dve.tensor_reduce(sumQ[:, :], QT[:, :].rearrange("p (b n) -> p b n", b=GB), AX, ALU.add))
                link(dve.tensor_tensor(qk_sum[:, :], sumQ[:, :], sumK[:, :], ALU.mult))
                for par in range(2):
                    ins = dve.tensor_tensor(mean_rows[:, par, :, :], head16[:, :].unsqueeze(1).to_broadcast([128, T, H]),
                                            qk_sum[:, par:GB:2].unsqueeze(2).to_broadcast([128, T, H]), ALU.mult)
                ins.then_inc(s["mean_ready"], 1)
                yield
                for j in range(T):
                    sc = tile_banks(g, j)[:, :].rearrange("p (h k) -> p h k", h=H)
                    if j == 0 and before(g):
                        dve.wait_ge(s["P_ready"], nth(g, T, 0))
                    dve.wait_ge(s["S_up"], nth(g, T, j + 1))
                    link(dve.tensor_reduce(mx[:, j, :], sc, AX, ALU.max))
                    dve.tensor_tensor(Dm[:, j, :, :], sc, mx[:, j, :].unsqueeze(2).to_broadcast([128, H, S]), ALU.subtract).then_inc(s[f"Dm{j}_ready"], 1)
                    yield
                for j in range(T):
                    dve.wait_ge(s["e1_ready"], nth(g, T, j + 1))
                    dve.tensor_reduce(s1[:, j, :], e1[:, j, :, :], AX, ALU.add)
                    dve.wait_ge(s["e2_ready"], nth(g, T, j + 1))
                    ins = dve.tensor_reduce(s2[:, j, :], e2[:, j, :, :], AX, ALU.add)
                    if j == T - 1:
                        link(ins)
                        link(dve.reciprocal(var[:, :, :], s1[:, :, :]))
                        link(dve.tensor_tensor(var[:, :, :], var[:, :, :], var[:, :, :], ALU.mult))
                        link(dve.tensor_tensor(var[:, :, :], var[:, :, :], s2[:, :, :], ALU.mult))
                        dve.tensor_scalar(var[:, :, :], var[:, :, :], -1.0 / S, None, ALU.add).then_inc(s["stats_ready"], 1)
                    yield
                yield
                yield
                dve.wait_ge(s["t_up"], nth(g, 1, 1))
                link(dve.tensor_scalar(zt[:, :, :], mix[:, 192:192 + TH].rearrange("p (j h) -> p j h", j=T), b3_all[:, :], -LOG_T, ALU.add, ALU.max))
                dve.tensor_scalar(zt[:, :, :], zt[:, :, :], LOG_T, None, ALU.min).then_inc(s["zt_ready"], 1)
                yield
                yield
                dve.wait_ge(s["inv_t_ready"], nth(g, 1, 1))
                for j in range(T):
                    dve.tensor_tensor(Dm[:, j, :, :], Dm[:, j, :, :], inv_t[:, j, :].unsqueeze(2).to_broadcast([128, H, S]), ALU.mult).then_inc(s["Dt_ready"], 1)
                yield
                yield
                yield

                def turned(j):
                    dve.wait_ge(s["PT_up"], nth(g, T, j + 1))
                    dve.tensor_scalar(PT[:, j, 0:4, :], tile_banks(g, j)[:, 0:512].rearrange("p (c q) -> p c q", c=4), 0.0, None, ALU.max).then_inc(s["PT_dve"], 1)

                def normalise(j):
                    dve.wait_ge(s["av_up"], nth(g, T, j + 1))
                    av = value_bank(g, j)[:, 144 * j:144 * j + 144].rearrange("p (c w) -> p c w", c=HP)
                    dj = den[:, j, :].rearrange("p (c a) -> p c a", a=2)
                    link(dve.tensor_scalar(dj, av[:, :, 2 * DK:VW], 1e-30, None, ALU.max))
                    link(dve.reciprocal(den[:, j, :], den[:, j, :]))
                    dve.tensor_tensor(ao[:, j, :].rearrange("p (c a k) -> p c a k", a=2, k=DK), av[:, :, 0:2 * DK].rearrange("p c (a k) -> p c a k", a=2),
                                      dj.unsqueeze(3).to_broadcast([128, HP, 2, DK]), ALU.mult).then_inc(s["ao_ready"], 1)

                turned(0)
                yield
                turned(1)
                normalise(0)
                yield
                normalise(1)
                yield
                yield
                dve.wait_ge(s["o_up"], nth(g, 1, 1))
                dve.wait_ge(s["x2b_ready"], nth(g, 1, 1))
                if before(g):
                    dve.wait_ge(s["acc_ready"], nth(g, 1, 0))
                dve.tensor_tensor(x3[:, :, :], x2b[:, :, :], at[1][:, 0:TOK].rearrange("p (j d) -> p j d", j=T), ALU.add).then_inc(s["x3_ready"], 1)
                dve.wait_ge(s["x3_ready"], nth(g, 1, 1))
                moments(link, x3, f_stats, f_mv)
                dve.tensor_scalar(f_pow_in[:, :], f_mv[:, :, 1], EPS, None, ALU.add).then_inc(s["f_pow_asked"], 1)
                assert k[0] == ATTEND_STEPS, k[0]
                yield

            def feed(g):
                link, k = linker("feed_step", FEED_STEPS, g)
                dve.wait_ge(s["f_pow_ready"], nth(g, 2, 1))
                link(dve.tensor_copy(f_small[:, 0, :], f_pow[:, :]))
                link(dve.tensor_tensor(f_small[:, 1, :], f_small[:, 0, :], f_small[:, 0, :], ALU.mult))
                link(dve.tensor_tensor(f_small[:, 2, :], f_small[:, 1, :], f_mv[:, :, 1], ALU.mult))
                dve.tensor_scalar(f_pow_in[:, :], f_small[:, 2, :], EPS, None, ALU.add).then_inc(s["f_pow_asked"], 1)
                link(centred(y3, x3, f_mv, f_small[:, 0]))
                dve.wait_ge(s["f_pow_ready"], nth(g, 2, 2))
                link(dve.tensor_tensor(f_small[:, 3, :], f_small[:, 0, :], f_pow[:, :], ALU.mult))
                ins = centred(h3, x3, f_mv, f_small[:, 3])
                ins.then_inc(s["h3_ready"], 1)
                dve.memset(wait_pad[:, :], 0.0).then_inc(s["y3_ready"], 1)
                yield
                dve.wait_ge(s["h3T_up"], nth(g, 1, 1))
                dve.tensor_scalar(h3T[:, :], feed_banks(g)[0][:, 0:TOK], vecs[:, C_LG:C_LG + 1], vecs[:, C_LB:C_LB + 1], ALU.mult, ALU.add).then_inc(s["h3T_ready"], 1)
                yield
                yield
                dve.wait_ge(s["z_up"], nth(g, 1, 1))
                dve.wait_ge(s["acc_ready"], nth(g, 1, 1))
                dve.wait_ge(s["out_done"], nth(g, 16, 16))
                dve.scalar_tensor_tensor(res[:, :, :].rearrange("p j d -> p (j d)"), feed_banks(g)[2], 0.5,
                                         acc[:, :, :].rearrange("p j d -> p (j d)"), ALU.mult, ALU.add).then_inc(s["res_ready"], 1)
                assert k[0] == FEED_STEPS, k[0]
                yield

            all_iterations(dve, experts, {"attend": attend, "feed": feed, "turn": turn, "route": route,
                                 "first_consts": first_consts, "later_consts": later_consts,
                                 "split_first": lambda: split_w1(0), "split_later": lambda: split_w1(2)}, steps_first=True)


_INS = ['x', 'ctx_1024', 'L0_ffn_norm_gamma', 'L0_ffn_slot_norm_gamma', 'L0_ffn_slot_embeds', 'L0_ffn_w1', 'L0_ffn_b1',
        'L0_ffn_w2', 'L0_ffn_b2', 'L1_xattn_Wq', 'L1_xattn_bq', 'L1_xattn_Wk', 'L1_xattn_bk', 'L1_xattn_Wv', 'L1_xattn_bv',
        'L1_xattn_Wo', 'L1_xattn_bo', 'L1_xattn_w1', 'L1_xattn_b1', 'L1_xattn_w2', 'L1_xattn_b2', 'L1_xattn_w3',
        'L1_xattn_b3', 'L1_ffn_ln_gamma', 'L1_ffn_ln_beta', 'L1_ffn_fc1_q', 'L1_ffn_fc1_scales', 'L1_ffn_fc1_bias',
        'L1_ffn_fc2_q', 'L1_ffn_fc2_scales', 'L1_ffn_fc2_bias']


def kernel(**inputs):
    import numpy as _np
    import concourse.bacc as _bacc
    from concourse import mybir as _mybir
    from concourse.bass_utils import run_bass_kernel_spmd as _run

    nc = _bacc.Bacc("TRN2", target_bir_lowering=False, num_devices=1)
    arrays, args = {}, {}
    for name in _INS:
        v = _np.ascontiguousarray(inputs[name])
        arrays[f"in_{name}"] = v
        args[name] = nc.dram_tensor(f"in_{name}", v.shape, _mybir.dt.from_np(v.dtype), kind="ExternalInput").ap()
    out = nc.dram_tensor("out_0", (32, 64, 128), _mybir.dt.float32, kind="ExternalOutput").ap()
    build(nc, args, out)
    r = _run(nc, [arrays], core_ids=[0])
    return r.results[0]["out_0"]
```
